# Optimizing a Trainium2 kernel written in Bass

```python
import numpy as np
import jax
import jax.numpy as jnp

def _softmax(x, axis=-1):
    return jax.nn.softmax(x, axis=axis)

def _gelu(x):
    return jax.nn.gelu(x, approximate=True)

def _silu(x):
    return jax.nn.silu(x)

def _sigmoid(x):
    return jax.nn.sigmoid(x)

def _layernorm(x, axis=-1, eps=1e-05):
    m = jnp.mean(x, axis=axis, keepdims=True)
    v = jnp.var(x, axis=axis, keepdims=True)
    return (x - m) / jnp.sqrt(v + eps)

def _scatter_add(tgt, idx, src, axis=0):
    return tgt.at[idx].add(src)

def _segment_sum(src, seg, n):
    return jax.ops.segment_sum(src, seg, n)
kernel_name = 'mk_decoder_postln_d2_seqx_r8_14312d'

def setup_inputs(seed: int=0):
    np.random.seed(seed)
    _w = jnp.asarray

    def _rec_inputs():
        import jax
        import jax.numpy as jnp
        _rk = jax.random.key(seed)
        x = -0.0005146 + 1 * jax.random.normal(jax.random.fold_in(_rk, 1), (4, 512, 128), jnp.float32)
        _lenS = 512 - jax.random.randint(jax.random.fold_in(_rk, 7), (4,), 0, max(1, 512 // 4) + 1, jnp.int32)
        _lenS2 = 32 - jax.random.randint(jax.random.fold_in(_rk, 8), (4,), 0, max(1, 32 // 4) + 1, jnp.int32)
        _ctx_1024P = jax.random.normal(jax.random.fold_in(_rk, 11), (4, 16, 128), jnp.float32)
        _ctx_1024c = jax.random.dirichlet(jax.random.fold_in(_rk, 511), 0.3 * jnp.ones((16,), jnp.float32), (4, 32))
        _ctx_1024t = jnp.einsum('bsk,bkd->bsd', _ctx_1024c, _ctx_1024P)
        _ctx_1024t = _ctx_1024t * jax.lax.rsqrt(jnp.mean(jnp.square(_ctx_1024t)) + 1e-12) * 0.953939
        ctx_1024 = -0.000392918 + 0.999932 * (_ctx_1024t + 0.3 * jax.random.normal(jax.random.fold_in(_rk, 611), (4, 32, 128), jnp.float32))
        return (x, ctx_1024)
    x, ctx_1024 = _rec_inputs()

    def _L0_attn_setup():
        import jax, jax.numpy as jnp
        import numpy as np
        from jax import lax
        D_MODEL = 128
        KERNEL = 7
        RMS_EPS = 1.1920929e-07

        def _depthwise_conv1d(x_bds, w, b):
            D = x_bds.shape[1]
            pad = w.shape[-1] // 2
            y = lax.conv_general_dilated(x_bds, w, window_strides=(1,), padding=[(pad, pad)], feature_group_count=D, dimension_numbers=('NCH', 'OIH', 'NCH'))
            return y + b[None, :, None]

        def _decay_scan(gated, decay):
            a = jnp.broadcast_to(decay[None, :, None], gated.shape)

            def combine(c1, c2):
                a1, b1 = c1
                a2, b2 = c2
                return (a1 * a2, a2 * b1 + b2)
            _, h = lax.associative_scan(combine, (a, gated), axis=2)
            return h
        key = jax.random.key(seed)
        ks = jax.random.split(key, 6)
        B, S, D, K = (4, 512, D_MODEL, KERNEL)
        x = jax.random.normal(ks[0], (B, S, D), dtype=jnp.float32)
        gate_w = jax.random.normal(ks[1], (D, 1, K), dtype=jnp.float32) * 0.1
        gate_b = jnp.zeros((D,), dtype=jnp.float32)
        cand_w = jax.random.normal(ks[2], (D, 1, K), dtype=jnp.float32) * 0.1
        cand_b = jnp.zeros((D,), dtype=jnp.float32)
        log_decay = jnp.full((D,), np.log(0.1), dtype=jnp.float32)
        out_w = jax.random.normal(ks[3], (D, D), dtype=jnp.float32) * 0.02
        out_b = jnp.zeros((D,), dtype=jnp.float32)
        norm_w = jnp.ones((D,), dtype=jnp.float32)
        return {'x': x, 'gate_w': gate_w, 'gate_b': gate_b, 'cand_w': cand_w, 'cand_b': cand_b, 'log_decay': log_decay, 'out_w': out_w, 'out_b': out_b, 'norm_w': norm_w}
    _L0_attn_all = _L0_attn_setup()
    _L0_attn_in = {k: v for k, v in _L0_attn_all.items() if k in ('gate_w', 'gate_b', 'cand_w', 'cand_b', 'log_decay', 'out_w', 'out_b', 'norm_w')}
    del _L0_attn_all

    def _L0_xattn_setup():
        import jax, jax.numpy as jnp
        import numpy as np
        DIM = 128
        DIM_HEAD = 64
        HEADS = 16
        INNER = DIM_HEAD * HEADS
        EPS = 1e-05

        def layer_norm(x, g, b):
            m = jnp.mean(x, axis=-1, keepdims=True)
            v = jnp.mean(jnp.square(x - m), axis=-1, keepdims=True)
            return (x - m) * jax.lax.rsqrt(v + EPS) * g + b
        key = jax.random.key(seed)
        ks = jax.random.split(key, 8)
        B, N_IMG, N_LAT = (4, 512, 64)
        std = 1.0 / np.sqrt(DIM)
        return {'image_embeds': jax.random.normal(ks[0], (B, N_IMG, DIM), dtype=jnp.float32), 'latents': jax.random.normal(ks[1], (B, N_LAT, DIM), dtype=jnp.float32), 'ln1_g': jnp.ones((DIM,), jnp.float32), 'ln1_b': jnp.zeros((DIM,), jnp.float32), 'ln2_g': jnp.ones((DIM,), jnp.float32), 'ln2_b': jnp.zeros((DIM,), jnp.float32), 'Wq': jax.random.normal(ks[2], (DIM, INNER), dtype=jnp.float32) * std, 'Wkv': jax.random.normal(ks[3], (DIM, 2 * INNER), dtype=jnp.float32) * std, 'Wo': jax.random.normal(ks[4], (INNER, DIM), dtype=jnp.float32) * std}
    _L0_xattn_all = _L0_xattn_setup()
    _L0_xattn_in = {k: v for k, v in _L0_xattn_all.items() if k in ('ln1_g', 'ln1_b', 'ln2_g', 'ln2_b', 'Wq', 'Wkv', 'Wo')}
    del _L0_xattn_all

    def _L0_ffn_setup():
        import jax, jax.numpy as jnp
        import numpy as np
        D_MODEL = 128
        N_HEAD = 16
        HEAD_DIM = D_MODEL // N_HEAD
        D_FF = 512
        N_EXPERTS = 4
        EPS = 1e-05

        def _layer_norm(x, gamma, beta):
            mu = jnp.mean(x, axis=-1, keepdims=True)
            var = jnp.mean((x - mu) ** 2, axis=-1, keepdims=True)
            return (x - mu) / jnp.sqrt(var + EPS) * gamma + beta
        key = jax.random.key(seed)
        ks = jax.random.split(key, 20)
        f32 = jnp.float32
        sc = 1.0 / np.sqrt(D_MODEL)
        scf = 1.0 / np.sqrt(D_FF)
        return {'src': jax.random.normal(ks[0], (4, 64, D_MODEL), f32), 'Wq': jax.random.normal(ks[1], (D_MODEL, D_MODEL), f32) * sc, 'bq': jnp.zeros((D_MODEL,), f32), 'Wk': jax.random.normal(ks[2], (D_MODEL, D_MODEL), f32) * sc, 'bk': jnp.zeros((D_MODEL,), f32), 'Wv': jax.random.normal(ks[3], (D_MODEL, D_MODEL), f32) * sc, 'bv': jnp.zeros((D_MODEL,), f32), 'Wo': jax.random.normal(ks[4], (D_MODEL, D_MODEL), f32) * sc, 'bo': jnp.zeros((D_MODEL,), f32), 'router_w': jax.random.normal(ks[5], (D_MODEL, 1), f32) * 0.05, 'router_b': jnp.zeros((1,), f32), 'W1': jax.random.normal(ks[6], (N_EXPERTS, D_MODEL, D_FF), f32) * sc, 'b1': jnp.zeros((N_EXPERTS, D_FF), f32), 'W2': jax.random.normal(ks[7], (N_EXPERTS, D_FF, D_MODEL), f32) * scf, 'b2': jnp.zeros((N_EXPERTS, D_MODEL), f32), 'ln1_g': jnp.ones((D_MODEL,), f32), 'ln1_b': jnp.zeros((D_MODEL,), f32), 'ln2_g': jnp.ones((D_MODEL,), f32), 'ln2_b': jnp.zeros((D_MODEL,), f32)}
    _L0_ffn_all = _L0_ffn_setup()
    _L0_ffn_in = {k: v for k, v in _L0_ffn_all.items() if k in ('Wq', 'bq', 'Wk', 'bk', 'Wv', 'bv', 'Wo', 'bo', 'router_w', 'router_b', 'W1', 'b1', 'W2', 'b2', 'ln1_g', 'ln1_b', 'ln2_g', 'ln2_b')}
    del _L0_ffn_all

    def _L1_attn_setup():
        import jax, jax.numpy as jnp
        import numpy as np
        D = 128
        H = 16
        HD = D // H
        K = 4
        I = int(D * 2.7)
        B, T = (2, 256)
        EPS = 1e-06
        GATE_BIAS = 4.0

        def _rmsnorm(x, w):
            return x * jax.lax.rsqrt(jnp.mean(x * x, axis=-1, keepdims=True) + EPS) * w

        def _causal_depthwise_conv(x, conv_w, conv_b):
            xt = jnp.transpose(x, (0, 2, 1))
            y = jax.lax.conv_general_dilated(xt, conv_w[:, None, :], window_strides=(1,), padding=[(K - 1, 0)], feature_group_count=D, dimension_numbers=('NCH', 'OIH', 'NCH'))
            y = jnp.transpose(y, (0, 2, 1)) + conv_b
            return jax.nn.silu(y)

        def _l2norm(x):
            return x * jax.lax.rsqrt(jnp.sum(x * x, axis=-1, keepdims=True) + EPS)

        def _gated_delta_rule(xc, wq, wk, wv, wb, wa):
            b, t = (xc.shape[0], xc.shape[1])
            q = _l2norm((xc @ wq).reshape(b, t, H, HD))
            k = _l2norm((xc @ wk).reshape(b, t, H, HD))
            v = (xc @ wv).reshape(b, t, H, HD)
            beta = jax.nn.sigmoid(xc @ wb)
            alpha = jax.nn.sigmoid(xc @ wa + GATE_BIAS)
            qt = jnp.moveaxis(q, 1, 0)
            kt = jnp.moveaxis(k, 1, 0)
            vt = jnp.moveaxis(v, 1, 0)
            bt = jnp.moveaxis(beta, 1, 0)
            at = jnp.moveaxis(alpha, 1, 0)
            S0 = jnp.zeros((b, H, HD, HD), xc.dtype)

            def step(S, inp):
                q_, k_, v_, b_, a_ = inp
                S = a_[..., None, None] * S
                pred = jnp.einsum('bhkv,bhk->bhv', S, k_)
                S = S + k_[..., :, None] * (b_[..., None] * (v_ - pred))[..., None, :]
                o = jnp.einsum('bhkv,bhk->bhv', S, q_)
                return (S, o)
            _, o = jax.lax.scan(step, S0, (qt, kt, vt, bt, at))
            return jnp.moveaxis(o, 1, 0).reshape(b, t, D)
        key = jax.random.key(seed)
        ks = jax.random.split(key, 16)
        s = D ** (-0.5)
        return {'x': jax.random.normal(ks[0], (B, T, D), jnp.float32), 'norm1_w': jnp.ones((D,), jnp.float32), 'norm2_w': jnp.ones((D,), jnp.float32), 'conv_w': jax.random.normal(ks[1], (D, K), jnp.float32) * 0.2, 'conv_b': jnp.zeros((D,), jnp.float32), 'wq': jax.random.normal(ks[2], (D, D), jnp.float32) * s, 'wk': jax.random.normal(ks[3], (D, D), jnp.float32) * s, 'wv': jax.random.normal(ks[4], (D, D), jnp.float32) * s, 'wb': jax.random.normal(ks[5], (D, H), jnp.float32) * s, 'wa': jax.random.normal(ks[6], (D, H), jnp.float32) * s, 'wo': jax.random.normal(ks[7], (D, D), jnp.float32) * s, 'wg': jax.random.normal(ks[8], (D, I), jnp.float32) * s, 'wu': jax.random.normal(ks[9], (D, I), jnp.float32) * s, 'wd': jax.random.normal(ks[10], (I, D), jnp.float32) * I ** (-0.5)}
    _L1_attn_all = _L1_attn_setup()
    _L1_attn_in = {k: v for k, v in _L1_attn_all.items() if k in ('norm1_w', 'norm2_w', 'conv_w', 'conv_b', 'wq', 'wk', 'wv', 'wb', 'wa', 'wo', 'wg', 'wu', 'wd')}
    del _L1_attn_all

    def _L1_xattn_setup():
        import jax, jax.numpy as jnp
        import numpy as np
        D_MODEL = 128
        NUM_HEADS = 16
        D_K = D_MODEL // NUM_HEADS

        def _split_heads(x):
            B, S, _ = x.shape
            return x.reshape(B, S, NUM_HEADS, D_K).transpose(0, 2, 1, 3)
        key = jax.random.key(seed)
        ks = jax.random.split(key, 11)
        B, S = (4, 256)
        s = 1.0 / np.sqrt(D_MODEL)
        return {'Q': jax.random.normal(ks[0], (B, S, D_MODEL), jnp.float32), 'K': jax.random.normal(ks[1], (B, S, D_MODEL), jnp.float32), 'V': jax.random.normal(ks[2], (B, S, D_MODEL), jnp.float32), 'Wq': jax.random.normal(ks[3], (D_MODEL, D_MODEL), jnp.float32) * s, 'bq': jax.random.normal(ks[4], (D_MODEL,), jnp.float32) * 0.01, 'Wk': jax.random.normal(ks[5], (D_MODEL, D_MODEL), jnp.float32) * s, 'bk': jax.random.normal(ks[6], (D_MODEL,), jnp.float32) * 0.01, 'Wv': jax.random.normal(ks[7], (D_MODEL, D_MODEL), jnp.float32) * s, 'bv': jax.random.normal(ks[8], (D_MODEL,), jnp.float32) * 0.01, 'Wo': jax.random.normal(ks[9], (D_MODEL, D_MODEL), jnp.float32) * s, 'bo': jax.random.normal(ks[10], (D_MODEL,), jnp.float32) * 0.01}
    _L1_xattn_all = _L1_xattn_setup()
    _L1_xattn_in = {k: v for k, v in _L1_xattn_all.items() if k in ('Wq', 'bq', 'Wk', 'bk', 'Wv', 'bv', 'Wo', 'bo')}
    del _L1_xattn_all

    def _L1_ffn_setup():
        import jax, jax.numpy as jnp
        import numpy as np
        HID = 128
        NH = 16
        NKV = 4
        HD = HID // NH
        E = 8
        TOPK = 2
        FFN = 256
        EPS = 1e-05
        THETA = 10000.0

        def _rmsnorm(x, w):
            var = jnp.mean(x * x, axis=-1, keepdims=True)
            return x * jax.lax.rsqrt(var + EPS) * w

        def _rope_tables(S):
            inv_freq = 1.0 / THETA ** (jnp.arange(0, HD, 2, dtype=jnp.float32) / HD)
            freqs = jnp.arange(S, dtype=jnp.float32)[:, None] * inv_freq[None, :]
            emb = jnp.concatenate([freqs, freqs], axis=-1)
            return (jnp.cos(emb), jnp.sin(emb))

        def _apply_rope(t, cos, sin):
            t1, t2 = jnp.split(t, 2, axis=-1)
            rot = jnp.concatenate([-t2, t1], axis=-1)
            return t * cos[None, :, None, :] + rot * sin[None, :, None, :]
        key = jax.random.key(seed)
        ks = jax.random.split(key, 6)
        B, S = (1, 256)
        x = jax.random.normal(ks[0], (B, S, HID), dtype=jnp.float32)
        wqkv = jax.random.normal(ks[1], ((NH + 2 * NKV) * HD, HID), dtype=jnp.float32) * 0.02
        wo = jax.random.normal(ks[2], (HID, NH * HD), dtype=jnp.float32) * 0.02
        gate_w = jax.random.normal(ks[3], (E, HID), dtype=jnp.float32) * 0.02
        w13 = jax.random.normal(ks[4], (E, 2 * FFN, HID), dtype=jnp.float32) * 0.02
        w2 = jax.random.normal(ks[5], (E, HID, FFN), dtype=jnp.float32) * 0.02
        return {'x': x, 'ln1_w': jnp.ones((HID,), jnp.float32), 'ln2_w': jnp.ones((HID,), jnp.float32), 'wqkv': wqkv, 'wo': wo, 'gate_w': gate_w, 'w13': w13, 'w2': w2}
    _L1_ffn_all = _L1_ffn_setup()
    _L1_ffn_in = {k: v for k, v in _L1_ffn_all.items() if k in ('ln1_w', 'ln2_w', 'wqkv', 'wo', 'gate_w', 'w13', 'w2')}
    del _L1_ffn_all
    return {'x': x, 'ctx_1024': ctx_1024, 'L0_attn_gate_w': _L0_attn_in['gate_w'], 'L0_attn_gate_b': _L0_attn_in['gate_b'], 'L0_attn_cand_w': _L0_attn_in['cand_w'], 'L0_attn_cand_b': _L0_attn_in['cand_b'], 'L0_attn_log_decay': _L0_attn_in['log_decay'], 'L0_attn_out_w': _L0_attn_in['out_w'], 'L0_attn_out_b': _L0_attn_in['out_b'], 'L0_attn_norm_w': _L0_attn_in['norm_w'], 'L0_xattn_ln1_g': _L0_xattn_in['ln1_g'], 'L0_xattn_ln1_b': _L0_xattn_in['ln1_b'], 'L0_xattn_ln2_g': _L0_xattn_in['ln2_g'], 'L0_xattn_ln2_b': _L0_xattn_in['ln2_b'], 'L0_xattn_Wq': _L0_xattn_in['Wq'], 'L0_xattn_Wkv': _L0_xattn_in['Wkv'], 'L0_xattn_Wo': _L0_xattn_in['Wo'], 'L0_ffn_Wq': _L0_ffn_in['Wq'], 'L0_ffn_bq': _L0_ffn_in['bq'], 'L0_ffn_Wk': _L0_ffn_in['Wk'], 'L0_ffn_bk': _L0_ffn_in['bk'], 'L0_ffn_Wv': _L0_ffn_in['Wv'], 'L0_ffn_bv': _L0_ffn_in['bv'], 'L0_ffn_Wo': _L0_ffn_in['Wo'], 'L0_ffn_bo': _L0_ffn_in['bo'], 'L0_ffn_router_w': _L0_ffn_in['router_w'], 'L0_ffn_router_b': _L0_ffn_in['router_b'], 'L0_ffn_W1': _L0_ffn_in['W1'], 'L0_ffn_b1': _L0_ffn_in['b1'], 'L0_ffn_W2': _L0_ffn_in['W2'], 'L0_ffn_b2': _L0_ffn_in['b2'], 'L0_ffn_ln1_g': _L0_ffn_in['ln1_g'], 'L0_ffn_ln1_b': _L0_ffn_in['ln1_b'], 'L0_ffn_ln2_g': _L0_ffn_in['ln2_g'], 'L0_ffn_ln2_b': _L0_ffn_in['ln2_b'], 'L1_attn_norm1_w': _L1_attn_in['norm1_w'], 'L1_attn_norm2_w': _L1_attn_in['norm2_w'], 'L1_attn_conv_w': _L1_attn_in['conv_w'], 'L1_attn_conv_b': _L1_attn_in['conv_b'], 'L1_attn_wq': _L1_attn_in['wq'], 'L1_attn_wk': _L1_attn_in['wk'], 'L1_attn_wv': _L1_attn_in['wv'], 'L1_attn_wb': _L1_attn_in['wb'], 'L1_attn_wa': _L1_attn_in['wa'], 'L1_attn_wo': _L1_attn_in['wo'], 'L1_attn_wg': _L1_attn_in['wg'], 'L1_attn_wu': _L1_attn_in['wu'], 'L1_attn_wd': _L1_attn_in['wd'], 'L1_xattn_Wq': _L1_xattn_in['Wq'], 'L1_xattn_bq': _L1_xattn_in['bq'], 'L1_xattn_Wk': _L1_xattn_in['Wk'], 'L1_xattn_bk': _L1_xattn_in['bk'], 'L1_xattn_Wv': _L1_xattn_in['Wv'], 'L1_xattn_bv': _L1_xattn_in['bv'], 'L1_xattn_Wo': _L1_xattn_in['Wo'], 'L1_xattn_bo': _L1_xattn_in['bo'], 'L1_ffn_ln1_w': _L1_ffn_in['ln1_w'], 'L1_ffn_ln2_w': _L1_ffn_in['ln2_w'], 'L1_ffn_wqkv': _L1_ffn_in['wqkv'], 'L1_ffn_wo': _L1_ffn_in['wo'], 'L1_ffn_gate_w': _L1_ffn_in['gate_w'], 'L1_ffn_w13': _L1_ffn_in['w13'], 'L1_ffn_w2': _L1_ffn_in['w2']}

def reference(x, ctx_1024, L0_attn_gate_w, L0_attn_gate_b, L0_attn_cand_w, L0_attn_cand_b, L0_attn_log_decay, L0_attn_out_w, L0_attn_out_b, L0_attn_norm_w, L0_xattn_ln1_g, L0_xattn_ln1_b, L0_xattn_ln2_g, L0_xattn_ln2_b, L0_xattn_Wq, L0_xattn_Wkv, L0_xattn_Wo, L0_ffn_Wq, L0_ffn_bq, L0_ffn_Wk, L0_ffn_bk, L0_ffn_Wv, L0_ffn_bv, L0_ffn_Wo, L0_ffn_bo, L0_ffn_router_w, L0_ffn_router_b, L0_ffn_W1, L0_ffn_b1, L0_ffn_W2, L0_ffn_b2, L0_ffn_ln1_g, L0_ffn_ln1_b, L0_ffn_ln2_g, L0_ffn_ln2_b, L1_attn_norm1_w, L1_attn_norm2_w, L1_attn_conv_w, L1_attn_conv_b, L1_attn_wq, L1_attn_wk, L1_attn_wv, L1_attn_wb, L1_attn_wa, L1_attn_wo, L1_attn_wg, L1_attn_wu, L1_attn_wd, L1_xattn_Wq, L1_xattn_bq, L1_xattn_Wk, L1_xattn_bk, L1_xattn_Wv, L1_xattn_bv, L1_xattn_Wo, L1_xattn_bo, L1_ffn_ln1_w, L1_ffn_ln2_w, L1_ffn_wqkv, L1_ffn_wo, L1_ffn_gate_w, L1_ffn_w13, L1_ffn_w2):
    import jax
    import jax.numpy as jnp

    def _L0_attn_ref(x, gate_w, gate_b, cand_w, cand_b, log_decay, out_w, out_b, norm_w):
        import jax, jax.numpy as jnp
        import numpy as np
        from jax import lax
        D_MODEL = 128
        KERNEL = 7
        RMS_EPS = 1.1920929e-07

        def _depthwise_conv1d(x_bds, w, b):
            D = x_bds.shape[1]
            pad = w.shape[-1] // 2
            y = lax.conv_general_dilated(x_bds, w, window_strides=(1,), padding=[(pad, pad)], feature_group_count=D, dimension_numbers=('NCH', 'OIH', 'NCH'))
            return y + b[None, :, None]

        def _decay_scan(gated, decay):
            a = jnp.broadcast_to(decay[None, :, None], gated.shape)

            def combine(c1, c2):
                a1, b1 = c1
                a2, b2 = c2
                return (a1 * a2, a2 * b1 + b2)
            _, h = lax.associative_scan(combine, (a, gated), axis=2)
            return h
        residual = x
        x_t = jnp.transpose(x, (0, 2, 1))
        gate = jax.nn.sigmoid(_depthwise_conv1d(x_t, gate_w, gate_b))
        cand = jnp.tanh(_depthwise_conv1d(x_t, cand_w, cand_b))
        gated = gate * cand
        decay = jnp.exp(log_decay)
        h = _decay_scan(gated, decay)
        h = jnp.transpose(h, (0, 2, 1))
        out = jnp.einsum('bsd,ed->bse', h, out_w) + out_b
        y = out + residual
        ms = jnp.mean(y * y, axis=-1, keepdims=True)
        return y * lax.rsqrt(ms + RMS_EPS) * norm_w

    def _L0_xattn_ref(image_embeds, latents, ln1_g, ln1_b, ln2_g, ln2_b, Wq, Wkv, Wo):
        import jax, jax.numpy as jnp
        import numpy as np
        DIM = 128
        DIM_HEAD = 64
        HEADS = 16
        INNER = DIM_HEAD * HEADS
        EPS = 1e-05

        def layer_norm(x, g, b):
            m = jnp.mean(x, axis=-1, keepdims=True)
            v = jnp.mean(jnp.square(x - m), axis=-1, keepdims=True)
            return (x - m) * jax.lax.rsqrt(v + EPS) * g + b
        B, S_lat, _ = latents.shape
        x = layer_norm(image_embeds, ln1_g, ln1_b)
        l = layer_norm(latents, ln2_g, ln2_b)
        q = l @ Wq
        kv_in = jnp.concatenate([x, l], axis=1)
        kv = kv_in @ Wkv
        k, v = jnp.split(kv, 2, axis=-1)

        def to_heads(t):
            return t.reshape(t.shape[0], t.shape[1], HEADS, DIM_HEAD).transpose(0, 2, 1, 3)
        q, k, v = (to_heads(q), to_heads(k), to_heads(v))
        scale = 1.0 / np.sqrt(np.sqrt(DIM_HEAD))
        w = jnp.einsum('bhqd,bhkd->bhqk', q * scale, k * scale)
        w = jax.nn.softmax(w.astype(jnp.float32), axis=-1).astype(q.dtype)
        out = jnp.einsum('bhqk,bhkd->bhqd', w, v)
        out = out.transpose(0, 2, 1, 3).reshape(B, S_lat, INNER)
        return out @ Wo

    def _L0_ffn_ref(src, Wq, bq, Wk, bk, Wv, bv, Wo, bo, router_w, router_b, W1, b1, W2, b2, ln1_g, ln1_b, ln2_g, ln2_b):
        import jax, jax.numpy as jnp
        import numpy as np
        D_MODEL = 128
        N_HEAD = 16
        HEAD_DIM = D_MODEL // N_HEAD
        D_FF = 512
        N_EXPERTS = 4
        EPS = 1e-05

        def _layer_norm(x, gamma, beta):
            mu = jnp.mean(x, axis=-1, keepdims=True)
            var = jnp.mean((x - mu) ** 2, axis=-1, keepdims=True)
            return (x - mu) / jnp.sqrt(var + EPS) * gamma + beta
        B, T, _ = src.shape
        q = (src @ Wq + bq).reshape(B, T, N_HEAD, HEAD_DIM)
        k = (src @ Wk + bk).reshape(B, T, N_HEAD, HEAD_DIM)
        v = (src @ Wv + bv).reshape(B, T, N_HEAD, HEAD_DIM)
        scale = HEAD_DIM ** (-0.5)
        scores = jnp.einsum('bqhd,bkhd->bhqk', q, k) * scale
        probs = jax.nn.softmax(scores, axis=-1)
        attn = jnp.einsum('bhqk,bkhd->bqhd', probs, v).reshape(B, T, D_MODEL)
        attn = attn @ Wo + bo
        x = _layer_norm(src + attn, ln1_g, ln1_b)
        keys = (x @ router_w + router_b)[..., 0]
        expert_idx = jnp.remainder(jnp.floor(keys).astype(jnp.int32), N_EXPERTS)
        ff_out = jnp.zeros_like(x)
        for e in range(N_EXPERTS):
            h = jax.nn.relu(x @ W1[e] + b1[e])
            y = h @ W2[e] + b2[e]
            ff_out = ff_out + jnp.where((expert_idx == e)[..., None], y, 0.0)
        return _layer_norm(x + ff_out, ln2_g, ln2_b)

    def _L1_attn_ref(x, norm1_w, norm2_w, conv_w, conv_b, wq, wk, wv, wb, wa, wo, wg, wu, wd):
        import jax, jax.numpy as jnp
        import numpy as np
        D = 128
        H = 16
        HD = D // H
        K = 4
        I = int(D * 2.7)
        B, T = (2, 256)
        EPS = 1e-06
        GATE_BIAS = 4.0

        def _rmsnorm(x, w):
            return x * jax.lax.rsqrt(jnp.mean(x * x, axis=-1, keepdims=True) + EPS) * w

        def _causal_depthwise_conv(x, conv_w, conv_b):
            xt = jnp.transpose(x, (0, 2, 1))
            y = jax.lax.conv_general_dilated(xt, conv_w[:, None, :], window_strides=(1,), padding=[(K - 1, 0)], feature_group_count=D, dimension_numbers=('NCH', 'OIH', 'NCH'))
            y = jnp.transpose(y, (0, 2, 1)) + conv_b
            return jax.nn.silu(y)

        def _l2norm(x):
            return x * jax.lax.rsqrt(jnp.sum(x * x, axis=-1, keepdims=True) + EPS)

        def _gated_delta_rule(xc, wq, wk, wv, wb, wa):
            b, t = (xc.shape[0], xc.shape[1])
            q = _l2norm((xc @ wq).reshape(b, t, H, HD))
            k = _l2norm((xc @ wk).reshape(b, t, H, HD))
            v = (xc @ wv).reshape(b, t, H, HD)
            beta = jax.nn.sigmoid(xc @ wb)
            alpha = jax.nn.sigmoid(xc @ wa + GATE_BIAS)
            qt = jnp.moveaxis(q, 1, 0)
            kt = jnp.moveaxis(k, 1, 0)
            vt = jnp.moveaxis(v, 1, 0)
            bt = jnp.moveaxis(beta, 1, 0)
            at = jnp.moveaxis(alpha, 1, 0)
            S0 = jnp.zeros((b, H, HD, HD), xc.dtype)

            def step(S, inp):
                q_, k_, v_, b_, a_ = inp
                S = a_[..., None, None] * S
                pred = jnp.einsum('bhkv,bhk->bhv', S, k_)
                S = S + k_[..., :, None] * (b_[..., None] * (v_ - pred))[..., None, :]
                o = jnp.einsum('bhkv,bhk->bhv', S, q_)
                return (S, o)
            _, o = jax.lax.scan(step, S0, (qt, kt, vt, bt, at))
            return jnp.moveaxis(o, 1, 0).reshape(b, t, D)
        residual = x
        xn = _rmsnorm(x, norm1_w)
        xc = _causal_depthwise_conv(xn, conv_w, conv_b)
        mixer_out = _gated_delta_rule(xc, wq, wk, wv, wb, wa) @ wo
        h = residual + mixer_out
        hn = _rmsnorm(h, norm2_w)
        ffn = jax.nn.silu(hn @ wg) * (hn @ wu) @ wd
        return h + ffn

    def _L1_xattn_ref(Q, K, V, Wq, bq, Wk, bk, Wv, bv, Wo, bo):
        import jax, jax.numpy as jnp
        import numpy as np
        D_MODEL = 128
        NUM_HEADS = 16
        D_K = D_MODEL // NUM_HEADS

        def _split_heads(x):
            B, S, _ = x.shape
            return x.reshape(B, S, NUM_HEADS, D_K).transpose(0, 2, 1, 3)
        q = _split_heads(Q @ Wq.T + bq)
        k = _split_heads(K @ Wk.T + bk)
        v = _split_heads(V @ Wv.T + bv)
        scale = 1.0 / jnp.sqrt(jnp.asarray(D_K, jnp.float32))
        scores = jnp.einsum('bhqd,bhkd->bhqk', q, k) * scale
        attn = jax.nn.softmax(scores, axis=-1)
        ctx = jnp.einsum('bhqk,bhkd->bhqd', attn, v)
        B, H, S, Dk = ctx.shape
        ctx = ctx.transpose(0, 2, 1, 3).reshape(B, S, H * Dk)
        return ctx @ Wo.T + bo

    def _L1_ffn_ref(x, ln1_w, ln2_w, wqkv, wo, gate_w, w13, w2):
        import jax, jax.numpy as jnp
        import numpy as np
        HID = 128
        NH = 16
        NKV = 4
        HD = HID // NH
        E = 8
        TOPK = 2
        FFN = 256
        EPS = 1e-05
        THETA = 10000.0

        def _rmsnorm(x, w):
            var = jnp.mean(x * x, axis=-1, keepdims=True)
            return x * jax.lax.rsqrt(var + EPS) * w

        def _rope_tables(S):
            inv_freq = 1.0 / THETA ** (jnp.arange(0, HD, 2, dtype=jnp.float32) / HD)
            freqs = jnp.arange(S, dtype=jnp.float32)[:, None] * inv_freq[None, :]
            emb = jnp.concatenate([freqs, freqs], axis=-1)
            return (jnp.cos(emb), jnp.sin(emb))

        def _apply_rope(t, cos, sin):
            t1, t2 = jnp.split(t, 2, axis=-1)
            rot = jnp.concatenate([-t2, t1], axis=-1)
            return t * cos[None, :, None, :] + rot * sin[None, :, None, :]
        B, S, _ = x.shape
        h = _rmsnorm(x, ln1_w)
        qkv = jnp.einsum('bsh,oh->bso', h, wqkv)
        q = qkv[..., :NH * HD].reshape(B, S, NH, HD)
        k = qkv[..., NH * HD:(NH + NKV) * HD].reshape(B, S, NKV, HD)
        v = qkv[..., (NH + NKV) * HD:].reshape(B, S, NKV, HD)
        cos, sin = _rope_tables(S)
        q = _apply_rope(q, cos, sin)
        k = _apply_rope(k, cos, sin)
        groups = NH // NKV
        k = jnp.repeat(k, groups, axis=2)
        v = jnp.repeat(v, groups, axis=2)
        scale = HD ** (-0.5)
        scores = jnp.einsum('bqhd,bkhd->bhqk', q, k) * scale
        causal = jnp.tril(jnp.ones((S, S), dtype=bool))
        scores = jnp.where(causal[None, None], scores, jnp.finfo(scores.dtype).min)
        probs = jax.nn.softmax(scores, axis=-1)
        attn = jnp.einsum('bhqk,bkhd->bqhd', probs, v).reshape(B, S, NH * HD)
        x = x + jnp.einsum('bso,ho->bsh', attn, wo)
        h = _rmsnorm(x, ln2_w).reshape(-1, HID)
        T = h.shape[0]
        logits = jnp.einsum('th,eh->te', h, gate_w)
        rprobs = jax.nn.softmax(logits.astype(jnp.float32), axis=-1)
        topw, topi = jax.lax.top_k(rprobs, TOPK)
        topw = topw / jnp.sum(topw, axis=-1, keepdims=True)
        wfull = jnp.zeros((T, E), jnp.float32).at[jnp.arange(T)[:, None], topi].set(topw)
        wfull = wfull.astype(h.dtype)
        out = jnp.zeros((T, HID), h.dtype)
        for e in range(E):
            w1 = w13[e, :FFN]
            w3 = w13[e, FFN:]
            g = jax.nn.silu(h @ w1.T) * (h @ w3.T)
            out = out + jnp.einsum('tf,hf->th', g, w2[e]) * wfull[:, e:e + 1]
        return x + out.reshape(B, S, HID)
    x = _layernorm(x + _L0_attn_ref(x, L0_attn_gate_w, L0_attn_gate_b, L0_attn_cand_w, L0_attn_cand_b, L0_attn_log_decay, L0_attn_out_w, L0_attn_out_b, L0_attn_norm_w), axis=-1)
    x = _layernorm(x + _L0_xattn_ref(ctx_1024, x, L0_xattn_ln1_g, L0_xattn_ln1_b, L0_xattn_ln2_g, L0_xattn_ln2_b, L0_xattn_Wq, L0_xattn_Wkv, L0_xattn_Wo), axis=-1)
    x = _layernorm(x + _L0_ffn_ref(x, L0_ffn_Wq, L0_ffn_bq, L0_ffn_Wk, L0_ffn_bk, L0_ffn_Wv, L0_ffn_bv, L0_ffn_Wo, L0_ffn_bo, L0_ffn_router_w, L0_ffn_router_b, L0_ffn_W1, L0_ffn_b1, L0_ffn_W2, L0_ffn_b2, L0_ffn_ln1_g, L0_ffn_ln1_b, L0_ffn_ln2_g, L0_ffn_ln2_b), axis=-1)
    x = _layernorm(x + _L1_attn_ref(x, L1_attn_norm1_w, L1_attn_norm2_w, L1_attn_conv_w, L1_attn_conv_b, L1_attn_wq, L1_attn_wk, L1_attn_wv, L1_attn_wb, L1_attn_wa, L1_attn_wo, L1_attn_wg, L1_attn_wu, L1_attn_wd), axis=-1)
    x = _layernorm(x + _L1_xattn_ref(x, ctx_1024, ctx_1024, L1_xattn_Wq, L1_xattn_bq, L1_xattn_Wk, L1_xattn_bk, L1_xattn_Wv, L1_xattn_bv, L1_xattn_Wo, L1_xattn_bo), axis=-1)
    x = _layernorm(x + _L1_ffn_ref(x, L1_ffn_ln1_w, L1_ffn_ln2_w, L1_ffn_wqkv, L1_ffn_wo, L1_ffn_gate_w, L1_ffn_w13, L1_ffn_w2), axis=-1)
    return x

_drawn_inputs = setup_inputs


def setup_inputs(seed=0):
    import zlib

    import numpy as np

    out = dict(_drawn_inputs(seed))
    spreads = {'L0_attn_gate_b': (0.0, 0.8),
     'L0_attn_cand_b': (0.0, 0.1),
     'L0_attn_log_decay': (-2.3025851249694824, 0.6),
     'L0_attn_out_b': (0.0, 0.1),
     'L0_attn_norm_w': (1.0, 0.2),
     'L0_xattn_ln1_g': (1.0, 0.2),
     'L0_xattn_ln1_b': (0.0, 0.1),
     'L0_xattn_ln2_g': (1.0, 0.2),
     'L0_xattn_ln2_b': (0.0, 0.1),
     'L0_ffn_bq': (0.0, 0.303),
     'L0_ffn_bk': (0.0, 0.8),
     'L0_ffn_bv': (0.0, 0.1),
     'L0_ffn_bo': (0.0, 0.1),
     'L0_ffn_b1': (0.0, 0.28),
     'L0_ffn_b2': (0.0, 0.1),
     'L0_ffn_ln1_g': (1.0, 0.2),
     'L0_ffn_ln1_b': (0.0, 0.1),
     'L0_ffn_ln2_g': (1.0, 0.2),
     'L0_ffn_ln2_b': (0.0, 0.1),
     'L1_attn_norm1_w': (1.0, 0.597),
     'L1_attn_norm2_w': (1.0, 0.2),
     'L1_attn_conv_b': (0.0, 0.1),
     'L1_ffn_ln1_w': (1.0, 0.6),
     'L1_ffn_ln2_w': (1.0, 0.6)}
    factors = {'L0_attn_gate_w': 3.965,
     'L1_attn_wb': 6.857,
     'L1_attn_wa': 8.0,
     'L1_xattn_bq': 8.0,
     'L1_xattn_bk': 8.0,
     'L1_xattn_bv': 5.658,
     'L1_xattn_bo': 5.736,
     'L1_ffn_wqkv': 4.6,
     'L1_ffn_wo': 4.381,
     'L1_ffn_gate_w': 8.0,
     'L1_ffn_w13': 8.0,
     'L1_ffn_w2': 8.0}
    for name, (base, spread) in spreads.items():
        noise = np.random.default_rng([zlib.crc32(name.encode()), seed]).standard_normal(out[name].shape)
        drawn = base * np.exp(spread * noise) if base else spread * noise
        out[name] = jnp.asarray(drawn.astype(out[name].dtype))
    for name, factor in factors.items():
        out[name] = (out[name] * factor).astype(out[name].dtype)
    return out
```

```python
from contextlib import ExitStack

import numpy as np
import concourse.bass as bass
from concourse import mybir

ALU = mybir.AluOpType
ACT = mybir.ActivationFunctionType
AX = mybir.AxisListType
F32 = mybir.dt.float32
I32 = mybir.dt.int32

B, T, D = 4, 512, 128
H, HD = 16, 8
XH, XD = 16, 64
S = 32
KEYS = T + S
QB = T // 128
UNITS = H * QB
E0, C0 = 4, 4
E1, C1 = 8, 2
FI, FC = 345, 3
FW = FI // FC
TAPS, CTAPS = 7, 4
BL = 4
NB = T // BL
CB = 16
NCB = NB // CB
NEG = -1.0e30
B7 = 25

VEC = {}
for _n, _w in (("gate_w", 7), ("cand_w", 7), ("gate_b", 1), ("cand_b", 1), ("log_decay", 1), ("out_b", 1),
               ("norm_w", 1), ("x_ln1_g", 1), ("x_ln1_b", 1), ("x_ln2_g", 1), ("x_ln2_b", 1), ("f_bq", 1),
               ("f_bk", 1), ("f_bv", 4), ("f_bo", 1), ("router_b", 1), ("f_b1", 16), ("f_b2", 4), ("f_ln1_g", 1),
               ("f_ln1_b", 1), ("f_ln2_g", 1), ("f_ln2_b", 1), ("norm1_w", 1), ("norm2_w", 1), ("conv_w", 4),
               ("conv_b", 1), ("c_bq", 1), ("c_bk", 1), ("c_bv", 1), ("c_bo", 1), ("m_ln1_w", 1), ("m_ln2_w", 1),
               ("eps_attn", 1), ("eps5", 1), ("eps6", 1), ("four", 1), ("head_mask", 16), ("tie_rank", 32)):
    VEC[_n] = (sum(w for _, w in VEC.values()), _w)
NVEC = sum(w for _, w in VEC.values())

GROUPS = {
    "wA": (("out_w", 128), ("ident", 128), ("ones", 128)),
    "wB": (("Wq", 1024), ("Wkv", 2048), ("Wo", 1024)),
    "wC": (("f_Wq", 128), ("f_Wk", 128), ("f_Wv", 512), ("f_Wo", 512), ("router", 128)),
    "wM0": (("W1", 2048), ("W2", 2048)),
    "wD": (("q_s", 256), ("k_s", 256), ("v_s", 128), ("b_s", 32), ("a_s", 32), ("o_s", 2048), ("wg", FI),
           ("wu", FI), ("wd", 384)),
    "wE": (("c_Wq", 128), ("c_Wk", 128), ("c_Wv", 128), ("c_Wo", 128), ("v_mask", 512)),
    "wF": (("m_q", 128), ("m_qr", 128), ("m_k", 128), ("m_kr", 128), ("m_v", 512), ("m_wo", 512), ("m_gate", 8),
           ("cos", 512), ("sin", 512), ("causal", 128), ("sel", 1024)),
    "wM1": (("w13", 4096), ("w2", 2048)),
}


def program(nc, xT, ctxT, vecs, groups, out, stages=6):
    ctx = ExitStack()
    with ctx:
        def sb(name, cols, dt=F32):
            return ctx.enter_context(nc.sbuf_tensor(name, [128, cols], dt))

        sem_of = {}

        def sem(name):
            if name not in sem_of:
                sem_of[name] = ctx.enter_context(nc.semaphore(name))
            return sem_of[name]

        vec = sb("vec", NVEC)
        x_cur = sb("x_cur", B * T).rearrange("p (b t) -> p b t", b=B)
        x_aux = sb("x_aux", B * T).rearrange("p (b t) -> p b t", b=B)
        cent = sb("cent", B * T).rearrange("p (b t) -> p b t", b=B)
        dev = sb("dev", B * T).rearrange("p (b t) -> p b t", b=B)
        ctx_in = sb("ctx_in", B * S)
        ctx_ln = sb("ctx_ln", B * S)
        stat = sb("stat", 64)
        width = {g: sum(w for _, w in cols) for g, cols in GROUPS.items()}
        reg1 = sb("reg1", max(width["wB"], width["wD"]))
        reg2 = sb("reg2", max(width["wM0"], width["wM1"]))
        place = {"wB": reg1, "wD": reg1, "wM0": reg2, "wM1": reg2}
        for g in ("wA", "wC", "wE", "wF"):
            place[g] = sb(g + "_sb", width[g])
        wt = {}
        for g, cols in GROUPS.items():
            at = 0
            for n, w in cols:
                wt[n] = place[g][:, at:at + w]
                at += w
        arena_cols = 27648
        arena = sb("arena", arena_cols)
        ps = ctx.enter_context(nc.psum_tensor("ps", [128, 8, 512], F32))

        def v(name, i=0, n=1):
            c = VEC[name][0] + i
            return vec[:, c:c + n]

        class Carve:
            def __init__(self):
                self.at = 0

            def __call__(self, cols):
                a = arena[:, self.at:self.at + cols]
                self.at += cols
                assert self.at <= arena_cols, self.at
                return a

        ident, ones = wt["ident"], wt["ones"]

        class Norm:
            count = 0

            def __init__(self, chunks, ready, gain=None, bias=None, eps="eps5", mean=True):
                self.chunks, self.ready, self.gain, self.bias, self.eps, self.mean = chunks, ready, gain, bias, eps, mean
                self.first = Norm.count
                Norm.count += len(chunks)

            def tmp(self, buf, n):
                _, _, w, slot = self.chunks[n]
                return buf[:, slot, 0:w]

            def pe(self, e):
                if self.mean:
                    for n, (src, _, w, slot) in enumerate(self.chunks):
                        e.wait_ge(*self.ready[n])
                        if self.first >= 1:
                            e.wait_ge(sem("norm_done"), self.first)
                        e.matmul(ps[:, slot, 0:w], ones, src, start=True, stop=True).then_inc(sem("norm_mean"), 1)
                for n, (src, _, w, slot) in enumerate(self.chunks):
                    if not self.mean and self.first >= 1:
                        e.wait_ge(sem("norm_done"), self.first)
                    e.wait_ge(sem("norm_sq"), self.first + n + 1)
                    i = e.matmul(ps[:, 4 + slot, 0:w], ones, self.tmp(dev, n), start=True, stop=True)
                    i.then_inc(sem("norm_var"), 1)

            def act(self, e):
                for n, (src, _, w, slot) in enumerate(self.chunks):
                    if self.mean:
                        e.wait_ge(sem("norm_cent"), self.first_mean + n + 1)
                    else:
                        e.wait_ge(*self.ready[n])
                    if self.first:
                        e.wait_ge(sem("norm_done"), self.first)
                    e.activation(self.tmp(dev, n), self.tmp(cent, n) if self.mean else src,
                                 ACT.Square).then_inc(sem("norm_sq"), 1)
                for n, (src, _, w, slot) in enumerate(self.chunks):
                    e.wait_ge(sem("norm_var"), self.first + n + 1)
                    e.activation(self.tmp(dev, n), ps[:, 4 + slot, 0:w], ACT.Ln,
                                 bias=v(self.eps)).then_inc(sem("norm_ln"), 1)
                for n, (src, _, w, slot) in enumerate(self.chunks):
                    e.wait_ge(sem("norm_ln"), self.first + n + 1)
                    e.activation(self.tmp(dev, n), self.tmp(dev, n), ACT.Exp, scale=-0.5).then_inc(sem("norm_dev"), 1)

            def dve(self, e):
                if self.mean:
                    for n, (src, _, w, slot) in enumerate(self.chunks):
                        e.wait_ge(sem("norm_mean"), self.first_mean + n + 1)
                        e.tensor_tensor(self.tmp(cent, n), src, ps[:, slot, 0:w],
                                        ALU.subtract).then_inc(sem("norm_cent"), 1)
                for n, (src, dst, w, slot) in enumerate(self.chunks):
                    c = self.tmp(cent, n) if self.mean else src
                    e.wait_ge(sem("norm_dev"), self.first + n + 1)
                    if self.mean:
                        e.wait_ge(sem("norm_cent"), self.first_mean + n + 1)
                    if self.gain is None:
                        e.tensor_tensor(dst, c, self.tmp(dev, n), ALU.mult).then_inc(sem("norm_done"), 1)
                    elif self.bias is None:
                        e.scalar_tensor_tensor(out=dst, in0=c, scalar=v(self.gain), in1=self.tmp(dev, n),
                                               op0=ALU.mult, op1=ALU.mult).then_inc(sem("norm_done"), 1)
                    else:
                        e.scalar_tensor_tensor(out=self.tmp(cent, n), in0=c, scalar=v(self.gain),
                                               in1=self.tmp(dev, n), op0=ALU.mult,
                                               op1=ALU.mult).then_inc(sem("norm_scaled"), 1)
                        e.wait_ge(sem("norm_scaled"), self.scaled + n + 1)
                        e.tensor_scalar(dst, self.tmp(cent, n), v(self.bias), None,
                                        ALU.add).then_inc(sem("norm_done"), 1)

            def done(self, n):
                return sem("norm_done"), self.first + n + 1

        mean_count, scaled_count = [0], [0]

        def make_norm(*a, **k):
            n = Norm(*a, **k)
            n.first_mean, n.scaled = mean_count[0], scaled_count[0]
            if n.mean:
                mean_count[0] += len(n.chunks)
            if n.bias is not None:
                scaled_count[0] += len(n.chunks)
            return n

        def batches(src, dst):
            return [(src[:, b, :], dst[:, b, :], T, b) for b in range(B)]

        def counted(name, base=0, step=1):
            return [(sem(name), base + step * (b + 1)) for b in range(B)]

        pe_steps, act_steps, dve_steps, pool_steps, sp_steps = [], [], [], [], []
        final = None

        def add_norm(n):
            pe_steps.append(n.pe)
            act_steps.append(n.act)
            dve_steps.append(n.dve)

        link_count = [0]

        def link(e, ins):
            link_count[0] += 1
            ins.then_inc(sem("dve_link"), 1)
            e.wait_ge(sem("dve_link"), link_count[0])

        def load_first(e):
            for g in ("wA",):
                e.dma_start(place[g][:, 0:width[g]], groups[g]).then_inc(sem("load_" + g), 16)
            for g in ("wB", "wC", "wM0", "wE", "wF"):
                e.dma_start(place[g][:, 0:width[g]], groups[g]).then_inc(sem("load_" + g), 16)
        P = TAPS // 2
        cv = Carve()
        x_pad = cv(B * (T + 2 * P)).rearrange("p (b t) -> p b t", b=B)
        gate = cv(B * T).rearrange("p (b t) -> p b t", b=B)
        cand = cv(B * T).rearrange("p (b t) -> p b t", b=B)
        hid = cv(B * T).rearrange("p (b t) -> p b t", b=B)
        y1 = cv(B * T).rearrange("p (b t) -> p b t", b=B)
        decay = stat[:, 63:64]

        def load_x(e):
            e.dma_start(vec[:, :], vecs).then_inc(sem("load_vec"), 16)
            e.dma_start(x_cur[:, :, :], xT).then_inc(sem("load_x"), 16)
            e.dma_start(x_pad[:, :, P:P + T], xT).then_inc(sem("load_x"), 16)
            e.dma_start(ctx_in[:, :], ctxT).then_inc(sem("load_ctx"), 16)
        sp_steps += [load_x, load_first]

        def b1_dve(e):
            e.memset(x_pad[:, :, 0:P], 0.0)
            link(e, e.memset(x_pad[:, :, P + T:], 0.0))
            e.wait_ge(sem("load_vec"), 16)
            e.wait_ge(sem("load_x"), 32)
            for k in range(TAPS):
                for n, (acc, w) in enumerate(((gate, "gate_w"), (cand, "cand_w"))):
                    src = x_pad[:, :, k:k + T]
                    if k == 0:
                        e.tensor_scalar(acc, src, v(w, k), None, ALU.mult).then_inc(sem(f"tap{n}"), 1)
                    else:
                        e.wait_ge(sem(f"tap{n}"), k)
                        e.scalar_tensor_tensor(out=acc, in0=src, scalar=v(w, k), in1=acc, op0=ALU.mult,
                                               op1=ALU.add).then_inc(sem(f"tap{n}"), 1)
            for b in range(B):
                e.wait_ge(sem("b1_cand"), b + 1)
                link(e, e.tensor_tensor(gate[:, b, :], gate[:, b, :], cand[:, b, :], ALU.mult))
                e.wait_ge(sem("b1_decay"), 1)
                e.tensor_tensor_scan(hid[:, b, :], decay.to_broadcast([128, T]), gate[:, b, :], 0.0, ALU.mult,
                                     ALU.add).then_inc(sem("b1_scan"), 1)
            for b in range(B):
                e.wait_ge(sem("b1_proj"), b + 1)
                e.scalar_tensor_tensor(out=y1[:, b, :], in0=ps[:, b, :], scalar=v("out_b"), in1=x_cur[:, b, :],
                                       op0=ALU.add, op1=ALU.add).then_inc(sem("b1_y"), 1)

        def b1_act(e):
            e.wait_ge(sem("load_vec"), 16)
            e.activation(decay, v("log_decay"), ACT.Exp).then_inc(sem("b1_decay"), 1)
            for b in range(B):
                e.wait_ge(sem("tap0"), TAPS)
                e.activation(gate[:, b, :], gate[:, b, :], ACT.Sigmoid, bias=v("gate_b"))
                e.wait_ge(sem("tap1"), TAPS)
                e.activation(cand[:, b, :], cand[:, b, :], ACT.Tanh, bias=v("cand_b")).then_inc(sem("b1_cand"), 1)

        def b1_pe(e):
            e.wait_ge(sem("load_wA"), 16)
            for b in range(B):
                e.wait_ge(sem("b1_scan"), b + 1)
                e.matmul(ps[:, b, :], wt["out_w"], hid[:, b, :], start=True, stop=True).then_inc(sem("b1_proj"), 1)
        pe_steps.append(b1_pe)
        act_steps.append(b1_act)
        dve_steps.append(b1_dve)
        n = make_norm(batches(y1, x_aux), counted("b1_y"), gain="norm_w", eps="eps_attn", mean=False)
        add_norm(n)

        def residual(name, k, prev):
            def f(e):
                for b in range(B):
                    e.wait_ge(*prev.done(b))
                    e.tensor_tensor(x_aux[:, b, :], x_aux[:, b, :], x_cur[:, b, :], ALU.add).then_inc(sem(name), 1)
            return f
        dve_steps.append(residual("b1_sum", 0, n))
        n = make_norm(batches(x_aux, x_cur), counted("b1_sum"))
        add_norm(n)
        final = n

        class Attn:
            def __init__(self, k, wide=False, causal=False):
                self.k, self.wide, self.causal = k, wide, causal
                self.base = k * B * UNITS
                c = Carve()
                if wide:
                    self.slots = 4
                    self.pt = c(4 * 4 * T).rearrange("p (s k q) -> p s k q", s=4, k=4)
                    self.ptc = c(4 * T).rearrange("p (s q) -> p s q", s=4)
                    self.p = c(8 * KEYS).rearrange("p (s k) -> p s k", s=8)
                    self.np = 8
                    self.qz = c(4 * T).rearrange("p (a r t) -> p a r t", a=2, r=2)
                    self.kt = c(2 * KEYS).rearrange("p (a t) -> p a t", a=2)
                    self.vv = c(4 * XH * XD).rearrange("p (k n) -> p k n", k=4)
                    self.vc = c(XH * XD)
                    self.kc = c(8 * B * S).rearrange("p (h n) -> p h n", h=8)
                else:
                    self.slots = 8
                    self.pt = c(8 * 4 * T).rearrange("p (s k q) -> p s k q", s=8, k=4)
                    self.p = c(4 * T).rearrange("p (s k) -> p s k", s=4)
                    self.np = 4
                    self.qt, self.kt = c(T), c(T)
                    self.qm = c(2 * T).rearrange("p (a t) -> p a t", a=2)
                    self.vv = c(4 * T).rearrange("p (k n) -> p k n", k=4)
                    self.x2 = c(T * B).rearrange("p (b t) -> p b t", b=B) if causal else None
                    self.ot = cent
                self.nm = stat[:, 0:4]
                self.sm = stat[:, 4:8]
                self.rs = stat[:, 8:12]

            def keys(self, u):
                return (u % QB + 1) * 128 if self.causal else (KEYS if self.wide else T)

            def s_view(self, u):
                if self.wide:
                    return ps[:, 2 * (u % 2):2 * (u % 2) + 2, 0:KEYS // 2]
                return ps[:, u % 4, 0:self.keys(u)]

            def p_view(self, u):
                if self.wide:
                    return self.p[:, u % self.np, :].rearrange("p (a k) -> p a k", a=2)
                return self.p[:, u % self.np, 0:self.keys(u)]

            def scores(self, e, b, u):
                n = self.base + b * UNITS + u
                h, q = u // QB, u % QB
                deep = 2 if self.wide else 4
                if n - deep >= 0:
                    e.wait_ge(sem("exp_done"), n - deep + 1)
                if self.wide:
                    e.wait_ge(sem("bank7_read"), b * B7 + 2 * (h // 2 + 1) + max(h // 2 - 2, 0))
                    e.wait_ge(sem("ctx_keys"), b * 8 + h // 2 + 1)
                    for a in range(2):
                        i = e.matmul(ps[:, 2 * (u % 2) + a, 0:KEYS // 2],
                                     self.qz[:, h // 2 % 2, h % 2, q * 128:q * 128 + 128],
                                     self.kt[:, h // 2 % 2, a * KEYS // 2:(a + 1) * KEYS // 2], start=True, stop=True)
                else:
                    e.wait_ge(sem("q_masked"), self.qm0 + b * H + h + 1)
                    i = e.matmul(self.s_view(u), self.qm[:, h % 2, q * 128:q * 128 + 128], self.kt[:, 0:self.keys(u)],
                                 start=True, stop=True)
                i.then_inc(sem("scored"), 1)

            def neg_max(self, e, b, u):
                n = self.base + b * UNITS + u
                e.wait_ge(sem("scored"), n + 1)
                if n >= 4:
                    e.wait_ge(sem("exp_done"), n - 3)
                if self.causal:
                    q = u % QB
                    link(e, e.tensor_tensor(ps[:, u % 4, q * 128:q * 128 + 128], ps[:, u % 4, q * 128:q * 128 + 128],
                                            wt["causal"], ALU.add))
                e.tensor_reduce(self.nm[:, u % 4:u % 4 + 1], self.s_view(u), AX.XY if self.wide else AX.X, ALU.max,
                                negate=True).then_inc(sem("max_done"), 1)

            def exp(self, e, b, u):
                n = self.base + b * UNITS + u
                e.wait_ge(sem("max_done"), n + 1)
                if self.wide:
                    if u % QB == 0 and n // QB >= 2:
                        e.wait_ge(sem("ctx_turned"), n // QB - 1)
                elif n - self.base >= 4:
                    e.wait_ge(sem("transposed"), n - 3)
                e.activation(self.p_view(u), self.s_view(u), ACT.Exp, bias=self.nm[:, u % 4:u % 4 + 1],
                             accum_out=self.sm[:, u % 4:u % 4 + 1]).then_inc(sem("exp_done"), 1)

            def normalise(self, e, b, u):
                n = self.base + b * UNITS + u
                e.wait_ge(sem("exp_done"), n + 1)
                i = e.reciprocal(self.rs[:, u % 4:u % 4 + 1], self.sm[:, u % 4:u % 4 + 1])
                link(e, i)
                w = self.keys(u)
                e.tensor_scalar(self.p[:, u % self.np, 0:w], self.p[:, u % self.np, 0:w], self.rs[:, u % 4:u % 4 + 1], None,
                                ALU.mult).then_inc(sem("prob_done"), 1)

            def transpose(self, e, b, u):
                n = self.base + b * UNITS + u
                e.wait_ge(sem("prob_done"), n + 1)
                if n >= 2:
                    e.wait_ge(sem("evacuated"), n - 1)
                for k in range((u % QB + 1) if self.causal else 4):
                    i = e.transpose(ps[:, 4 + u % 2, k * 128:k * 128 + 128], self.p[:, u % self.np, k * 128:k * 128 + 128],
                                    ident)
                i.then_inc(sem("transposed"), 1)
                if self.wide and u % QB == QB - 1:
                    if b * XH + u // QB >= 1:
                        e.wait_ge(sem("ctx_probs"), b * XH + u // QB)
                    for q in range(QB):
                        i = e.transpose(ps[0:S, 6, q * 128:q * 128 + 128],
                                        self.p[:, (u - QB + 1 + q) % self.np, T:KEYS], ident)
                    i.then_inc(sem("ctx_turned"), 1)

            def evacuate(self, e, b, u):
                n = self.base + b * UNITS + u
                h, q = u // QB, u % QB
                e.wait_ge(sem("transposed"), n + 1)
                if q == 0:
                    g = (b * H + h - self.slots) // self.per
                    if g >= 0:
                        e.wait_ge(sem("pv_done"), self.pv0 + g + 1)
                kk = (q + 1) if self.causal else 4
                e.copy(self.pt[:, h % self.slots, 0:kk, q * 128:q * 128 + 128],
                       ps[:, 4 + u % 2, 0:kk * 128].rearrange("p (k q) -> p k q", k=kk)).then_inc(sem("evacuated"), 1)

            def pv(self, e, b, g, parts=range(4)):
                per, w = self.per, 128 // self.per
                h0 = g * per
                bank = 7 if self.wide else 6
                if parts[0] == 0:
                    e.wait_ge(sem("evacuated"), self.base + b * UNITS + (h0 + per) * QB)
                    if self.wide:
                        e.wait_ge(sem("ctx_probs"), b * XH + h0 + per)
                        self.bank_wait(e)
                    elif self.pv0 + b * (H // per) + g >= 1:
                        e.wait_ge(sem("pv_read"), self.pr0 + b * (H // per) + g)
                last = 4 if self.wide else 3
                for k in parts:
                    for j in range(per):
                        h = h0 + j
                        q0 = k * 128 if self.causal else 0
                        v_of = self.vv[:, k, :] if k < 4 else self.vc
                        p_of = self.pt[:, h % self.slots, k, q0:T] if k < 4 else self.ptc[:, h % self.slots, :]
                        i = e.matmul(ps[w * j:w * j + w, bank, q0:T], v_of[:, h * w:h * w + w], p_of,
                                     start=(k == 0), stop=(k == last), skip_group_check=True)
                if parts[-1] == last:
                    i.then_inc(sem("pv_done"), 1)
                    if self.wide:
                        self.bank_used()

        if stages >= 2:
            n_lat = make_norm(batches(x_cur, x_aux), [final.done(b) for b in range(B)], gain="x_ln2_g", bias="x_ln2_b")
            add_norm(n_lat)
            n_ctx = make_norm([(ctx_in[:, :], ctx_ln[:, :], B * S, 0)], [(sem("load_ctx"), 16)], gain="x_ln1_g",
                              bias="x_ln1_b")
            add_norm(n_ctx)
            ot_lo, ot_hi = cent, dev
            at = Attn(0, wide=True)
            at.per, at.pv0 = 2, 0
            Wq, Wkv, Wo = wt["Wq"], wt["Wkv"], wt["Wo"]

            def ot_of(g):
                return (ot_lo if g < 4 else ot_hi)[:, g % 4, :]

            def b2_pe(e):
                uses = [0]

                def b7_wait(e2):
                    if uses[0] >= 1:
                        e2.wait_ge(sem("bank7_read"), uses[0])

                def b7_used():
                    uses[0] += 1
                at.bank_wait, at.bank_used = b7_wait, b7_used
                e.wait_ge(sem("load_wB"), 16)
                e.wait_ge(*n_ctx.done(0))
                for hp in range(8):
                    if hp == 4:
                        e.wait_ge(sem("ctx_k_read"), 4)
                    i = e.matmul(ps[:, hp % 4, 0:B * S], Wkv[:, hp * 128:hp * 128 + 128], ctx_ln[:, :], start=True,
                                 stop=True)
                    i.then_inc(sem("ctx_k_proj"), 1)

                def qproj(b, hp):
                    b7_wait(e)
                    e.matmul(ps[:, 7, :], Wq[:, hp * 128:hp * 128 + 128], x_aux[:, b, :], start=True,
                             stop=True).then_inc(sem("bank7_written"), 1)
                    b7_used()

                def kproj(b, hp):
                    b7_wait(e)
                    e.matmul(ps[:, 7, :], Wkv[:, hp * 128:hp * 128 + 128], x_aux[:, b, :], start=True,
                             stop=True).then_inc(sem("bank7_written"), 1)
                    b7_used()
                for b in range(B):
                    e.wait_ge(*n_lat.done(b))
                    for k in range(5):
                        src = x_aux[:, b, k * 128:k * 128 + 128] if k < 4 else ctx_ln[:, b * S:b * S + S]
                        m = 128 if k < 4 else S
                        for a in range(2):
                            j = b * 10 + 2 * k + a
                            if j >= 2:
                                e.wait_ge(sem("v_read"), j - 1)
                            if b >= 1 and j % 10 < 2:
                                e.wait_ge(sem("evacuated"), at.base + b * UNITS)
                            e.matmul(ps[0:m, 4 + j % 2, :], src, Wkv[:, 1024 + a * 512:1536 + a * 512], start=True,
                                     stop=True).then_inc(sem("v_proj"), 1)
                    qproj(b, 0)
                    kproj(b, 0)
                    e.wait_ge(sem("v_read"), 10 * b + 10)
                    for i in range(UNITS + 8):
                        if i < UNITS:
                            at.scores(e, b, i)
                        if 2 <= i < UNITS + 2:
                            at.transpose(e, b, i - 2)
                        hp, r = i // 8, i % 8
                        if r == 1 and hp < 7:
                            qproj(b, hp + 1)
                        if r == 2 and hp < 7:
                            kproj(b, hp + 1)
                        if r >= 3 and hp >= 1:
                            at.pv(e, b, hp - 1, [r - 3])
                    b7_wait(e)
                    for hp in range(8):
                        i = e.matmul(ps[:, 7, :], Wo[:, hp * 128:hp * 128 + 128], ot_of(hp), start=(hp == 0),
                                     stop=(hp == 7))
                    i.then_inc(sem("b2_out"), 1)
                    b7_used()

            def b2_act(e):
                e.wait_ge(sem("b2_zeros"), 1)
                for hp in range(8):
                    e.wait_ge(sem("ctx_k_proj"), hp + 1)
                    e.copy(at.kc[:, hp, :], ps[:, hp % 4, 0:B * S]).then_inc(sem("ctx_k_read"), 1)
                for b in range(B):
                    for k in range(5):
                        m = 128 if k < 4 else S
                        if b >= 1 and k == 0:
                            e.wait_ge(sem("pv_done"), 8 * b)
                        for a in range(2):
                            j = b * 10 + 2 * k + a
                            e.wait_ge(sem("v_proj"), j + 1)
                            dst = at.vv[:, k, a * 512:a * 512 + 512] if k < 4 else at.vc[0:S, a * 512:a * 512 + 512]
                            e.copy(dst, ps[0:m, 4 + j % 2, :]).then_inc(sem("v_read"), 1)
                    for i in range(UNITS + 2):
                        if i < UNITS:
                            at.exp(e, b, i)
                        if i >= 2:
                            at.evacuate(e, b, i - 2)

            def b2_dve(e):
                written, pvs = [0], [0]
                e.memset(at.ptc[:, :, :], 0.0)
                e.memset(at.vc, 0.0)
                e.memset(at.qz[:, :, :, :], 0.0).then_inc(sem("b2_zeros"), 1)
                e.wait_ge(sem("b2_zeros"), 1)

                def qread(b, hp):
                    written[0] += 1
                    e.wait_ge(sem("bank7_written"), written[0])
                    if b * 8 + hp >= 2:
                        e.wait_ge(sem("scored"), (b * 8 + hp - 1) * 8)
                    for r in range(2):
                        i = e.tensor_scalar(at.qz[64 * r:64 * r + 64, hp % 2, r, :], ps[64 * r:64 * r + 64, 7, :],
                                            0.125, None, ALU.mult)
                    i.then_inc(sem("bank7_read"), 1)

                def kread(b, hp):
                    written[0] += 1
                    e.wait_ge(sem("bank7_written"), written[0])
                    e.tensor_copy(at.kt[:, hp % 2, 0:T], ps[:, 7, :]).then_inc(sem("bank7_read"), 1)

                def pread(b, g):
                    pvs[0] += 1
                    e.wait_ge(sem("pv_done"), pvs[0])
                    if b >= 1 and g == 0:
                        e.wait_ge(sem("b2_out"), b)
                    e.tensor_copy(ot_of(g), ps[:, 7, :]).then_inc(sem("bank7_read"), 1)

                def cread(b, h):
                    n = b * XH + h
                    e.wait_ge(sem("ctx_turned"), n + 1)
                    if n >= 4:
                        e.wait_ge(sem("pv_done"), (n - 4) // 2 + 1)
                    e.tensor_copy(at.ptc[0:S, h % 4, :], ps[0:S, 6, :]).then_inc(sem("ctx_probs"), 1)
                for b in range(B):
                    qread(b, 0)
                    kread(b, 0)
                    for i in range(UNITS + 9):
                        if i < UNITS:
                            at.neg_max(e, b, i)
                        if 1 <= i <= UNITS:
                            at.normalise(e, b, i - 1)
                        if i >= 6 and (i - 2) % 4 == 0 and (i - 2) // 4 - 1 < XH:
                            cread(b, (i - 2) // 4 - 1)
                        hp, r = i // 8, i % 8
                        if r == 0 and hp >= 2:
                            pread(b, hp - 2)
                        if r == 1 and hp < 7:
                            qread(b, hp + 1)
                        if r == 2 and hp < 7:
                            kread(b, hp + 1)
                    e.wait_ge(sem("b2_out"), b + 1)
                    e.tensor_tensor(x_aux[:, b, :], ps[:, 7, :], x_cur[:, b, :], ALU.add).then_inc(sem("bank7_read"), 1)

            def b2_pool(e):
                for b in range(B):
                    for hp in range(8):
                        n = b * 8 + hp
                        e.wait_ge(sem("ctx_k_read"), hp + 1)
                        if n >= 2:
                            e.wait_ge(sem("scored"), (n - 1) * 8)
                        e.tensor_copy(at.kt[:, hp % 2, T:KEYS],
                                      at.kc[:, hp, b * S:b * S + S]).then_inc(sem("ctx_keys"), 1)

            pe_steps.append(b2_pe)
            act_steps.append(b2_act)
            dve_steps.append(b2_dve)
            pool_steps.append(b2_pool)
            n = make_norm(batches(x_aux, x_cur), counted("bank7_read", 0, B7))
            add_norm(n)
            final = n

        def narrow(at, src, src_ready, dst, tag, load, wq, wk, wv, wo, rope=None, biased=False):
            nproj = (4 if rope else 2) + 4
            at.per, at.pv0, at.pr0 = 4, 8 * B + at.idx * 4 * B, at.idx * 4 * B
            at.qm0 = at.idx * B * H
            SC = HD ** -0.5
            proj, read, outs = sem(tag + "_proj"), sem(tag + "_proj_read"), sem(tag + "_out")
            qrdy = sem(tag + "_q_ready")

            def pe(e):
                e.wait_ge(sem("load_" + load), 16)
                e.wait_ge(*src_ready[B - 1])
                for b in range(B):
                    if b:
                        e.wait_ge(sem("evacuated"), at.base + b * UNITS)
                        e.wait_ge(sem(tag + "_res"), b)
                    mats = [wt[w] for w in ([wq, rope[0], wk, rope[1]] if rope else [wq, wk])]
                    for j in range(nproj):
                        if j >= 4:
                            e.wait_ge(read, nproj * b + j - 3)
                        k = j - len(mats)
                        if k < 0:
                            i = e.matmul(ps[:, 4 + j % 4, :], mats[j], src[:, b, :], start=True, stop=True)
                        else:
                            i = e.matmul(ps[:, 4 + j % 4, :], src[:, b, k * 128:k * 128 + 128], wt[wv], start=True,
                                         stop=True)
                        i.then_inc(proj, 1)
                    e.wait_ge(read, nproj * (b + 1))
                    for i in range(UNITS + 4):
                        if i < UNITS:
                            at.scores(e, b, i)
                        if 2 <= i < UNITS + 2:
                            at.transpose(e, b, i - 2)
                        if i >= 19 and (i - 19) % 16 == 0:
                            at.pv(e, b, (i - 19) // 16)
                    e.wait_ge(sem("pv_read"), at.pr0 + 4 * (b + 1))
                    for g in range(4):
                        i = e.matmul(ps[:, 7, :], wt[wo][:, g * 128:g * 128 + 128], at.ot[:, g, :], start=(g == 0),
                                     stop=(g == 3))
                    i.then_inc(outs, 1)

            def act(e):
                for b in range(B):
                    for i in range(UNITS + 2):
                        if i < UNITS:
                            at.exp(e, b, i)
                        if i >= 2:
                            at.evacuate(e, b, i - 2)

            def dve(e):
                def rotate(b, j, dst_, scale):
                    e.wait_ge(proj, nproj * b + j + 1)
                    e.scalar_tensor_tensor(out=dev[:, j, :], in0=ps[:, 4 + j, :], scalar=scale, in1=wt["cos"],
                                           op0=ALU.mult, op1=ALU.mult).then_inc(read, 1)
                    e.wait_ge(proj, nproj * b + j + 2)
                    e.scalar_tensor_tensor(out=dev[:, j + 1, :], in0=ps[:, 5 + j, :], scalar=scale, in1=wt["sin"],
                                           op0=ALU.mult, op1=ALU.mult).then_inc(read, 1)
                    e.wait_ge(read, nproj * b + j + 2)
                    return e.tensor_tensor(dst_, dev[:, j, :], dev[:, j + 1, :], ALU.add)
                for b in range(B):
                    if b:
                        e.wait_ge(sem("q_masked"), at.qm0 + b * H)
                        e.wait_ge(sem("scored"), at.base + b * UNITS)
                    if rope:
                        if b:
                            e.wait_ge(qrdy, b)
                            e.wait_ge(sem(tag + "_k_ready"), b)
                        rotate(b, 0, at.qt, SC).then_inc(qrdy, 1)
                        rotate(b, 2, at.kt, 1.0).then_inc(sem(tag + "_k_ready"), 1)
                    else:
                        e.wait_ge(proj, nproj * b + 1)
                        e.tensor_scalar(at.qt, ps[:, 4, :], v("f_bq"), SC, ALU.add, ALU.mult).then_inc(read, 1)
                        e.wait_ge(proj, nproj * b + 2)
                        e.tensor_scalar(at.kt, ps[:, 5, :], v("f_bk"), None, ALU.add).then_inc(read, 1)
                    if b:
                        e.wait_ge(sem("pv_done"), at.pv0 + 4 * b)
                    for k in range(4):
                        j = nproj - 4 + k
                        e.wait_ge(proj, nproj * b + j + 1)
                        e.tensor_copy(at.vv[:, k, :], ps[:, 4 + j % 4, :]).then_inc(read, 1)
                    for i in range(UNITS + 5):
                        if i < UNITS:
                            at.neg_max(e, b, i)
                        if 1 <= i <= UNITS:
                            at.normalise(e, b, i - 1)
                        if i >= 20 and (i - 20) % 16 == 0:
                            g = (i - 20) // 16
                            e.wait_ge(sem("pv_done"), at.pv0 + 4 * b + g + 1)
                            if b and g == 0:
                                e.wait_ge(outs, b)
                            if biased:
                                o = e.tensor_scalar(at.ot[:, g, :], ps[:, 6, :], v("f_bv", g), None, ALU.add)
                            else:
                                o = e.tensor_copy(at.ot[:, g, :], ps[:, 6, :])
                            o.then_inc(sem("pv_read"), 1)
                    e.wait_ge(outs, b + 1)
                    if biased:
                        o = e.scalar_tensor_tensor(out=dst[:, b, :], in0=ps[:, 7, :], scalar=v("f_bo"),
                                                   in1=x_cur[:, b, :], op0=ALU.add, op1=ALU.add)
                    else:
                        o = e.tensor_tensor(dst[:, b, :], ps[:, 7, :], x_cur[:, b, :], ALU.add)
                    o.then_inc(sem(tag + "_res"), 1)

            def pool(e):
                for b in range(B):
                    for h in range(H):
                        n = b * H + h
                        if h == 0:
                            e.wait_ge(qrdy if rope else read, (b + 1) if rope else nproj * b + 1)
                        if n >= 2:
                            e.wait_ge(sem("scored"), at.base + (n - 1) * QB)
                        e.tensor_scalar(at.qm[:, h % 2, :], at.qt, v("head_mask", h), 1.0, ALU.mult,
                                        ALU.mult).then_inc(sem("q_masked"), 1)
            pe_steps.append(pe)
            act_steps.append(act)
            dve_steps.append(dve)
            pool_steps.append(pool)

        if stages >= 3:
            at3 = Attn(1)
            at3.idx = 0
            narrow(at3, x_cur, [final.done(b) for b in range(B)], x_aux, "b3", "wC", "f_Wq", "f_Wk", "f_Wv", "f_Wo",
                   biased=True)
            n3 = make_norm(batches(x_aux, x_aux), counted("b3_res"), gain="f_ln1_g", bias="f_ln1_b")
            add_norm(n3)

            c = Carve()
            mask = c(2 * 4 * T).rearrange("p (a e t) -> p a e t", a=2, e=4)
            act_r = c(4 * T).rearrange("p (s t) -> p s t", s=4)
            key, key_f, key_c = c(T), c(T), c(T)
            key_i = c(T).bitcast(I32)
            W1, W2 = wt["W1"], wt["W2"]
            NI = E0 * C0

            def moe_pe(e):
                e.wait_ge(sem("load_wM0"), 16)

                def route(b):
                    e.wait_ge(*n3.done(b))
                    if b == 0:
                        e.wait_ge(*n3.done(3))
                    if b >= 2:
                        e.wait_ge(sem("key_read"), b - 1)
                    e.matmul(ps[:, 6 + b % 2, :], wt["router"], x_aux[:, b, :], start=True,
                             stop=True).then_inc(sem("routed"), 1)

                def down(b, i):
                    e.wait_ge(sem("relu_gated"), b * NI + i + 1)
                    if i == 0 and b >= 2:
                        e.wait_ge(sem("b3_sum"), b - 1)
                    e.matmul(ps[:, 4 + b % 2, :], W2[:, i * 128:i * 128 + 128], act_r[:, i % 4, :], start=(i == 0),
                             stop=(i == NI - 1)).then_inc(sem("moe_down"), 1)
                route(0)
                for b in range(B):
                    if b + 1 < B:
                        route(b + 1)
                    for i in range(NI + 3):
                        if i < NI:
                            n = b * NI + i
                            if n >= 4:
                                e.wait_ge(sem("relu_done"), n - 3)
                            e.matmul(ps[:, i % 4, :], W1[:, i * 128:i * 128 + 128], x_aux[:, b, :], start=True,
                                     stop=True).then_inc(sem("moe_up"), 1)
                        if i >= 3:
                            down(b, i - 3)

            def moe_act(e):
                for n in range(B * NI):
                    e.wait_ge(sem("moe_up"), n + 1)
                    if n >= 4:
                        e.wait_ge(sem("moe_down"), n - 3)
                    e.activation(act_r[:, n % 4, :], ps[:, n % 4, :], ACT.Relu,
                                 bias=v("f_b1", n % NI)).then_inc(sem("relu_done"), 1)

            def moe_pool(e):
                for n in range(B * NI):
                    b, ex = n // NI, n % NI // C0
                    e.wait_ge(sem("masks"), b + 1)
                    e.wait_ge(sem("relu_done"), n + 1)
                    e.tensor_tensor(act_r[:, n % 4, :], act_r[:, n % 4, :], mask[:, b % 2, ex, :],
                                    ALU.mult).then_inc(sem("relu_gated"), 1)

            def moe_dve(e):
                def masks(b):
                    e.wait_ge(sem("routed"), b + 1)
                    if b >= 2:
                        e.wait_ge(sem("relu_gated"), (b - 1) * NI)
                    i = e.tensor_scalar(key, ps[:, 6 + b % 2, :], v("router_b"), None, ALU.add)
                    i.then_inc(sem("key_read"), 1)
                    e.wait_ge(sem("key_read"), b + 1)
                    link(e, e.tensor_copy(key_i, key))
                    link(e, e.tensor_copy(key_f, key_i))
                    link(e, e.tensor_tensor(key_c, key_f, key, ALU.is_gt))
                    link(e, e.tensor_tensor(key_f, key_f, key_c, ALU.subtract))
                    link(e, e.tensor_copy(key_i, key_f))
                    link(e, e.tensor_scalar(key_i, key_i, E0 - 1, None, ALU.bitwise_and))
                    link(e, e.tensor_copy(key_f, key_i))
                    for ex in range(E0):
                        i = e.tensor_scalar(mask[:, b % 2, ex, :], key_f, float(ex), None, ALU.is_equal)
                    i.then_inc(sem("masks"), 1)

                def total(b):
                    e.wait_ge(sem("moe_down"), (b + 1) * NI)
                    e.wait_ge(sem("masks"), b + 1)
                    link(e, e.tensor_tensor(x_aux[:, b, :], ps[:, 4 + b % 2, :], x_aux[:, b, :], ALU.add))
                    for ex in range(E0):
                        i = e.scalar_tensor_tensor(out=x_aux[:, b, :], in0=mask[:, b % 2, ex, :],
                                                   scalar=v("f_b2", ex), in1=x_aux[:, b, :], op0=ALU.mult, op1=ALU.add)
                        if ex < E0 - 1:
                            link(e, i)
                    i.then_inc(sem("b3_sum"), 1)
                masks(0)
                for b in range(B):
                    if b + 1 < B:
                        masks(b + 1)
                    total(b)

            def moe_sp(e):
                e.wait_ge(sem("b2_out"), B)
                e.dma_start(reg1[:, 0:width["wD"]], groups["wD"]).then_inc(sem("load_wD"), 16)
                e.wait_ge(sem("b4_o" if stages >= 4 else "moe_down"), 1)
                e.dma_start(reg2[:, 0:width["wM1"]], groups["wM1"]).then_inc(sem("load_wM1"), 16)
            pe_steps.append(moe_pe)
            act_steps.append(moe_act)
            pool_steps.append(moe_pool)
            dve_steps.append(moe_dve)
            sp_steps.append(moe_sp)
            n = make_norm(batches(x_aux, x_aux), counted("b3_sum"), gain="f_ln2_g", bias="f_ln2_b")
            add_norm(n)
            dve_steps.append(residual("b3_both", 0, n))
            n = make_norm(batches(x_aux, x_cur), counted("b3_both"))
            add_norm(n)
            final = n

        def gated(tag, per, rows, src, src_done, w_gate, w_up, w_down, act_r, weight=None, load=None, weight_ready=None,
                  extra=None):
            s_up, s_silu, s_prod, s_down = (sem(f"{tag}_{x}") for x in ("up", "silu", "prod", "down"))
            s_in = sem(tag + "_gated") if weight else s_prod
            extra = extra or {}
            R = rows

            def pe(e):
                if load:
                    e.wait_ge(sem("load_" + load), 16)
                e.wait_ge(*src_done[B - 1])
                for step in extra.get("pe_first", ()):
                    step(e)
                for b in range(B):
                    for i in range(per + 2):
                        n = b * per + i
                        if i < per:
                            if n >= 2:
                                e.wait_ge(s_silu, n - 1)
                                e.wait_ge(s_prod, n - 1)
                            e.matmul(ps[0:R, n % 2, :], w_gate(i), src[:, b, :], start=True, stop=True)
                            e.matmul(ps[0:R, 2 + n % 2, :], w_up(i), src[:, b, :], start=True,
                                     stop=True).then_inc(s_up, 1)
                        if i >= 2:
                            m = n - 2
                            e.wait_ge(s_in, m + 1)
                            if i == 2 and b >= 2:
                                e.wait_ge(sem(tag + "_sum"), b - 1)
                            e.matmul(ps[:, 4 + b % 2, :], w_down(i - 2), act_r[0:R, m % 4, :], start=(i == 2),
                                     stop=(i == per + 1)).then_inc(s_down, 1)
                        if "pe" in extra:
                            extra["pe"](e, b, i)

            def act(e):
                for step in extra.get("act_first", ()):
                    step(e)
                for n in range(B * per):
                    e.wait_ge(s_up, n + 1)
                    if n >= 4:
                        e.wait_ge(s_down, n - 3)
                    e.activation(act_r[0:R, n % 4, :], ps[0:R, n % 2, :], ACT.Silu).then_inc(s_silu, 1)
                    if "act" in extra:
                        extra["act"](e, n // per, n % per)

            def dve(e):
                for step in extra.get("dve_first", ()):
                    step(e)
                for b in range(B):
                    for i in range(per):
                        n = b * per + i
                        e.wait_ge(s_silu, n + 1)
                        e.tensor_tensor(act_r[0:R, n % 4, :], act_r[0:R, n % 4, :], ps[0:R, 2 + n % 2, :],
                                        ALU.mult).then_inc(s_prod, 1)
                        if "dve" in extra:
                            extra["dve"](e, b, i)
                    e.wait_ge(s_down, (b + 1) * per)
                    extra["total"](e, b).then_inc(sem(tag + "_sum"), 1)

            def pool(e):
                for b in range(B):
                    for i in range(per):
                        n = b * per + i
                        if i == 0:
                            e.wait_ge(*weight_ready(b))
                        e.wait_ge(s_prod, n + 1)
                        e.tensor_tensor(act_r[:, n % 4, :], act_r[:, n % 4, :], weight(b, i),
                                        ALU.mult).then_inc(s_in, 1)
            pe_steps.append(pe)
            act_steps.append(act)
            dve_steps.append(dve)
            if weight:
                pool_steps.append(pool)

        if stages >= 4:
            c = Carve()
            blocks = lambda x: x.rearrange("p (n i d) -> p n i d", i=BL, d=HD)
            q_raw = c(T * HD).rearrange("p (t d) -> p t d", d=HD)
            k_hat = c(T * HD).rearrange("p (t d) -> p t d", d=HD)
            y_flat = c(T * 12)
            y = y_flat.rearrange("p (t w) -> p t w", w=12)
            hist_flat = c((NB + 1) * 32)
            hist = hist_flat.rearrange("p (n j d) -> p n j d", j=4, d=HD)
            terms_flat = c(2 * CB * 144)
            terms = terms_flat.rearrange("p (c n i j d) -> p (c n) i j d", c=2, n=CB, i=BL, j=4)
            alpha, beta, gamma, to_end, t_one, t_two = (c(T) for _ in range(6))
            rank1 = c(2 * 32 * (BL + 1)).rearrange("p (a j d l) -> p a j d l", a=2, j=4, l=BL + 1)
            k_sq = terms_flat[:, 0:T * HD].rearrange("p (t d) -> p t d", d=HD)
            prod_k = terms_flat
            q_sq = hist_flat[:, 0:T * HD].rearrange("p (t d) -> p t d", d=HD)
            kk_dot = hist_flat[:, 0:3 * T].rearrange("p (s n i) -> p s n i", s=3, i=BL)
            xp = y_flat[:, 0:B * (T + CTAPS - 1)].rearrange("p (b t) -> p b t", b=B)
            qk_dot = x_aux.rearrange("p s (n i) -> p s n i", i=BL)
            prod_q = (reg2[:, 0:T * HD], reg2[:, T * HD:T * HD + T * HD // 2])
            prod_o = reg2[:, 0:2 * CB * BL * 32].rearrange("p (c n i j d) -> p c n i j d", c=2, n=CB, i=BL, j=4)
            o_tmp = terms_flat[:, 0:4 * T].rearrange("p (n i j) -> p n i j", i=BL, j=4)
            r_k, r_q, coef = dev[:, 0, :], dev[:, 1, :], dev[:, 2, :]
            neg_delta = reg2[:, T * HD:T * (HD + 4)].rearrange("p (n i j) -> p n i j", i=BL, j=4)
            o_tok = cent.rearrange("p b t -> p (b t)").rearrange("p (t j) -> p t j", j=4)
            PADW = CTAPS - 1
            n = make_norm([(x_cur[:, b, :], xp[:, b, PADW:], T, b) for b in range(B)],
                          [final.done(b) for b in range(B)], gain="norm1_w", eps="eps6", mean=False)
            add_norm(n)
            n4 = n
            cols = [("a_s", 0), ("b_s", 0)] + [("k_s", d) for d in range(8)] + [("q_s", d) for d in range(8)] \
                + [("v_s", j) for j in range(4)]

            def b4_pe(e):
                e.wait_ge(sem("load_wD"), 16)
                e.wait_ge(sem("b4_xc"), 1)
                for g, (w, d) in enumerate(cols):
                    if 8 <= g < 10:
                        e.wait_ge(sem("b4_act_read"), g - 7)
                    elif g >= 10:
                        e.wait_ge(sem("b4_dve_read"), g - 9)
                    for b in range(B):
                        i = e.matmul(ps[32 * b:32 * b + 32, g % 8, :], wt[w][:, d * 32:d * 32 + 32], x_aux[:, b, :],
                                     start=True, stop=True)
                    i.then_inc(sem("b4_proj"), 1)

            def b4_act(e):
                e.wait_ge(sem("b4_conv"), CTAPS)
                e.activation(x_aux[:, :, :], x_aux[:, :, :], ACT.Silu, bias=v("conv_b")).then_inc(sem("b4_xc"), 1)
                e.wait_ge(sem("b4_proj"), 1)
                e.activation(alpha, ps[:, 0, :], ACT.Sigmoid, bias=v("four")).then_inc(sem("b4_act_read"), 1)
                e.wait_ge(sem("b4_proj"), 2)
                e.activation(beta, ps[:, 1, :], ACT.Sigmoid).then_inc(sem("b4_act_read"), 1)
                e.wait_ge(sem("b4_dve_read"), 8)
                e.activation(k_sq, k_hat, ACT.Square).then_inc(sem("b4_square"), 1)
                e.wait_ge(sem("b4_dve_read"), 16)
                e.activation(q_sq, q_raw, ACT.Square).then_inc(sem("b4_square"), 1)
                for n_, r in enumerate((r_k, r_q)):
                    e.wait_ge(sem("b4_len"), n_ + 1)
                    e.activation(r, r, ACT.Ln, bias=v("eps6")).then_inc(sem("b4_ln"), 1)
                    e.wait_ge(sem("b4_ln"), n_ + 1)
                    e.activation(r, r, ACT.Exp, scale=-0.5).then_inc(sem("b4_rlen"), 1)
                e.wait_ge(sem("b4_solved"), 1)
                for n_ in range(NB):
                    if n_:
                        e.wait_ge(sem("b4_state"), n_)
                    e.activation(rank1[:, n_ % 2, :, :, BL], hist[:, n_, :, :], ACT.Copy,
                                 scale=gamma[:, BL * n_ + BL - 1:BL * n_ + BL]).then_inc(sem("b4_carry"), 1)

            def per_d(x, n_=HD):
                return x.unsqueeze(2).to_broadcast([128, T, n_])

            def b4_dve(e):
                link(e, e.memset(xp[:, :, 0:PADW], 0.0))
                for b in range(B):
                    e.wait_ge(*n4.done(b))
                for k in range(CTAPS):
                    if k == 0:
                        i = e.tensor_scalar(x_aux[:, :, :], xp[:, :, 0:T], v("conv_w"), None, ALU.mult)
                    else:
                        e.wait_ge(sem("b4_conv"), k)
                        i = e.scalar_tensor_tensor(out=x_aux[:, :, :], in0=xp[:, :, k:k + T], scalar=v("conv_w", k),
                                                   in1=x_aux[:, :, :], op0=ALU.mult, op1=ALU.add)
                    i.then_inc(sem("b4_conv"), 1)
                for g in range(2, 22):
                    e.wait_ge(sem("b4_proj"), g + 1)
                    if g < 10:
                        i = e.tensor_copy(k_hat[:, :, g - 2], ps[:, g % 8, :])
                    elif g < 18:
                        i = e.tensor_copy(q_raw[:, :, g - 10], ps[:, g % 8, :])
                    else:
                        e.wait_ge(sem("b4_act_read"), 2)
                        i = e.scalar_tensor_tensor(out=y[:, :, g - 10], in0=ps[:, g % 8, :], scalar=-1.0,
                                                   in1=beta, op0=ALU.mult, op1=ALU.mult)
                    i.then_inc(sem("b4_dve_read"), 1)
                e.wait_ge(sem("b4_square"), 1)
                e.tensor_reduce(r_k, k_sq, AX.X, ALU.add).then_inc(sem("b4_len"), 1)
                e.wait_ge(sem("b4_square"), 2)
                e.tensor_reduce(r_q, q_sq, AX.X, ALU.add).then_inc(sem("b4_len"), 1)
                blk = lambda x: x.rearrange("p (n i) -> p n i", i=BL)
                a_, g_, e_, t1, t2, cf = (blk(x) for x in (alpha, gamma, to_end, t_one, t_two, coef))
                link(e, e.tensor_copy(gamma, alpha))
                for i in range(1, BL):
                    link(e, e.tensor_tensor(g_[:, :, i], g_[:, :, i - 1], a_[:, :, i], ALU.mult))
                e.tensor_tensor(t1[:, :, 1:], a_[:, :, 1:], a_[:, :, :BL - 1], ALU.mult).then_inc(sem("b4_decay"), 1)
                e.wait_ge(sem("b4_decay"), 1)
                link(e, e.tensor_tensor(t2[:, :, 2:], t1[:, :, 2:], a_[:, :, :BL - 2], ALU.mult))
                e.memset(e_[:, :, 3], -1.0)
                e.tensor_scalar(e_[:, :, 2], a_[:, :, 3], -1.0, None, ALU.mult)
                e.tensor_scalar(e_[:, :, 1], t1[:, :, 3], -1.0, None, ALU.mult)
                link(e, e.tensor_scalar(e_[:, :, 0], t2[:, :, 3], -1.0, None, ALU.mult))
                e.wait_ge(sem("b4_rlen"), 1)
                e.tensor_tensor(k_hat, k_hat, per_d(r_k), ALU.mult).then_inc(sem("b4_khat"), 1)
                e.wait_ge(sem("b4_khat"), 1)
                k4, q4, y4 = (x.rearrange("p (n i) d -> p n i d", i=BL) for x in (k_hat, q_raw, y))
                span = (None, a_, t1, t2)

                def dots(red, out_, s_):
                    view = red[:, 0:NB * (BL - s_) * HD].rearrange("p (n i d) -> p n i d", n=NB, d=HD)
                    return e.tensor_reduce(out_[:, :, s_:], view, AX.X, ALU.add)

                def spread(x, i0, i1, w):
                    return x[:, :, i0:i1].unsqueeze(3).to_broadcast([128, NB, i1 - i0, w])
                for s_ in range(1, BL):
                    view = prod_k[:, 0:NB * (BL - s_) * HD].rearrange("p (n i d) -> p n i d", n=NB, d=HD)
                    link(e, e.tensor_tensor(view, k4[:, :, s_:, :], k4[:, :, :BL - s_, :], ALU.mult))
                    link(e, dots(prod_k, kk_dot[:, s_ - 1], s_))
                    link(e, e.tensor_tensor(kk_dot[:, s_ - 1, :, s_:], kk_dot[:, s_ - 1, :, s_:], span[s_][:, :, s_:],
                                            ALU.mult))
                    link(e, e.tensor_tensor(kk_dot[:, s_ - 1, :, s_:], kk_dot[:, s_ - 1, :, s_:],
                                            blk(beta)[:, :, s_:], ALU.mult))
                link(e, e.tensor_tensor(coef, gamma, beta, ALU.mult))
                link(e, e.tensor_tensor(y[:, :, 0:HD], k_hat, per_d(coef), ALU.mult))
                tmp12 = prod_k[:, 0:NB * 12].rearrange("p (n w) -> p n w", w=12)
                for i in range(1, BL):
                    for s_ in range(1, i + 1):
                        c_ = kk_dot[:, s_ - 1, :, i].unsqueeze(2).to_broadcast([128, NB, 12])
                        link(e, e.tensor_tensor(tmp12, y4[:, :, i - s_, :], c_, ALU.mult))
                        link(e, e.tensor_tensor(y4[:, :, i, :], y4[:, :, i, :], tmp12, ALU.subtract))
                e.memset(hist[:, 0, :, :], 0.0).then_inc(sem("b4_solved"), 1)
                for n_, s_ in enumerate((0, 2, 1, 3)):
                    e.wait_ge(sem("b4_qk"), n_ + 1)
                    i = dots(prod_q[n_ % 2], qk_dot[:, s_], s_)
                    i.then_inc(sem("b4_qkred"), 1)
                e.wait_ge(sem("b4_qkred"), 4)
                for s_ in range(1, BL):
                    link(e, e.tensor_tensor(qk_dot[:, s_, :, s_:], qk_dot[:, s_, :, s_:], span[s_][:, :, s_:], ALU.mult))
                link(e, e.tensor_tensor(k_hat, k_hat, per_d(to_end), ALU.mult))
                e.wait_ge(sem("b4_solved"), 1)

                def outputs(ch):
                    e.wait_ge(sem("b4_qprod"), ch + 1)
                    o_ = o_tok[:, ch * CB * BL:(ch + 1) * CB * BL, :]
                    return e.tensor_reduce(o_, prod_o[:, ch % 2].rearrange("p n i j d -> p (n i) j d"), AX.X, ALU.add)
                for n_ in range(NB):
                    ch = n_ // CB
                    if n_ % CB == 0:
                        e.wait_ge(sem("b4_vset"), ch + 1)
                        if ch >= 2:
                            outputs(ch - 2)
                    if n_:
                        e.wait_ge(sem("b4_state"), n_)
                    slot = n_ % (2 * CB)
                    e.tensor_tensor(terms[:, slot, :, :, 0:HD],
                                    y4[:, n_, :, 0:HD].unsqueeze(2).to_broadcast([128, BL, 4, HD]),
                                    hist[:, n_, :, :].unsqueeze(1).to_broadcast([128, BL, 4, HD]),
                                    ALU.mult).then_inc(sem("b4_scan"), 1)
                    e.wait_ge(sem("b4_scan"), 3 * n_ + 1)
                    e.tensor_reduce(neg_delta[:, n_, :, :], terms[:, slot, :, :, :], AX.X,
                                    ALU.add).then_inc(sem("b4_scan"), 1)
                    e.wait_ge(sem("b4_scan"), 3 * n_ + 2)
                    e.tensor_tensor(rank1[:, n_ % 2, :, :, 0:BL],
                                    neg_delta[:, n_, :, :].rearrange("p l j -> p j l").unsqueeze(2).to_broadcast(
                                        [128, 4, HD, BL]),
                                    k4[:, n_, :, :].rearrange("p l d -> p d l").unsqueeze(1).to_broadcast(
                                        [128, 4, HD, BL]), ALU.mult).then_inc(sem("b4_scan"), 1)
                    e.wait_ge(sem("b4_scan"), 3 * n_ + 3)
                    e.wait_ge(sem("b4_carry"), n_ + 1)
                    e.tensor_reduce(hist[:, n_ + 1, :, :], rank1[:, n_ % 2, :, :, :], AX.X,
                                    ALU.add).then_inc(sem("b4_state"), 1)
                outputs(NCB - 2)
                link(e, outputs(NCB - 1))
                o4 = o_tok.rearrange("p (n i) j -> p n i j", i=BL)
                for s_ in range(BL):
                    link(e, e.tensor_tensor(o_tmp[:, :, s_:, :], neg_delta[:, :, :BL - s_, :],
                                            spread(qk_dot[:, s_], s_, BL, 4), ALU.mult))
                    link(e, e.tensor_tensor(o4[:, :, s_:, :], o4[:, :, s_:, :], o_tmp[:, :, s_:, :], ALU.subtract))
                e.tensor_tensor(o_tok, o_tok, per_d(r_q, 4), ALU.mult).then_inc(sem("b4_o"), 1)
                for b in range(B):
                    e.wait_ge(sem("b4_mix"), b + 1)
                    e.tensor_tensor(x_aux[:, b, :], ps[:, b, :], x_cur[:, b, :], ALU.add).then_inc(sem("b4_h"), 1)

            def b4_pool(e):
                k4, q4 = (x.rearrange("p (n i) d -> p n i d", i=BL) for x in (k_hat, q_raw))
                e.wait_ge(sem("b4_khat"), 1)
                for n_, s_ in enumerate((0, 2, 1, 3)):
                    if n_ >= 2:
                        e.wait_ge(sem("b4_qkred"), n_ - 1)
                    view = prod_q[n_ % 2][:, 0:NB * (BL - s_) * HD].rearrange("p (n i d) -> p n i d", n=NB, d=HD)
                    e.tensor_tensor(view, q4[:, :, s_:, :], k4[:, :, :BL - s_, :], ALU.mult).then_inc(sem("b4_qk"), 1)
                e.wait_ge(sem("b4_qk"), 4)
                e.tensor_tensor(q_raw, q_raw, per_d(gamma), ALU.mult).then_inc(sem("b4_qdecay"), 1)
                e.wait_ge(sem("b4_qdecay"), 1)

                def vset(ch):
                    if ch >= 2:
                        e.wait_ge(sem("b4_scan"), 3 * CB * (ch - 1))
                    for i in range(BL):
                        o = e.tensor_copy(terms[:, ch % 2 * CB:(ch % 2 + 1) * CB, i, :, HD],
                                          y[:, ch * CB * BL + i:(ch + 1) * CB * BL:BL, HD:12])
                    o.then_inc(sem("b4_vset"), 1)
                e.wait_ge(sem("b4_solved"), 1)
                vset(0)
                vset(1)
                for ch in range(NCB):
                    e.wait_ge(sem("b4_scan"), 3 * CB * ch + 3 * CB)
                    for i in range(BL):
                        o = e.tensor_tensor(prod_o[:, ch % 2, :, i, :, :],
                                            q4[:, ch * CB:(ch + 1) * CB, i, :].unsqueeze(2).to_broadcast([128, CB, 4, HD]),
                                            hist[:, ch * CB:(ch + 1) * CB, :, :], ALU.mult)
                    o.then_inc(sem("b4_qprod"), 1)
                    if ch + 2 < NCB:
                        vset(ch + 2)

            def b4_pe2(e):
                e.wait_ge(sem("b4_o"), 1)
                for b in range(B):
                    for j in range(4):
                        i = e.matmul(ps[:, b, :], wt["o_s"][:, (b * 4 + j) * 128:(b * 4 + j + 1) * 128],
                                     o_tok[:, :, j], start=(j == 0), stop=(j == 3))
                    i.then_inc(sem("b4_mix"), 1)
            pe_steps += [b4_pe, b4_pe2]
            act_steps.append(b4_act)
            dve_steps.append(b4_dve)
            pool_steps.append(b4_pool)

            c = Carve()
            hn = c(B * T).rearrange("p (b t) -> p b t", b=B)
            act4 = c(4 * T).rearrange("p (s t) -> p s t", s=4)
            n = make_norm([(x_aux[:, b, :], hn[:, b, :], T, b) for b in range(B)], counted("b4_h"), gain="norm2_w",
                          eps="eps6", mean=False)
            add_norm(n)

            def b4_total(e, b):
                link(e, e.tensor_tensor(x_aux[:, b, :], ps[:, 4 + b % 2, :], x_aux[:, b, :], ALU.add))
                return e.tensor_tensor(x_aux[:, b, :], x_aux[:, b, :], x_cur[:, b, :], ALU.add)
            gated("b4f", FC, FW, hn, [n.done(b) for b in range(B)],
                  lambda i: wt["wg"][:, i * FW:(i + 1) * FW], lambda i: wt["wu"][:, i * FW:(i + 1) * FW],
                  lambda i: wt["wd"][0:FW, i * 128:(i + 1) * 128], act4, extra={"total": b4_total})
            n = make_norm(batches(x_aux, x_cur), counted("b4f_sum"))
            add_norm(n)
            final = n

        if stages >= 5:
            c = Carve()
            qc = c(B * T).rearrange("p (b t) -> p b t", b=B)
            kc = c(B * S).rearrange("p (b s) -> p b s", b=B)
            kblk = c(B * H * S).rearrange("p (b h s) -> p b h s", b=B, h=H)
            vblk = c(B * 4 * 128).rearrange("p (b c n) -> p b c n", b=B, c=4)
            pc = c(4 * T).rearrange("p (a h s) -> p a h s", a=4, h=H)
            ptc = c(2 * 4 * T).rearrange("p (a c q) -> p a c q", a=2, c=4)
            oc = c(2 * T).rearrange("p (a t) -> p a t", a=2)
            st5 = c(3 * 4 * H).rearrange("p (k a h) -> p k a h", k=3, a=4)
            fin5 = final
            N5 = B * QB

            def b5_pe(e):
                e.wait_ge(sem("load_wE"), 16)
                e.wait_ge(*fin5.done(B - 1))
                for b in range(B):
                    e.matmul(ps[:, b, :], wt["c_Wq"], x_cur[:, b, :], start=True, stop=True).then_inc(sem("b5_proj"), 1)
                e.wait_ge(sem("load_ctx"), 16)
                e.matmul(ps[:, 4, 0:B * S], wt["c_Wk"], ctx_in[:, :], start=True, stop=True).then_inc(sem("b5_proj"), 1)
                for b in range(B):
                    for r in range(4):
                        i = e.matmul(ps[32 * r:32 * r + 32, 5, b * 128:b * 128 + 128], ctx_in[:, b * S:b * S + S],
                                     wt["c_Wv"], start=True, stop=True)
                i.then_inc(sem("b5_proj"), 1)
                e.wait_ge(sem("b5_blocks"), 1)

                def pv(b):
                    e.wait_ge(sem("b5_evac"), QB * (b + 1))
                    if b >= 2:
                        e.wait_ge(sem("b5_heads"), b - 1)
                    for k in range(4):
                        i = e.matmul(ps[:, 4 + b % 2, :], vblk[:, b, k, :], ptc[:, b % 2, k, :], start=(k == 0),
                                     stop=(k == 3))
                    i.then_inc(sem("b5_pv"), 1)

                def outp(b):
                    e.wait_ge(sem("b5_heads"), b + 1)
                    if b >= 2:
                        e.wait_ge(sem("b5_sum"), b - 1)
                    e.matmul(ps[:, 6 + b % 2, :], wt["c_Wo"], oc[:, b % 2, :], start=True,
                             stop=True).then_inc(sem("b5_out"), 1)
                for n_ in range(N5 + 6):
                    b, q = n_ // QB, n_ % QB
                    if n_ < N5:
                        if n_ >= 2:
                            e.wait_ge(sem("b5_shift"), n_ - 1)
                        e.matmul(ps[:, n_ % 2, :], qc[:, b, q * 128:q * 128 + 128], kblk[:, b, :, :], start=True,
                                 stop=True).then_inc(sem("b5_score"), 1)
                    if 2 <= n_ < N5 + 2:
                        m = n_ - 2
                        e.wait_ge(sem("b5_prob"), m + 1)
                        if m >= 2:
                            e.wait_ge(sem("b5_evac"), m - 1)
                        for k in range(4):
                            i = e.transpose(ps[:, 2 + m % 2, k * 128:k * 128 + 128], pc[:, m % 4, 4 * k:4 * k + 4, :],
                                            ident)
                        i.then_inc(sem("b5_turn"), 1)
                    if n_ >= 7 and (n_ - 7) % 4 == 0:
                        pv((n_ - 7) // 4)
                    if n_ >= 9 and (n_ - 9) % 4 == 0:
                        outp((n_ - 9) // 4)

            def b5_act(e):
                for n_ in range(N5 + 2):
                    if n_ < N5:
                        e.wait_ge(sem("b5_shift"), n_ + 1)
                        e.activation(pc[:, n_ % 4, :, :], pc[:, n_ % 4, :, :], ACT.Exp).then_inc(sem("b5_exp"), 1)
                    if n_ >= 2:
                        m = n_ - 2
                        b, q = m // QB, m % QB
                        e.wait_ge(sem("b5_turn"), m + 1)
                        if b >= 2 and q == 0:
                            e.wait_ge(sem("b5_pv"), b - 1)
                        e.copy(ptc[:, b % 2, :, q * 128:q * 128 + 128],
                               ps[:, 2 + m % 2, :].rearrange("p (k q) -> p k q", k=4)).then_inc(sem("b5_evac"), 1)

            def b5_dve(e):
                for b in range(B):
                    e.wait_ge(sem("b5_proj"), b + 1)
                    e.tensor_scalar(qc[:, b, :], ps[:, b, :], v("c_bq"), HD ** -0.5, ALU.add, ALU.mult)
                e.wait_ge(sem("b5_proj"), 5)
                link(e, e.tensor_scalar(kc, ps[:, 4, 0:B * S].rearrange("p (b s) -> p b s", b=B), v("c_bk"), None,
                                        ALU.add))
                e.wait_ge(sem("b5_proj"), 6)
                for b in range(B):
                    e.tensor_tensor(kblk[:, b, :, :], kc[:, b, :].unsqueeze(1).to_broadcast([128, H, S]),
                                    v("head_mask", 0, H).unsqueeze(2).to_broadcast([128, H, S]), ALU.mult)
                    i = e.tensor_tensor(vblk[:, b, :, :],
                                        ps[:, 5, b * 128:b * 128 + 128].unsqueeze(1).to_broadcast([128, 4, 128]),
                                        wt["v_mask"].rearrange("p (c n) -> p c n", c=4), ALU.mult)
                i.then_inc(sem("b5_blocks"), 1)

                def heads(b):
                    e.wait_ge(sem("b5_pv"), b + 1)
                    if b >= 2:
                        e.wait_ge(sem("b5_out"), b - 1)
                    e.tensor_scalar(oc[:, b % 2, :], ps[:, 4 + b % 2, :], v("c_bv"), None,
                                    ALU.add).then_inc(sem("b5_heads"), 1)

                def total(b):
                    e.wait_ge(sem("b5_out"), b + 1)
                    e.scalar_tensor_tensor(out=x_aux[:, b, :], in0=ps[:, 6 + b % 2, :], scalar=v("c_bo"),
                                           in1=x_cur[:, b, :], op0=ALU.add, op1=ALU.add).then_inc(sem("b5_sum"), 1)
                hs = lambda x: x.unsqueeze(2).to_broadcast([128, H, S])
                for n_ in range(N5 + 7):
                    if n_ < N5:
                        a = n_ % 4
                        score = ps[:, n_ % 2, :].rearrange("p (h s) -> p h s", h=H)
                        e.wait_ge(sem("b5_score"), n_ + 1)
                        link(e, e.tensor_reduce(st5[:, 0, a, :], score, AX.X, ALU.max))
                        if n_ >= 4:
                            e.wait_ge(sem("b5_turn"), n_ - 3)
                        e.tensor_tensor(pc[:, a, :, :], score, hs(st5[:, 0, a, :]),
                                        ALU.subtract).then_inc(sem("b5_shift"), 1)
                    if 1 <= n_ <= N5:
                        m, a = n_ - 1, (n_ - 1) % 4
                        e.wait_ge(sem("b5_exp"), m + 1)
                        link(e, e.tensor_reduce(st5[:, 1, a, :], pc[:, a, :, :], AX.X, ALU.add))
                        link(e, e.reciprocal(st5[:, 2, a, :], st5[:, 1, a, :]))
                        e.tensor_tensor(pc[:, a, :, :], pc[:, a, :, :], hs(st5[:, 2, a, :]),
                                        ALU.mult).then_inc(sem("b5_prob"), 1)
                    if n_ >= 8 and (n_ - 8) % 4 == 0:
                        heads((n_ - 8) // 4)
                    if n_ >= 10 and (n_ - 10) % 4 == 0:
                        total((n_ - 10) // 4)
            pe_steps.append(b5_pe)
            act_steps.append(b5_act)
            dve_steps.append(b5_dve)
            n = make_norm(batches(x_aux, x_cur), counted("b5_sum"))
            add_norm(n)
            final = n

        if stages >= 6:
            n6 = make_norm(batches(x_cur, x_aux), [final.done(b) for b in range(B)], gain="m_ln1_w", mean=False)
            add_norm(n6)
            at6 = Attn(2, causal=True)
            at6.idx = 1
            narrow(at6, x_aux, [n6.done(b) for b in range(B)], at6.x2, "b6", "wF", "m_q", "m_k", "m_v", "m_wo",
                   rope=("m_qr", "m_kr"))
            x2 = at6.x2
            n7 = make_norm(batches(x2, x_aux), counted("b6_res"), gain="m_ln2_w", mean=False)
            add_norm(n7)
            c = Carve()
            wide_w = c(2 * E1 * T).rearrange("p (a e t) -> p a e t", a=2, e=E1)
            act6 = c(4 * T).rearrange("p (s t) -> p s t", s=4)
            w_pad = c(QB * 128).rearrange("p (q n) -> p q n", q=QB)
            w_T = c(T)
            r8 = [c(QB * E1).rearrange("p (q e) -> p q e", q=QB) for _ in range(6)]
            r1 = [c(QB) for _ in range(8)]
            assert c.at <= 16384 + 2048 + 1024 + 1024 + 2048
            sel = wt["sel"].rearrange("p (e n) -> p e n", e=E1)
            rank = v("tie_rank", 0, QB * E1).rearrange("p (q e) -> p q e", q=QB)

            def r_logit(e, b):
                if b:
                    e.wait_ge(sem("r_wide"), 8 * b)
                for q in range(QB):
                    i = e.matmul(ps[:, 6, q * E1:q * E1 + E1], x_aux[:, b, q * 128:q * 128 + 128], wt["m_gate"],
                                 start=True, stop=True)
                i.then_inc(sem("r_logit"), 1)

            def r_turn(e, b):
                e.wait_ge(sem("r_weights"), b + 1)
                for q in range(QB):
                    i = e.transpose(ps[:, 7, q * 128:q * 128 + 128], w_pad[:, q, :], ident)
                i.then_inc(sem("r_turn"), 1)

            def r_spread(e, b, ex):
                n_ = b * E1 + ex
                e.wait_ge(sem("r_turned"), b + 1)
                if ex >= 2:
                    e.wait_ge(sem("r_wide"), n_ - 1)
                e.matmul(ps[:, 6 + ex % 2, :], sel[:, ex, :], w_T, start=True, stop=True).then_inc(sem("r_spread"), 1)

            def r_exp(e, b):
                e.wait_ge(sem("r_shift"), b + 1)
                e.activation(r8[0], r8[0], ACT.Exp).then_inc(sem("r_exp"), 1)

            def r_wide(e, b, ex):
                n_ = b * E1 + ex
                e.wait_ge(sem("r_spread"), n_ + 1)
                if b >= 2 and ex == 0:
                    e.wait_ge(sem("b6f_gated"), (b - 1) * E1 * C1)
                e.copy(wide_w[:, b % 2, ex, :], ps[:, 6 + ex % 2, :]).then_inc(sem("r_wide"), 1)

            def top2_a(e, b):
                pr = r8[0]
                lg = ps[:, 6, 0:QB * E1].rearrange("p (q e) -> p q e", q=QB)
                bc = lambda x: x.unsqueeze(2).to_broadcast([128, QB, E1])
                e.wait_ge(sem("r_logit"), b + 1)
                link(e, e.tensor_reduce(r1[0], lg, AX.X, ALU.max))
                e.tensor_tensor(pr, lg, bc(r1[0]), ALU.subtract).then_inc(sem("r_shift"), 1)

            def top2_b(e, b):
                pr, eq, sel1, p2, sel2, both = r8
                bc = lambda x: x.unsqueeze(2).to_broadcast([128, QB, E1])
                e.wait_ge(sem("r_exp"), b + 1)
                link(e, e.tensor_reduce(r1[1], pr, AX.X, ALU.add))
                link(e, e.reciprocal(r1[2], r1[1]))
                link(e, e.tensor_tensor(pr, pr, bc(r1[2]), ALU.mult))
                link(e, e.tensor_reduce(r1[3], pr, AX.X, ALU.max))
                link(e, e.tensor_tensor(eq, pr, bc(r1[3]), ALU.is_equal))
                link(e, e.tensor_tensor(eq, eq, rank, ALU.mult))
                link(e, e.tensor_reduce(r1[4], eq, AX.X, ALU.max))
                link(e, e.tensor_tensor(sel1, eq, bc(r1[4]), ALU.is_equal))
                link(e, e.scalar_tensor_tensor(out=p2, in0=sel1, scalar=-2.0, in1=pr, op0=ALU.mult, op1=ALU.add))
                link(e, e.tensor_reduce(r1[5], p2, AX.X, ALU.max))
                link(e, e.tensor_tensor(eq, p2, bc(r1[5]), ALU.is_equal))
                link(e, e.tensor_tensor(eq, eq, rank, ALU.mult))
                link(e, e.tensor_reduce(r1[6], eq, AX.X, ALU.max))
                link(e, e.tensor_tensor(sel2, eq, bc(r1[6]), ALU.is_equal))
                link(e, e.tensor_tensor(r1[7], r1[3], r1[5], ALU.add))
                link(e, e.reciprocal(r1[7], r1[7]))
                link(e, e.tensor_tensor(both, sel1, sel2, ALU.add))
                link(e, e.tensor_tensor(both, both, pr, ALU.mult))
                if b:
                    e.wait_ge(sem("r_turn"), b)
                e.tensor_tensor(w_pad[:, :, 0:E1], both, bc(r1[7]), ALU.mult).then_inc(sem("r_weights"), 1)

            def r_turned(e, b):
                e.wait_ge(sem("r_turn"), b + 1)
                if b:
                    e.wait_ge(sem("r_spread"), E1 * b)
                e.tensor_copy(w_T, ps[:, 7, :]).then_inc(sem("r_turned"), 1)

            def pe_extra(e, b, i):
                if b + 1 < B:
                    if i == 1:
                        r_logit(e, b + 1)
                    if i == 5:
                        r_turn(e, b + 1)
                    if 8 <= i < 16:
                        r_spread(e, b + 1, i - 8)

            def act_extra(e, b, i):
                if b + 1 < B:
                    if i == 1:
                        r_exp(e, b + 1)
                    if 8 <= i < 16:
                        r_wide(e, b + 1, i - 8)

            def dve_extra(e, b, i):
                if b + 1 < B:
                    if i == 1:
                        top2_a(e, b + 1)
                    if i == 2:
                        top2_b(e, b + 1)
                    if i == 6:
                        r_turned(e, b + 1)

            def b6_total(e, b):
                link(e, e.tensor_tensor(x_aux[:, b, :], ps[:, 4 + b % 2, :], x2[:, b, :], ALU.add))
                return e.tensor_tensor(x_aux[:, b, :], x_aux[:, b, :], x_cur[:, b, :], ALU.add)

            def first_pe(e):
                r_logit(e, 0)
                r_turn(e, 0)
                for ex in range(E1):
                    r_spread(e, 0, ex)

            def first_act(e):
                r_exp(e, 0)
                for ex in range(E1):
                    r_wide(e, 0, ex)

            def first_dve(e):
                e.memset(w_pad, 0.0)
                top2_a(e, 0)
                top2_b(e, 0)
                r_turned(e, 0)
            w13, w2 = wt["w13"], wt["w2"]

            def w13_of(i, half):
                ex, k = i // C1, i % C1
                at_ = ex * 512 + half * 256 + k * 128
                return w13[:, at_:at_ + 128]
            gated("b6f", E1 * C1, 128, x_aux, [n7.done(b) for b in range(B)], lambda i: w13_of(i, 0),
                  lambda i: w13_of(i, 1), lambda i: w2[:, i * 128:(i + 1) * 128], act6, load="wM1",
                  weight=lambda b, i: wide_w[:, b % 2, i // C1, :], weight_ready=lambda b: (sem("r_wide"), E1 * (b + 1)),
                  extra={"pe": pe_extra, "act": act_extra, "dve": dve_extra, "total": b6_total,
                         "pe_first": [first_pe], "act_first": [first_act], "dve_first": [first_dve]})
            n = make_norm(batches(x_aux, x_cur), counted("b6f_sum"))
            add_norm(n)
            final = n

        def store(e):
            for b in range(B):
                e.wait_ge(*final.done(b))
                e.dma_start(out[:, b, :], x_cur[:, b, :]).then_inc(sem("stored"), 16)
            e.wait_ge(sem("stored"), 16 * B)
        sp_steps.append(store)

        block = ctx.enter_context(nc.Block())

        @block.sync
        def _(eng):
            for step in sp_steps:
                step(eng)

        @block.tensor
        def _(eng):
            for step in pe_steps:
                step(eng)

        @block.scalar
        def _(eng):
            for step in act_steps:
                step(eng)

        @block.vector
        def _(eng):
            for step in dve_steps:
                step(eng)

        @block.gpsimd
        def _(eng):
            for step in pool_steps:
                step(eng)


def feature_major(a):
    return np.ascontiguousarray(np.transpose(a, (2, 0, 1)))


def spread_rows(w):
    n = w.shape[1]
    out = np.zeros((4, 32, 4, n), w.dtype)
    out[:, :8] = np.transpose(w.reshape(4, 4, 8, n), (1, 2, 0, 3))
    return out.reshape(128, 4 * n)


def spread_cols(w):
    out = np.zeros((128, 16, 32), w.dtype)
    out[:, :, :8] = w.reshape(128, 16, 8)
    return out.reshape(128, 512)


def layouts(i):
    f = np.float32
    one = lambda a: np.asarray(a).reshape(-1, 1)
    vec = {
        "gate_w": i["L0_attn_gate_w"].reshape(D, 7), "cand_w": i["L0_attn_cand_w"].reshape(D, 7),
        "gate_b": one(i["L0_attn_gate_b"]), "cand_b": one(i["L0_attn_cand_b"]),
        "log_decay": one(i["L0_attn_log_decay"]), "out_b": one(i["L0_attn_out_b"]),
        "norm_w": one(i["L0_attn_norm_w"]),
        "x_ln1_g": one(i["L0_xattn_ln1_g"]), "x_ln1_b": one(i["L0_xattn_ln1_b"]),
        "x_ln2_g": one(i["L0_xattn_ln2_g"]), "x_ln2_b": one(i["L0_xattn_ln2_b"]),
        "f_bq": one(i["L0_ffn_bq"]), "f_bk": one(i["L0_ffn_bk"]), "f_bv": spread_rows(one(i["L0_ffn_bv"])),
        "f_bo": one(i["L0_ffn_bo"]), "router_b": np.repeat(one(i["L0_ffn_router_b"]), 128, 0),
        "f_b1": np.transpose(i["L0_ffn_b1"].reshape(16, 128)), "f_b2": np.transpose(i["L0_ffn_b2"]),
        "f_ln1_g": one(i["L0_ffn_ln1_g"]), "f_ln1_b": one(i["L0_ffn_ln1_b"]),
        "f_ln2_g": one(i["L0_ffn_ln2_g"]), "f_ln2_b": one(i["L0_ffn_ln2_b"]),
        "norm1_w": one(i["L1_attn_norm1_w"]), "norm2_w": one(i["L1_attn_norm2_w"]),
        "conv_w": i["L1_attn_conv_w"], "conv_b": one(i["L1_attn_conv_b"]),
        "c_bq": one(i["L1_xattn_bq"]), "c_bk": one(i["L1_xattn_bk"]), "c_bv": one(i["L1_xattn_bv"]),
        "c_bo": one(i["L1_xattn_bo"]), "m_ln1_w": one(i["L1_ffn_ln1_w"]), "m_ln2_w": one(i["L1_ffn_ln2_w"]),
        "eps_attn": np.full((128, 1), 1.1920929e-07, f), "eps5": np.full((128, 1), 1e-5, f),
        "eps6": np.full((128, 1), 1e-6, f), "four": np.full((128, 1), 4.0, f),
        "head_mask": np.repeat(np.eye(H, dtype=f), HD, 0),
        "tie_rank": np.tile(np.arange(E1, 0, -1).astype(f), (128, 4)),
    }
    for n, (_, w) in VEC.items():
        assert vec[n].shape == (128, w), (n, vec[n].shape)
    tr = np.transpose
    qkv = i["L1_ffn_wqkv"]
    group = np.repeat(np.arange(4), 4)
    mk = qkv[128:160].reshape(4, 8, 128)[group].reshape(128, 128)
    mv = qkv[160:192].reshape(4, 8, 128)[group].reshape(128, 128)
    swap = lambda w: w.reshape(16, 2, 4, 128)[:, ::-1].reshape(128, 128)
    inv = (1.0 / f(10000.0) ** (np.arange(0, HD, 2, dtype=f) / f(HD))).astype(f)
    ang = np.arange(T, dtype=f)[:, None] * inv[None, :]
    cos, sin = np.cos(ang).astype(f), np.sin(ang).astype(f)
    cosT = np.tile(np.concatenate([cos, cos], 1).T, (16, 1))
    sinT = np.tile(np.concatenate([-sin, sin], 1).T, (16, 1))
    ws = i["L1_attn_wq"], i["L1_attn_wk"]
    dhv = lambda w: np.repeat(tr(w.reshape(128, 16, 8), (0, 2, 1)), 2, 2).reshape(128, 256)
    o_s = np.zeros((4, 16, 2, 4, 4, 128), f)
    for b in range(4):
        o_s[b, :, :, b] = i["L1_attn_wo"].reshape(16, 2, 4, 128)
    wd = np.zeros((128, 3, 128), f)
    wd[:FW] = tr(i["L1_attn_wd"].reshape(3, FW, 128), (1, 0, 2))
    vm = (np.arange(128)[:, None, None] // 32 + 4 * np.arange(4)[None, :, None]
          == np.arange(128)[None, None, :] // 8).astype(f).reshape(128, 512)
    causal = np.where(np.arange(128)[None, :] > np.arange(128)[:, None], f(NEG), f(0))
    sel = np.zeros((128, 8, 128), f)
    for ex in range(8):
        sel[ex, ex] = 1.0
    mats = {
        "out_w": tr(i["L0_attn_out_w"]), "ident": np.eye(128, dtype=f), "ones": np.full((128, 128), 1.0 / D, f),
        "Wq": i["L0_xattn_Wq"], "Wkv": i["L0_xattn_Wkv"],
        "Wo": tr(i["L0_xattn_Wo"].reshape(8, 128, 128), (1, 0, 2)).reshape(128, 1024),
        "f_Wq": i["L0_ffn_Wq"], "f_Wk": i["L0_ffn_Wk"], "f_Wv": spread_cols(i["L0_ffn_Wv"]),
        "f_Wo": spread_rows(i["L0_ffn_Wo"]), "router": np.repeat(i["L0_ffn_router_w"], 128, 1),
        "W1": tr(i["L0_ffn_W1"], (1, 0, 2)).reshape(128, 2048),
        "W2": tr(i["L0_ffn_W2"].reshape(16, 128, 128), (1, 0, 2)).reshape(128, 2048),
        "q_s": dhv(ws[0]), "k_s": dhv(ws[1]),
        "v_s": tr(i["L1_attn_wv"].reshape(128, 32, 4), (0, 2, 1)).reshape(128, 128),
        "b_s": np.repeat(i["L1_attn_wb"], 2, 1), "a_s": np.repeat(i["L1_attn_wa"], 2, 1),
        "o_s": o_s.reshape(128, 2048), "wg": i["L1_attn_wg"], "wu": i["L1_attn_wu"], "wd": wd.reshape(128, 384),
        "c_Wq": tr(i["L1_xattn_Wq"]), "c_Wk": tr(i["L1_xattn_Wk"]), "c_Wv": tr(i["L1_xattn_Wv"]),
        "c_Wo": tr(i["L1_xattn_Wo"]), "v_mask": vm,
        "m_q": tr(qkv[:128]), "m_qr": tr(swap(qkv[:128])), "m_k": tr(mk), "m_kr": tr(swap(mk)),
        "m_v": spread_cols(tr(mv)), "m_wo": spread_rows(tr(i["L1_ffn_wo"])), "m_gate": tr(i["L1_ffn_gate_w"]),
        "cos": cosT, "sin": sinT, "causal": causal, "sel": sel.reshape(128, 1024),
        "w13": tr(i["L1_ffn_w13"], (2, 0, 1)).reshape(128, 4096),
        "w2": tr(i["L1_ffn_w2"].reshape(8, 128, 2, 128), (3, 0, 2, 1)).reshape(128, 2048),
    }
    arrays = {"xT": feature_major(i["x"]), "ctxT": feature_major(i["ctx_1024"]).reshape(128, B * S),
              "vecs": np.concatenate([vec[n] for n in VEC], 1)}
    for g, cols in GROUPS.items():
        for n, w in cols:
            assert mats[n].shape == (128, w), (n, mats[n].shape)
        arrays[g] = np.concatenate([mats[n] for n, _ in cols], 1)
    return {k: np.ascontiguousarray(a) for k, a in arrays.items()}


def kernel(**inputs):
    import concourse.bacc as _bacc
    from concourse.bass_utils import run_bass_kernel_spmd as _run

    arrays = layouts(inputs)
    nc = _bacc.Bacc("TRN2", target_bir_lowering=False, num_devices=1)
    aps = {k: nc.dram_tensor(k + "_dram", a.shape, F32, kind="ExternalInput").ap() for k, a in arrays.items()}
    out = nc.dram_tensor("out_dram", (128, B, T), F32, kind="ExternalOutput").ap()
    program(nc, aps["xT"], aps["ctxT"], aps["vecs"], {g: aps[g] for g in GROUPS}, out)
    r = _run(nc, [{k + "_dram": a for k, a in arrays.items()}], core_ids=[0])
    return np.ascontiguousarray(np.transpose(r.results[0]["out_dram"], (1, 2, 0)))
```

```python
from contextlib import ExitStack

import numpy as np
import concourse.bass as bass
from concourse import mybir

ALU = mybir.AluOpType
ACT = mybir.ActivationFunctionType
AX = mybir.AxisListType
F32 = mybir.dt.float32
I32 = mybir.dt.int32
BF16 = mybir.dt.bfloat16

B, T, D = 4, 512, 128
H, HD = 16, 8
XH, XD = 16, 64
S = 32
KEYS = T + S
QB = T // 128
UNITS = H * QB
E0, C0 = 4, 4
E1, C1 = 8, 2
FI, FC = 345, 3
FW = FI // FC
TAPS, CTAPS = 7, 4
PV_AT = 6
BL = 4
NB = T // BL
CB = 16
NCB = NB // CB
NEG = -1.0e30
B7 = 25

VEC = {}
for _n, _w in (("gate_w", 7), ("cand_w", 7), ("gate_b", 1), ("cand_b", 1), ("log_decay", 1), ("out_b", 1),
               ("norm_w", 1), ("x_ln1_g", 1), ("x_ln1_b", 1), ("x_ln2_g", 1), ("x_ln2_b", 1), ("f_bq", 1),
               ("f_bk", 1), ("f_bo", 1), ("router_b", 1), ("f_b1", 16), ("f_b2", 4), ("f_ln1_g", 1),
               ("f_ln1_b", 1), ("f_ln2_g", 1), ("f_ln2_b", 1), ("norm1_w", 1), ("norm2_w", 1), ("conv_w", 4),
               ("conv_b", 1), ("c_bq", 1), ("c_bk", 1), ("c_bv", 1), ("c_bo", 1), ("m_ln1_w", 1), ("m_ln2_w", 1),
               ("eps_attn", 1), ("eps5", 1), ("eps6", 1), ("four", 1), ("head_mask", 16), ("sum_pick", 4), ("tie_rank", 32)):
    VEC[_n] = (sum(w for _, w in VEC.values()), _w)
NVEC = sum(w for _, w in VEC.values())

GROUPS = {
    "wA": (("out_w", 128), ("ident", 128), ("ones", 128)),
    "wB": (("Wq", 1024), ("Wkv", 2048), ("Wo", 1024)),
    "wC": (("f_Wq", 128), ("f_Wk", 128), ("f_Wv", 128), ("f_bv", 128), ("f_Wo", 512), ("router", 128)),
    "wM0": (("W1", 2048), ("W2", 2048)),
    "wD": (("q_s", 256), ("k_s", 256), ("v_s", 128), ("b_s", 32), ("a_s", 32), ("o_s", 2048), ("wg", FI),
           ("wu", FI), ("wd", 384)),
    "wE": (("c_Wq", 128), ("c_Wk", 128), ("c_Wv", 128), ("c_Wo", 128), ("v_mask", 512)),
    "wF": (("m_q", 128), ("m_qr", 128), ("m_k", 128), ("m_kr", 128), ("m_v", 128), ("m_wo", 512), ("m_gate", 8),
           ("cos", 512), ("sin", 512), ("causal", 128), ("sel", 1024)),
    "wM1": (("w13", 4096), ("w2", 2048)),
}


def program(nc, xT, ctxT, vecs, groups, out, stages=6):
    ctx = ExitStack()
    with ctx:
        def sb(name, cols, dt=F32):
            return ctx.enter_context(nc.sbuf_tensor(name, [128, cols], dt))

        sem_of = {}

        def sem(name):
            if name not in sem_of:
                sem_of[name] = ctx.enter_context(nc.semaphore(name))
            return sem_of[name]

        vec = sb("vec", NVEC)
        x_cur = sb("x_cur", B * T).rearrange("p (b t) -> p b t", b=B)
        x_aux = sb("x_aux", B * T).rearrange("p (b t) -> p b t", b=B)
        cent = sb("cent", B * T).rearrange("p (b t) -> p b t", b=B)
        dev = sb("dev", B * T).rearrange("p (b t) -> p b t", b=B)
        ctx_in = sb("ctx_in", B * S)
        ctx_ln = sb("ctx_ln", B * S)
        stat = sb("stat", 64)
        width = {g: sum(w for _, w in cols) for g, cols in GROUPS.items()}
        reg1 = sb("reg1", max(width["wB"], width["wD"]))
        reg2 = sb("reg2", max(width["wM0"], width["wM1"]))
        place = {"wB": reg1, "wD": reg1, "wM0": reg2, "wM1": reg2}
        for g in ("wA", "wC", "wE", "wF"):
            place[g] = sb(g + "_sb", width[g])
        wt = {}
        for g, cols in GROUPS.items():
            at = 0
            for n, w in cols:
                wt[n] = place[g][:, at:at + w]
                at += w
        wt_bf = sb("wt_bf", 256, BF16)
        arena_cols = 28160
        arena = sb("arena", arena_cols)
        ps = ctx.enter_context(nc.psum_tensor("ps", [128, 8, 512], F32))

        def v(name, i=0, n=1):
            c = VEC[name][0] + i
            return vec[:, c:c + n]

        class Carve:
            def __init__(self):
                self.at = 0

            def __call__(self, cols):
                a = arena[:, self.at:self.at + cols]
                self.at += cols
                assert self.at <= arena_cols, self.at
                return a

        ident, ones = wt["ident"], wt["ones"]

        class Norm:
            count = 0

            def __init__(self, chunks, ready, gain=None, bias=None, eps="eps5", mean=True,
                         other_table=False):
                self.other_table = other_table
                self.chunks, self.ready, self.gain, self.bias, self.eps, self.mean = chunks, ready, gain, bias, eps, mean
                self.first = Norm.count
                Norm.count += len(chunks)

            def tmp(self, buf, n):
                _, _, w, slot = self.chunks[n]
                return buf[:, slot, 0:w]

            def pe(self, e):
                if self.mean:
                    for n, (src, _, w, slot) in enumerate(self.chunks):
                        e.wait_ge(*self.ready[n])
                        if self.first >= 1:
                            e.wait_ge(sem("norm_done"), self.first)
                        e.matmul(ps[:, slot, 0:w], ones, src, start=True, stop=True).then_inc(sem("norm_mean"), 1)
                for n, (src, _, w, slot) in enumerate(self.chunks):
                    if not self.mean and self.first >= 1:
                        e.wait_ge(sem("norm_done"), self.first)
                    e.wait_ge(sem("norm_sq"), self.first + n + 1)
                    i = e.matmul(ps[:, 4 + slot, 0:w], ones, self.tmp(dev, n), start=True, stop=True)
                    i.then_inc(sem("norm_var"), 1)

            def act(self, e):
                if self.other_table:
                    e.preload_act_table_set("natural_log_exp_and_others")
                for n, (src, _, w, slot) in enumerate(self.chunks):
                    if self.mean:
                        e.wait_ge(sem("norm_cent"), self.first_mean + n + 1)
                    else:
                        e.wait_ge(*self.ready[n])
                    if self.first:
                        e.wait_ge(sem("norm_done"), self.first)
                    e.activation(self.tmp(dev, n), self.tmp(cent, n) if self.mean else src,
                                 ACT.Square).then_inc(sem("norm_sq"), 1)
                for n, (src, _, w, slot) in enumerate(self.chunks):
                    e.wait_ge(sem("norm_var"), self.first + n + 1)
                    e.activation(self.tmp(dev, n), ps[:, 4 + slot, 0:w], ACT.Ln,
                                 bias=v(self.eps)).then_inc(sem("norm_ln"), 1)
                for n, (src, _, w, slot) in enumerate(self.chunks):
                    e.wait_ge(sem("norm_ln"), self.first + n + 1)
                    e.activation(self.tmp(dev, n), self.tmp(dev, n), ACT.Exp, scale=-0.5).then_inc(sem("norm_dev"), 1)

            def dve(self, e):
                if self.mean:
                    for n, (src, _, w, slot) in enumerate(self.chunks):
                        e.wait_ge(sem("norm_mean"), self.first_mean + n + 1)
                        e.tensor_tensor(self.tmp(cent, n), src, ps[:, slot, 0:w],
                                        ALU.subtract).then_inc(sem("norm_cent"), 1)
                for n, (src, dst, w, slot) in enumerate(self.chunks):
                    c = self.tmp(cent, n) if self.mean else src
                    e.wait_ge(sem("norm_dev"), self.first + n + 1)
                    if self.mean:
                        e.wait_ge(sem("norm_cent"), self.first_mean + n + 1)
                    if self.gain is None:
                        e.tensor_tensor(dst, c, self.tmp(dev, n), ALU.mult).then_inc(sem("norm_done"), 1)
                    elif self.bias is None:
                        e.scalar_tensor_tensor(out=dst, in0=c, scalar=v(self.gain), in1=self.tmp(dev, n),
                                               op0=ALU.mult, op1=ALU.mult).then_inc(sem("norm_done"), 1)
                    else:
                        e.scalar_tensor_tensor(out=self.tmp(cent, n), in0=c, scalar=v(self.gain),
                                               in1=self.tmp(dev, n), op0=ALU.mult,
                                               op1=ALU.mult).then_inc(sem("norm_scaled"), 1)
                        e.wait_ge(sem("norm_scaled"), self.scaled + n + 1)
                        e.tensor_scalar(dst, self.tmp(cent, n), v(self.bias), None,
                                        ALU.add).then_inc(sem("norm_done"), 1)

            def done(self, n):
                return sem("norm_done"), self.first + n + 1

        mean_count, scaled_count = [0], [0]

        def make_norm(*a, **k):
            n = Norm(*a, **k)
            n.first_mean, n.scaled = mean_count[0], scaled_count[0]
            if n.mean:
                mean_count[0] += len(n.chunks)
            if n.bias is not None:
                scaled_count[0] += len(n.chunks)
            return n

        def batches(src, dst):
            return [(src[:, b, :], dst[:, b, :], T, b) for b in range(B)]

        def counted(name, base=0, step=1):
            return [(sem(name), base + step * (b + 1)) for b in range(B)]

        pe_steps, act_steps, dve_steps, pool_steps, sp_steps = [], [], [], [], []
        final = None

        def add_norm(n):
            pe_steps.append(n.pe)
            act_steps.append(n.act)
            dve_steps.append(n.dve)

        link_count = [0]

        def link(e, ins):
            link_count[0] += 1
            ins.then_inc(sem("dve_link"), 1)
            e.wait_ge(sem("dve_link"), link_count[0])

        def load_first(e):
            for g in ("wA",):
                e.dma_start(place[g][:, 0:width[g]], groups[g]).then_inc(sem("load_" + g), 16)
            for g in ("wB", "wC", "wM0", "wE", "wF"):
                e.dma_start(place[g][:, 0:width[g]], groups[g]).then_inc(sem("load_" + g), 16)
        P = TAPS // 2
        cv = Carve()
        x_pad = cv(B * (T + 2 * P)).rearrange("p (b t) -> p b t", b=B)
        gate = cv(B * T).rearrange("p (b t) -> p b t", b=B)
        cand = cv(B * T).rearrange("p (b t) -> p b t", b=B)
        hid = cv(B * T).rearrange("p (b t) -> p b t", b=B)
        y1 = cv(B * T).rearrange("p (b t) -> p b t", b=B)
        decay = stat[:, 63:64]

        def load_x(e):
            e.dma_start(vec[:, :], vecs).then_inc(sem("load_vec"), 16)
            e.dma_start(x_cur[:, :, :], xT).then_inc(sem("load_x"), 16)
            e.dma_start(x_pad[:, :, P:P + T], xT).then_inc(sem("load_x"), 16)
            e.dma_start(ctx_in[:, :], ctxT).then_inc(sem("load_ctx"), 16)
        sp_steps += [load_x, load_first]

        def b1_dve(e):
            e.memset(x_pad[:, :, 0:P], 0.0)
            link(e, e.memset(x_pad[:, :, P + T:], 0.0))
            e.wait_ge(sem("load_vec"), 16)
            e.wait_ge(sem("load_x"), 32)
            for k in range(TAPS):
                for n, (acc, w) in enumerate(((gate, "gate_w"), (cand, "cand_w"))):
                    src = x_pad[:, :, k:k + T]
                    if k == 0:
                        e.tensor_scalar(acc, src, v(w, k), None, ALU.mult).then_inc(sem(f"tap{n}"), 1)
                    else:
                        e.wait_ge(sem(f"tap{n}"), k)
                        e.scalar_tensor_tensor(out=acc, in0=src, scalar=v(w, k), in1=acc, op0=ALU.mult,
                                               op1=ALU.add).then_inc(sem(f"tap{n}"), 1)
            for b in range(B):
                e.wait_ge(sem("b1_cand"), b + 1)
                link(e, e.tensor_tensor(gate[:, b, :], gate[:, b, :], cand[:, b, :], ALU.mult))
                e.wait_ge(sem("b1_decay"), 1)
                e.tensor_tensor_scan(hid[:, b, :], decay.to_broadcast([128, T]), gate[:, b, :], 0.0, ALU.mult,
                                     ALU.add).then_inc(sem("b1_scan"), 1)
            for b in range(B):
                e.wait_ge(sem("b1_proj"), b + 1)
                e.scalar_tensor_tensor(out=y1[:, b, :], in0=ps[:, b, :], scalar=v("out_b"), in1=x_cur[:, b, :],
                                       op0=ALU.add, op1=ALU.add).then_inc(sem("b1_y"), 1)

        def b1_act(e):
            e.wait_ge(sem("load_vec"), 16)
            e.activation(decay, v("log_decay"), ACT.Exp).then_inc(sem("b1_decay"), 1)
            for b in range(B):
                e.wait_ge(sem("tap0"), TAPS)
                e.activation(gate[:, b, :], gate[:, b, :], ACT.Sigmoid, bias=v("gate_b"))
                e.wait_ge(sem("tap1"), TAPS)
                e.activation(cand[:, b, :], cand[:, b, :], ACT.Tanh, bias=v("cand_b")).then_inc(sem("b1_cand"), 1)

        def b1_pe(e):
            e.wait_ge(sem("load_wA"), 16)
            for b in range(B):
                e.wait_ge(sem("b1_scan"), b + 1)
                e.matmul(ps[:, b, :], wt["out_w"], hid[:, b, :], start=True, stop=True).then_inc(sem("b1_proj"), 1)
        pe_steps.append(b1_pe)
        act_steps.append(b1_act)
        dve_steps.append(b1_dve)
        n = make_norm(batches(y1, x_aux), counted("b1_y"), gain="norm_w", eps="eps_attn", mean=False, other_table=True)
        add_norm(n)

        def residual(name, k, prev):
            def f(e):
                for b in range(B):
                    e.wait_ge(*prev.done(b))
                    e.tensor_tensor(x_aux[:, b, :], x_aux[:, b, :], x_cur[:, b, :], ALU.add).then_inc(sem(name), 1)
            return f
        dve_steps.append(residual("b1_sum", 0, n))
        n = make_norm(batches(x_aux, x_cur), counted("b1_sum"))
        add_norm(n)
        final = n

        class Attn:
            def __init__(self, k, wide=False, causal=False):
                self.k, self.wide, self.causal = k, wide, causal
                self.base = k * B * UNITS
                c = Carve()
                if wide:
                    self.slots = 4
                    self.pt = c(4 * 4 * T).rearrange("p (s k q) -> p s k q", s=4, k=4)
                    self.ptc = c(4 * T).rearrange("p (s q) -> p s q", s=4)
                    self.p = c(8 * KEYS).rearrange("p (s k) -> p s k", s=8)
                    self.np = 8
                    self.qz = c(4 * T).rearrange("p (a r t) -> p a r t", a=2, r=2)
                    self.kt = c(2 * KEYS).rearrange("p (a t) -> p a t", a=2)
                    self.vv = c(4 * XH * XD).rearrange("p (k n) -> p k n", k=4)
                    self.vc = c(XH * XD)
                    self.kc = c(8 * B * S).rearrange("p (h n) -> p h n", h=8)
                else:
                    self.slots = 8
                    self.pt = c(8 * 4 * T).rearrange("p (s k q) -> p s k q", s=8, k=4)
                    self.p = c(4 * T).rearrange("p (s k) -> p s k", s=4)
                    self.np = 4
                    self.qt, self.kt = c(T), c(T)
                    self.qm = c(2 * T).rearrange("p (a t) -> p a t", a=2)
                    self.vv = c(4 * T).rearrange("p (k n) -> p k n", k=4)
                    self.x2 = c(T * B).rearrange("p (b t) -> p b t", b=B) if causal else None
                    self.ot = cent
                self.nm = stat[:, 0:4]
                self.sm = stat[:, 4:8]
                self.rs = stat[:, 8:12]

            def keys(self, u):
                return (u % QB + 1) * 128 if self.causal else (KEYS if self.wide else T)

            def s_view(self, u):
                if self.wide:
                    return ps[:, 2 * (u % 2):2 * (u % 2) + 2, 0:KEYS // 2]
                return ps[:, u % 4, 0:self.keys(u)]

            def p_view(self, u):
                if self.wide:
                    return self.p[:, u % self.np, :].rearrange("p (a k) -> p a k", a=2)
                return self.p[:, u % self.np, 0:self.keys(u)]

            def scores(self, e, b, u):
                n = self.base + b * UNITS + u
                h, q = u // QB, u % QB
                deep = 2 if self.wide else 4
                if n - deep >= 0:
                    e.wait_ge(sem("exp_done"), n - deep + 1)
                if self.wide:
                    e.wait_ge(sem("bank7_read"), b * B7 + 2 * (h // 2 + 1) + max(h // 2 - 2, 0))
                    e.wait_ge(sem("ctx_keys"), b * 8 + h // 2 + 1)
                    for a in range(2):
                        i = e.matmul(ps[:, 2 * (u % 2) + a, 0:KEYS // 2],
                                     self.qz[:, h // 2 % 2, h % 2, q * 128:q * 128 + 128],
                                     self.kt[:, h // 2 % 2, a * KEYS // 2:(a + 1) * KEYS // 2], start=True, stop=True)
                else:
                    e.wait_ge(sem("q_masked"), self.qm0 + b * H + h + 1)
                    i = e.matmul(self.s_view(u), self.qm[:, h % 2, q * 128:q * 128 + 128], self.kt[:, 0:self.keys(u)],
                                 start=True, stop=True)
                i.then_inc(sem("scored"), 1)

            def neg_max(self, e, b, u):
                n = self.base + b * UNITS + u
                e.wait_ge(sem("scored"), n + 1)
                if n >= 4:
                    e.wait_ge(sem("exp_done"), n - 3)
                if self.causal:
                    q = u % QB
                    link(e, e.tensor_tensor(ps[:, u % 4, q * 128:q * 128 + 128], ps[:, u % 4, q * 128:q * 128 + 128],
                                            wt["causal"], ALU.add))
                e.tensor_reduce(self.nm[:, u % 4:u % 4 + 1], self.s_view(u), AX.XY if self.wide else AX.X, ALU.max,
                                negate=True).then_inc(sem("max_done"), 1)

            def exp(self, e, b, u):
                n = self.base + b * UNITS + u
                e.wait_ge(sem("max_done"), n + 1)
                if self.wide:
                    if u % QB == 0 and n // QB >= 2:
                        e.wait_ge(sem("ctx_turned"), n // QB - 1)
                elif n - self.base >= 4:
                    e.wait_ge(sem("transposed"), n - 3)
                e.activation(self.p_view(u), self.s_view(u), ACT.Exp, bias=self.nm[:, u % 4:u % 4 + 1],
                             accum_out=self.sm[:, u % 4:u % 4 + 1]).then_inc(sem("exp_done"), 1)

            def normalise(self, e, b, u):
                n = self.base + b * UNITS + u
                e.wait_ge(sem("exp_done"), n + 1)
                i = e.reciprocal(self.rs[:, u % 4:u % 4 + 1], self.sm[:, u % 4:u % 4 + 1])
                link(e, i)
                w = self.keys(u)
                e.tensor_scalar(self.p[:, u % self.np, 0:w], self.p[:, u % self.np, 0:w], self.rs[:, u % 4:u % 4 + 1], None,
                                ALU.mult).then_inc(sem("prob_done"), 1)

            def transpose(self, e, b, u):
                n = self.base + b * UNITS + u
                e.wait_ge(sem("prob_done"), n + 1)
                if n >= 2:
                    e.wait_ge(sem("evacuated"), n - 1)
                for k in range((u % QB + 1) if self.causal else 4):
                    i = e.transpose(ps[:, 4 + u % 2, k * 128:k * 128 + 128], self.p[:, u % self.np, k * 128:k * 128 + 128],
                                    ident)
                i.then_inc(sem("transposed"), 1)
                if self.wide and u % QB == QB - 1:
                    if b * XH + u // QB >= 1:
                        e.wait_ge(sem("ctx_probs"), b * XH + u // QB)
                    for q in range(QB):
                        i = e.transpose(ps[0:S, 6, q * 128:q * 128 + 128],
                                        self.p[:, (u - QB + 1 + q) % self.np, T:KEYS], ident)
                    i.then_inc(sem("ctx_turned"), 1)

            def evacuate(self, e, b, u):
                n = self.base + b * UNITS + u
                h, q = u // QB, u % QB
                e.wait_ge(sem("transposed"), n + 1)
                if q == 0:
                    g = (b * H + h - self.slots) // self.per
                    if g >= 0:
                        e.wait_ge(sem("pv_done"), self.pv0 + g + 1)
                kk = (q + 1) if self.causal else 4
                e.copy(self.pt[:, h % self.slots, 0:kk, q * 128:q * 128 + 128],
                       ps[:, 4 + u % 2, 0:kk * 128].rearrange("p (k q) -> p k q", k=kk)).then_inc(sem("evacuated"), 1)

            def pv(self, e, b, g, parts=range(4)):
                per, w = self.per, 128 // self.per
                h0 = g * per
                bank = 7 if self.wide else 6
                if parts[0] == 0:
                    e.wait_ge(sem("evacuated"), self.base + b * UNITS + (h0 + per) * QB)
                    if self.wide:
                        e.wait_ge(sem("ctx_probs"), b * XH + h0 + per)
                        self.bank_wait(e)
                    elif self.pv0 + b * (H // per) + g >= 1:
                        e.wait_ge(sem("pv_read"), self.pr0 + b * (H // per) + g)
                last = 4 if self.wide else 3
                for k in parts:
                    for j in range(per):
                        h = h0 + j
                        q0 = k * 128 if self.causal else 0
                        v_of = self.vv[:, k, :] if k < 4 else self.vc
                        p_of = self.pt[:, h % self.slots, k, q0:T] if k < 4 else self.ptc[:, h % self.slots, :]
                        i = e.matmul(ps[w * j:w * j + w, bank, q0:T], v_of[:, h * w:h * w + w], p_of,
                                     start=(k == 0), stop=(k == last), skip_group_check=True)
                if parts[-1] == last:
                    i.then_inc(sem("pv_done"), 1)
                    if self.wide:
                        self.bank_used()

        if stages >= 2:
            n_lat = make_norm(batches(x_cur, x_aux), [final.done(b) for b in range(B)], gain="x_ln2_g", bias="x_ln2_b")
            add_norm(n_lat)
            n_ctx = make_norm([(ctx_in[:, :], ctx_ln[:, :], B * S, 0)], [(sem("load_ctx"), 16)], gain="x_ln1_g",
                              bias="x_ln1_b")
            add_norm(n_ctx)
            ot_lo, ot_hi = cent, dev
            at = Attn(0, wide=True)
            at.per, at.pv0 = 2, 0
            Wq, Wkv, Wo = wt["Wq"], wt["Wkv"], wt["Wo"]

            def ot_of(g):
                return (ot_lo if g < 4 else ot_hi)[:, g % 4, :]

            def b2_pe(e):
                uses = [0]

                def b7_wait(e2):
                    if uses[0] >= 1:
                        e2.wait_ge(sem("bank7_read"), uses[0])

                def b7_used():
                    uses[0] += 1
                at.bank_wait, at.bank_used = b7_wait, b7_used
                e.wait_ge(sem("load_wB"), 16)
                e.wait_ge(*n_ctx.done(0))
                for hp in range(8):
                    if hp == 4:
                        e.wait_ge(sem("ctx_k_read"), 4)
                    i = e.matmul(ps[:, hp % 4, 0:B * S], Wkv[:, hp * 128:hp * 128 + 128], ctx_ln[:, :], start=True,
                                 stop=True)
                    i.then_inc(sem("ctx_k_proj"), 1)

                def qproj(b, hp):
                    b7_wait(e)
                    e.matmul(ps[:, 7, :], Wq[:, hp * 128:hp * 128 + 128], x_aux[:, b, :], start=True,
                             stop=True).then_inc(sem("bank7_written"), 1)
                    b7_used()

                def kproj(b, hp):
                    b7_wait(e)
                    e.matmul(ps[:, 7, :], Wkv[:, hp * 128:hp * 128 + 128], x_aux[:, b, :], start=True,
                             stop=True).then_inc(sem("bank7_written"), 1)
                    b7_used()
                for b in range(B):
                    e.wait_ge(*n_lat.done(b))
                    for k in range(5):
                        src = x_aux[:, b, k * 128:k * 128 + 128] if k < 4 else ctx_ln[:, b * S:b * S + S]
                        m = 128 if k < 4 else S
                        for a in range(2):
                            j = b * 10 + 2 * k + a
                            if j >= 2:
                                e.wait_ge(sem("v_read"), j - 1)
                            if b >= 1 and j % 10 < 2:
                                e.wait_ge(sem("evacuated"), at.base + b * UNITS)
                            e.matmul(ps[0:m, 4 + j % 2, :], src, Wkv[:, 1024 + a * 512:1536 + a * 512], start=True,
                                     stop=True).then_inc(sem("v_proj"), 1)
                    qproj(b, 0)
                    kproj(b, 0)
                    e.wait_ge(sem("v_read"), 10 * b + 10)
                    for i in range(UNITS + 8):
                        if i < UNITS:
                            at.scores(e, b, i)
                        if 2 <= i < UNITS + 2:
                            at.transpose(e, b, i - 2)
                        hp, r = i // 8, i % 8
                        if r == 1 and hp < 7:
                            qproj(b, hp + 1)
                        if r == 2 and hp < 7:
                            kproj(b, hp + 1)
                        if r >= 3 and hp >= 1:
                            at.pv(e, b, hp - 1, [r - 3])
                    b7_wait(e)
                    for hp in range(8):
                        i = e.matmul(ps[:, 7, :], Wo[:, hp * 128:hp * 128 + 128], ot_of(hp), start=(hp == 0),
                                     stop=(hp == 7))
                    i.then_inc(sem("b2_out"), 1)
                    b7_used()

            def b2_act(e):
                e.wait_ge(sem("b2_zeros"), 1)
                for hp in range(8):
                    e.wait_ge(sem("ctx_k_proj"), hp + 1)
                    e.copy(at.kc[:, hp, :], ps[:, hp % 4, 0:B * S]).then_inc(sem("ctx_k_read"), 1)
                for b in range(B):
                    for k in range(5):
                        m = 128 if k < 4 else S
                        if b >= 1 and k == 0:
                            e.wait_ge(sem("pv_done"), 8 * b)
                        for a in range(2):
                            j = b * 10 + 2 * k + a
                            e.wait_ge(sem("v_proj"), j + 1)
                            dst = at.vv[:, k, a * 512:a * 512 + 512] if k < 4 else at.vc[0:S, a * 512:a * 512 + 512]
                            e.copy(dst, ps[0:m, 4 + j % 2, :]).then_inc(sem("v_read"), 1)
                    for i in range(UNITS + 2):
                        if i < UNITS:
                            at.exp(e, b, i)
                        if i >= 2:
                            at.evacuate(e, b, i - 2)

            def b2_dve(e):
                written, pvs = [0], [0]
                e.memset(at.ptc[:, :, :], 0.0)
                e.memset(at.vc, 0.0)
                e.memset(at.qz[:, :, :, :], 0.0).then_inc(sem("b2_zeros"), 1)
                e.wait_ge(sem("b2_zeros"), 1)

                def qread(b, hp):
                    written[0] += 1
                    e.wait_ge(sem("bank7_written"), written[0])
                    if b * 8 + hp >= 2:
                        e.wait_ge(sem("scored"), (b * 8 + hp - 1) * 8)
                    for r in range(2):
                        i = e.tensor_scalar(at.qz[64 * r:64 * r + 64, hp % 2, r, :], ps[64 * r:64 * r + 64, 7, :],
                                            0.125, None, ALU.mult)
                    i.then_inc(sem("bank7_read"), 1)

                def kread(b, hp):
                    written[0] += 1
                    e.wait_ge(sem("bank7_written"), written[0])
                    e.tensor_copy(at.kt[:, hp % 2, 0:T], ps[:, 7, :]).then_inc(sem("bank7_read"), 1)

                def pread(b, g):
                    pvs[0] += 1
                    e.wait_ge(sem("pv_done"), pvs[0])
                    if b >= 1 and g == 0:
                        e.wait_ge(sem("b2_out"), b)
                    e.tensor_copy(ot_of(g), ps[:, 7, :]).then_inc(sem("bank7_read"), 1)

                def cread(b, h):
                    n = b * XH + h
                    e.wait_ge(sem("ctx_turned"), n + 1)
                    if n >= 4:
                        e.wait_ge(sem("pv_done"), (n - 4) // 2 + 1)
                    e.tensor_copy(at.ptc[0:S, h % 4, :], ps[0:S, 6, :]).then_inc(sem("ctx_probs"), 1)
                for b in range(B):
                    qread(b, 0)
                    kread(b, 0)
                    for i in range(UNITS + 9):
                        if i < UNITS:
                            at.neg_max(e, b, i)
                        if 1 <= i <= UNITS:
                            at.normalise(e, b, i - 1)
                        if i >= 6 and (i - 2) % 4 == 0 and (i - 2) // 4 - 1 < XH:
                            cread(b, (i - 2) // 4 - 1)
                        hp, r = i // 8, i % 8
                        if r == 0 and hp >= 2:
                            pread(b, hp - 2)
                        if r == 1 and hp < 7:
                            qread(b, hp + 1)
                        if r == 2 and hp < 7:
                            kread(b, hp + 1)
                    e.wait_ge(sem("b2_out"), b + 1)
                    e.tensor_tensor(x_aux[:, b, :], ps[:, 7, :], x_cur[:, b, :], ALU.add).then_inc(sem("bank7_read"), 1)

            def b2_pool(e):
                for b in range(B):
                    for hp in range(8):
                        n = b * 8 + hp
                        e.wait_ge(sem("ctx_k_read"), hp + 1)
                        if n >= 2:
                            e.wait_ge(sem("scored"), (n - 1) * 8)
                        e.tensor_copy(at.kt[:, hp % 2, T:KEYS],
                                      at.kc[:, hp, b * S:b * S + S]).then_inc(sem("ctx_keys"), 1)

            pe_steps.append(b2_pe)
            act_steps.append(b2_act)
            dve_steps.append(b2_dve)
            pool_steps.append(b2_pool)
            n = make_norm(batches(x_aux, x_cur), counted("bank7_read", 0, B7))
            add_norm(n)
            final = n

        def narrow(src, src_ready, dst, tag, load, wq, wk, wv, wo, bias_v=None, rope=None):
            causal = rope is not None
            SC = HD ** -0.5
            NG, LAG, STEPS = B * 4, 2, B * 4 + 3
            ROWS = 9 * HD
            NQ = 4 if rope else 2
            c = Carve()
            packs = [[c(H * T // 2).bitcast(BF16).rearrange("p (h t) -> p h t", h=H) for _ in range(2)]
                     for _ in range(2)]
            q_pack, k_pack = packs
            p_t = c(8 * T).rearrange("p (s t) -> p s t", s=8)
            vv = c(2 * 4 * H * 32).rearrange("p (a k h n) -> p a k h n", a=2, k=4, h=H)
            parts = c(2 * 3 * T // 2).bitcast(BF16).rearrange("p (w i t) -> p w i t", w=2, i=3)
            raw = c(2 * T).rearrange("p (a t) -> p a t", a=2)
            m_t, m_rest = c(128)[0:16], c(128)[0:16]
            m_parts = c(192)[0:16].bitcast(BF16).rearrange("p (i t) -> p i t", i=3)
            rs_wide = c(T)
            ones_row = p_t[0:3, 7, 0:T // 2].bitcast(BF16)
            nm = stat[:, 16:48].rearrange("p (a u) -> p a u", a=2)
            rs = stat[:, 48:64]
            ot = cent
            scr = nc.dram_tensor(tag + "_parts", (B, 2, 3 * HD, H * T), BF16, kind="Internal").ap()
            scr_m = nc.dram_tensor(tag + "_maxima", (NG, 3, 16 * 128), BF16, kind="Internal").ap()
            (ones_set, score, max_done, score2, exp_done, turned, m_split, m_out, m_rows, part_done, raw_done, b6_read,
             written, b7_read, qk_ready, split_q, split_k, parts_out, packed, rs_spread, vv_set, ones_rows) = (
                sem(f"{tag}_{x}") for x in ("ones_set", "score", "max", "score2", "exp", "turned", "m_split", "m_out",
                                            "m_rows", "part", "raw", "b6_read", "written", "b7_read", "qk_ready",
                                            "split_q", "split_k", "parts_out", "packed", "rs_spread", "vv_set", "ones_rows"))
            group_w = lambda G: slice(G % 4 * 4, G % 4 * 4 + 4)

            uses = [("qk", 0, j) for j in range(NQ)]
            for G in range(STEPS):
                if G % 4 == 0 and G // 4 + 1 < B:
                    uses += [("qk", G // 4 + 1, j) for j in range(NQ)]
                if G % 4 == 0 and G // 4 < B:
                    uses.append(("v", G // 4, 0))
                if G % 4 == 2 and G >= 6:
                    uses.append(("out", (G - 6) // 4, 0))
            at7 = {u: n_ + 1 for n_, u in enumerate(uses)}

            def at6(G, i):
                before = min(max(G - 1, 0), NG) + 2 * min(max(G - 3, 0), NG)
                return before + (1 if 1 <= G <= NG and i else 0) + (i if i else 1)

            def keys(u):
                return (u % 4 + 1) * 128 if causal else T

            def pe(e):
                e.wait_ge(sem("load_" + load), 16)
                e.wait_ge(*src_ready[B - 1])
                mats = [wt[w] for w in ([wq, rope[0], wk, rope[1]] if rope else [wq, wk])]

                def qk(b, j):
                    if b:
                        e.wait_ge(b7_read, at7["qk", b, j] - 1)
                    e.matmul(ps[:, 7 if b else 4 + j, :], mats[j], src[:, b, :], start=True,
                             stop=True).then_inc(written, 1)

                def pv(n_):
                    G, p = n_ // 4, n_ % 4
                    b = G // 4
                    e.wait_ge(exp_done, 4 * n_ + 4)
                    if p == 0:
                        e.wait_ge(b7_read, at7["v", b, 0])
                        if G:
                            e.wait_ge(raw_done, G)
                    q0 = p * 128 if causal else 0
                    for j in range(4):
                        i = e.matmul(ps[32 * j:32 * j + 32, 5, q0:T], vv[:, b % 2, p, G % 4 * 4 + j, :],
                                     p_t[:, n_ % 2 * 4 + j, q0:T], start=(p == 0), stop=(p == 3),
                                     skip_group_check=True)
                    i.then_inc(part_done, 1)
                for j in range(NQ):
                    qk(0, j)
                for step in range(STEPS * 16):
                    G, u = step // 16, step % 16
                    if G < NG:
                        h, q = G % 4 * 4 + u // 4, u % 4
                        if u == 0 and G % 4 == 0:
                            e.wait_ge(packed, 16 * 12 * (G // 4 + 1))
                        if step >= 2:
                            e.wait_ge(max_done, step - 1)
                        pack = (G // 4) % 2
                        i = e.matmul(ps[:, step % 2, 0:keys(u)], q_pack[pack][0:ROWS, h, q * 128:q * 128 + 128],
                                     k_pack[pack][0:ROWS, h, 0:keys(u)], start=True, stop=not causal,
                                     skip_group_check=True)
                        if causal:
                            i = e.matmul(ps[:, step % 2, q * 128:q * 128 + 128], wt_bf[:, 0:128], wt_bf[:, 128:256],
                                         start=False, stop=True, skip_group_check=True)
                        i.then_inc(score, 1)
                    if 2 <= G < NG + 2:
                        G2, m = G - LAG, step - 16 * LAG
                        h, k = G2 % 4 * 4 + u % 4, u // 4
                        if u == 0:
                            e.wait_ge(m_rows, 16 * (G2 + 1))
                            if G2 == 0:
                                e.wait_ge(ones_rows, 32)
                        if m >= 3:
                            e.wait_ge(exp_done, m - 2)
                        pack = (G2 // 4) % 2
                        q0 = k * 128 if causal else 0
                        i = e.matmul(ps[:, 2 + m % 3, q0:T], k_pack[pack][0:ROWS + 3, h, k * 128:k * 128 + 128],
                                     q_pack[pack][0:ROWS + 3, h, q0:T], start=True, stop=not causal,
                                     skip_group_check=True)
                        if causal:
                            i = e.matmul(ps[:, 2 + m % 3, q0:q0 + 128], wt_bf[:, 128:256], wt_bf[:, 0:128],
                                         start=False, stop=True, skip_group_check=True)
                        i.then_inc(score2, 1)
                    n_ = (step - 16 * LAG - PV_AT) // 4
                    if (step - PV_AT) % 4 == 0 and 0 <= n_ < 4 * NG:
                        pv(n_)
                    if u == 1 and 1 <= G <= NG:
                        e.wait_ge(max_done, 16 * G)
                        if at6(G, 0) > 1:
                            e.wait_ge(b6_read, at6(G, 0) - 1)
                        e.transpose(ps[0:16, 6, 0:128], nm[:, (G - 1) % 2, :], ident).then_inc(turned, 1)
                    if u == 5 and G >= 3:
                        e.wait_ge(raw_done, G - 2)
                        e.wait_ge(b6_read, at6(G, 1) - 1)
                        for q in range(4):
                            i = e.matmul(ps[:, 6, 4 * q:4 * q + 4], raw[:, (G - 3) % 2, q * 128:q * 128 + 128],
                                         v("sum_pick", 0, 4), start=True, stop=True)
                        i.then_inc(turned, 1)
                    if u == 8 and G >= 3:
                        e.wait_ge(rs_spread, G - 2)
                        for q in range(4):
                            i = e.matmul(ps[:, 6, q * 128:q * 128 + 128], rs_wide[:, q * 128:q * 128 + 128], ident,
                                         start=True, stop=True)
                        i.then_inc(turned, 1)
                    if G % 4 == 0 and G // 4 + 1 < B and u % 3 == 0 and 3 <= u < 3 + 3 * NQ:
                        qk(G // 4 + 1, u // 3 - 1)
                    if G % 4 == 0 and G // 4 < B and u == 15:
                        b = G // 4
                        e.wait_ge(b7_read, at7["v", b, 0] - 1)
                        for k in range(4):
                            i = e.matmul(ps[:, 7, k * 128:k * 128 + 128], src[:, b, k * 128:k * 128 + 128], wt[wv],
                                         start=True, stop=True)
                        i.then_inc(written, 1)
                    if G % 4 == 2 and G >= 6 and u == 11:
                        b = (G - 6) // 4
                        e.wait_ge(b6_read, at6(G, 2))
                        e.wait_ge(b7_read, at7["out", b, 0] - 1)
                        for g in range(4):
                            i = e.matmul(ps[:, 7, :], wt[wo][:, g * 128:g * 128 + 128], ot[:, g, :], start=(g == 0),
                                         stop=(g == 3))
                        i.then_inc(written, 1)

            def act(e):
                for m in range(16 * (NG + 1)):
                    G, u = m // 16 + LAG, m % 16
                    if m < 16 * NG:
                        e.wait_ge(score2, m + 1)
                        if m >= 8:
                            e.wait_ge(part_done, (m - 8) // 4 + 1)
                        q0 = u // 4 * 128 if causal else 0
                        e.activation(p_t[:, m % 8, q0:T], ps[:, 2 + m % 3, q0:T], ACT.Exp).then_inc(exp_done, 1)
                    if u == 3 and G >= 3:
                        e.wait_ge(part_done, 4 * (G - 2))
                        if G >= 5:
                            e.wait_ge(b6_read, at6(G - 2, 2))
                        e.copy(raw[:, (G - 3) % 2, :], ps[:, 5, :]).then_inc(raw_done, 1)
                    if u == 6 and G >= 3:
                        e.wait_ge(b6_read, at6(G, 1))
                        if G >= 4:
                            e.wait_ge(turned, at6(G - 1, 2))
                        e.copy(rs_wide.rearrange("p (n r) -> p n r", r=32),
                               rs.unsqueeze(2).to_broadcast([128, 16, 32])).then_inc(rs_spread, 1)

            def split(e, b, which):
                for step in range(4):
                    for w in which:
                        s_, base = (split_q, split_k)[w], 4 * b
                        x, rest, part = dev[:, 2 * w, :], dev[:, 2 * w + 1, :], parts[:, w, :, :]
                        if step == 0:
                            e.wait_ge(qk_ready, 2 * b + w + 1)
                            if b:
                                e.wait_ge(parts_out, 16 * 2 * b)
                            i = e.tensor_copy(part[:, 0, :], x)
                        else:
                            e.wait_ge(s_, base + step)
                            if step == 1:
                                i = e.tensor_tensor(rest, x, part[:, 0, :], ALU.subtract)
                            elif step == 2:
                                i = e.tensor_copy(part[:, 1, :], rest)
                            else:
                                i = e.tensor_tensor(part[:, 2, :], rest, part[:, 1, :], ALU.subtract)
                        i.then_inc(s_, 1)

            def dve(e):
                e.memset(ones_row, 1.0).then_inc(ones_set, 1)
                if causal:
                    e.wait_ge(sem("load_" + load), 16)
                    e.tensor_copy(wt_bf[:, 0:128], ident)
                    link(e, e.tensor_copy(wt_bf[:, 128:256], wt["causal"]))

                def qk(b, j):
                    e.wait_ge(written, at7["qk", b, j])
                    if b and j == 0:
                        e.wait_ge(split_q, 4 * b)
                        e.wait_ge(split_k, 4 * b)
                    bank = ps[:, 7 if b else 4 + j, :]
                    if rope:
                        e.scalar_tensor_tensor(out=dev[:, j, :], in0=bank, scalar=SC if j < 2 else 1.0,
                                               in1=wt["sin" if j % 2 else "cos"], op0=ALU.mult,
                                               op1=ALU.mult).then_inc(b7_read, 1)
                        if j % 2:
                            e.wait_ge(b7_read, at7["qk", b, j])
                            e.tensor_tensor(dev[:, j - 1, :], dev[:, j - 1, :], dev[:, j, :],
                                            ALU.add).then_inc(qk_ready, 1)
                    else:
                        if j == 0:
                            i = e.tensor_scalar(dev[:, 0, :], bank, v("f_bq"), SC, ALU.add, ALU.mult)
                        else:
                            i = e.tensor_scalar(dev[:, 2, :], bank, v("f_bk"), None, ALU.add)
                        i.then_inc(b7_read, 1)
                        e.wait_ge(b7_read, at7["qk", b, j])
                        e.nop().then_inc(qk_ready, 1)
                for j in range(NQ):
                    qk(0, j)
                split(e, 0, (0, 1))
                for step in range(STEPS * 16):
                    G, u = step // 16, step % 16
                    if G < NG:
                        e.wait_ge(score, step + 1)
                        if u == 0 and G >= 2:
                            e.wait_ge(turned, at6(G - 1, 0))
                        e.tensor_reduce(nm[:, G % 2, u:u + 1], ps[:, step % 2, 0:keys(u)], AX.X, ALU.max,
                                        negate=True).then_inc(max_done, 1)
                    if u == 2 and 1 <= G <= NG:
                        e.wait_ge(turned, at6(G, 0))
                        if G >= 2:
                            e.wait_ge(m_split, 4 * (G - 1))
                        e.tensor_copy(m_t, ps[0:16, 6, 0:128]).then_inc(b6_read, 1)
                    if u == 6 and G >= 3:
                        e.wait_ge(turned, at6(G, 1))
                        e.reciprocal(rs, ps[:, 6, 0:16]).then_inc(b6_read, 1)
                    if u == 9 and G >= 3:
                        G3 = G - 3
                        e.wait_ge(turned, at6(G, 2))
                        if G3 % 4 == 0 and G3:
                            e.wait_ge(written, at7["out", G3 // 4 - 1, 0])
                        e.tensor_tensor(ot[:, G3 % 4, :], raw[:, G3 % 2, :], ps[:, 6, :],
                                        ALU.mult).then_inc(b6_read, 1)
                    if G % 4 == 0 and G // 4 + 1 < B and u % 3 == 1 and 3 <= u < 3 + 3 * NQ:
                        qk(G // 4 + 1, u // 3 - 1)
                    if G % 4 == 1 and G // 4 < B and u == 0:
                        b = G // 4
                        e.wait_ge(written, at7["v", b, 0])
                        e.wait_ge(vv_set, 3)
                        if b >= 2:
                            e.wait_ge(part_done, 16 * (b - 1))
                        out_v = vv[:, b % 2, :, :, 0:HD]
                        in_v = ps[:, 7, :].rearrange("p (k h d) -> p k h d", k=4, h=H)
                        if bias_v:
                            bias = wt[bias_v].rearrange("p (h d) -> p h d", h=H).unsqueeze(1).to_broadcast(
                                [128, 4, H, HD])
                            e.tensor_tensor(out_v, in_v, bias, ALU.add).then_inc(b7_read, 1)
                        else:
                            e.tensor_copy(out_v, in_v).then_inc(b7_read, 1)
                    if G % 4 == 2 and G >= 6 and u == 13:
                        b = (G - 6) // 4
                        e.wait_ge(written, at7["out", b, 0])
                        if bias_v:
                            o = e.scalar_tensor_tensor(out=dst[:, b, :], in0=ps[:, 7, :], scalar=v("f_bo"),
                                                       in1=x_cur[:, b, :], op0=ALU.add, op1=ALU.add)
                        else:
                            o = e.tensor_tensor(dst[:, b, :], ps[:, 7, :], x_cur[:, b, :], ALU.add)
                        o.then_inc(b7_read, 1)

            def pool(e):
                e.wait_ge(*src_ready[B - 1])
                e.memset(vv[:, 0, :, :, :], 0.0).then_inc(vv_set, 1)
                e.memset(vv[:, 1, :, :, :], 0.0).then_inc(vv_set, 1)
                e.wait_ge(vv_set, 2)
                e.memset(vv[:, :, :, :, HD:HD + 1].rearrange("p a k h n -> p (a k h) n"), 1.0).then_inc(vv_set, 1)
                for G in range(NG + 1):
                    if G:
                        s_, base = m_split, 4 * (G - 1)
                        e.wait_ge(b6_read, at6(G, 0))
                        if G >= 2:
                            e.wait_ge(m_out, 16 * (G - 1))
                        e.tensor_copy(m_parts[:, 0, :], m_t).then_inc(s_, 1)
                        e.wait_ge(s_, base + 1)
                        e.tensor_tensor(m_rest, m_t, m_parts[:, 0, :], ALU.subtract).then_inc(s_, 1)
                        e.wait_ge(s_, base + 2)
                        e.tensor_copy(m_parts[:, 1, :], m_rest).then_inc(s_, 1)
                        e.wait_ge(s_, base + 3)
                        e.tensor_tensor(m_parts[:, 2, :], m_rest, m_parts[:, 1, :], ALU.subtract).then_inc(s_, 1)
                        e.wait_ge(s_, base + 4)
                        e.dma_start(scr_m[G - 1].rearrange("i (u t) -> u i t", u=16), m_parts).then_inc(m_out, 16)
                        e.wait_ge(m_out, 16 * G)
                        e.dma_start(q_pack[(G - 1) // 4 % 2][ROWS:ROWS + 3, group_w(G - 1), :],
                                    scr_m[G - 1].rearrange("i (h t) -> i h t", h=4)).then_inc(m_rows, 16)
                    if G % 4 < 2 and G // 4 + 1 < B:
                        split(e, G // 4 + 1, (G % 4,))

            def sp(e):
                e.wait_ge(ones_set, 1)
                for a in range(2):
                    e.dma_start(k_pack[a][ROWS:ROWS + 3, :, :],
                                ones_row.unsqueeze(1).to_broadcast([3, H, T])).then_inc(ones_rows, 16)
                for b in range(B):
                    for w in range(2):
                        e.wait_ge((split_q, split_k)[w], 4 * b + 4)
                        e.dma_start(scr[b, w].rearrange("(i d) (h t) -> (d h) i t", i=3, h=H),
                                    parts[:, w, :, :]).then_inc(parts_out, 16)
                    e.wait_ge(parts_out, 16 * 2 * (b + 1))
                    if b >= 2:
                        e.wait_ge(score2, 64 * (b - 1))
                    for i in range(3):
                        e.dma_start(q_pack[b % 2][24 * i:24 * i + 24, :, :],
                                    scr[b, 0].rearrange("r (h t) -> r h t", h=H)).then_inc(packed, 16)
                        for j in range(3):
                            r = 24 * i + 8 * j
                            e.dma_start(k_pack[b % 2][r:r + 8, :, :], scr[b, 1, 8 * i:8 * i + 8].rearrange(
                                "r (h t) -> r h t", h=H)).then_inc(packed, 16)
            pe_steps.append(pe)
            act_steps.append(act)
            dve_steps.append(dve)
            pool_steps.append(pool)
            sp_steps.append(sp)
            return [(b7_read, at7["out", b, 0]) for b in range(B)]

        if stages >= 3:
            b3_res = narrow(x_cur, [final.done(b) for b in range(B)], x_aux, "b3", "wC", "f_Wq", "f_Wk", "f_Wv", "f_Wo",
                            bias_v="f_bv")
            n3 = make_norm(batches(x_aux, x_aux), b3_res, gain="f_ln1_g", bias="f_ln1_b")
            add_norm(n3)

            c = Carve()
            mask = c(2 * 4 * T).rearrange("p (a e t) -> p a e t", a=2, e=4)
            act_r = c(4 * T).rearrange("p (s t) -> p s t", s=4)
            key, key_f, key_c = c(T), c(T), c(T)
            key_i = c(T).bitcast(I32)
            W1, W2 = wt["W1"], wt["W2"]
            NI = E0 * C0

            def moe_pe(e):
                e.wait_ge(sem("load_wM0"), 16)

                def route(b):
                    e.wait_ge(*n3.done(b))
                    if b == 0:
                        e.wait_ge(*n3.done(3))
                    if b >= 2:
                        e.wait_ge(sem("key_read"), b - 1)
                    e.matmul(ps[:, 6 + b % 2, :], wt["router"], x_aux[:, b, :], start=True,
                             stop=True).then_inc(sem("routed"), 1)

                def down(b, i):
                    e.wait_ge(sem("relu_gated"), b * NI + i + 1)
                    if i == 0 and b >= 2:
                        e.wait_ge(sem("b3_sum"), b - 1)
                    e.matmul(ps[:, 4 + b % 2, :], W2[:, i * 128:i * 128 + 128], act_r[:, i % 4, :], start=(i == 0),
                             stop=(i == NI - 1)).then_inc(sem("moe_down"), 1)
                route(0)
                for b in range(B):
                    if b + 1 < B:
                        route(b + 1)
                    for i in range(NI + 3):
                        if i < NI:
                            n = b * NI + i
                            if n >= 4:
                                e.wait_ge(sem("relu_done"), n - 3)
                            e.matmul(ps[:, i % 4, :], W1[:, i * 128:i * 128 + 128], x_aux[:, b, :], start=True,
                                     stop=True).then_inc(sem("moe_up"), 1)
                        if i >= 3:
                            down(b, i - 3)

            def moe_act(e):
                for n in range(B * NI):
                    e.wait_ge(sem("moe_up"), n + 1)
                    if n >= 4:
                        e.wait_ge(sem("moe_down"), n - 3)
                    e.activation(act_r[:, n % 4, :], ps[:, n % 4, :], ACT.Relu,
                                 bias=v("f_b1", n % NI)).then_inc(sem("relu_done"), 1)

            def moe_pool(e):
                for n in range(B * NI):
                    b, ex = n // NI, n % NI // C0
                    e.wait_ge(sem("masks"), b + 1)
                    e.wait_ge(sem("relu_done"), n + 1)
                    e.tensor_tensor(act_r[:, n % 4, :], act_r[:, n % 4, :], mask[:, b % 2, ex, :],
                                    ALU.mult).then_inc(sem("relu_gated"), 1)

            def moe_dve(e):
                def masks(b):
                    e.wait_ge(sem("routed"), b + 1)
                    if b >= 2:
                        e.wait_ge(sem("relu_gated"), (b - 1) * NI)
                    i = e.tensor_scalar(key, ps[:, 6 + b % 2, :], v("router_b"), None, ALU.add)
                    i.then_inc(sem("key_read"), 1)
                    e.wait_ge(sem("key_read"), b + 1)
                    link(e, e.tensor_copy(key_i, key))
                    link(e, e.tensor_copy(key_f, key_i))
                    link(e, e.tensor_tensor(key_c, key_f, key, ALU.is_gt))
                    link(e, e.tensor_tensor(key_f, key_f, key_c, ALU.subtract))
                    link(e, e.tensor_copy(key_i, key_f))
                    link(e, e.tensor_scalar(key_i, key_i, E0 - 1, None, ALU.bitwise_and))
                    link(e, e.tensor_copy(key_f, key_i))
                    for ex in range(E0):
                        i = e.tensor_scalar(mask[:, b % 2, ex, :], key_f, float(ex), None, ALU.is_equal)
                    i.then_inc(sem("masks"), 1)

                def total(b):
                    e.wait_ge(sem("moe_down"), (b + 1) * NI)
                    e.wait_ge(sem("masks"), b + 1)
                    link(e, e.tensor_tensor(x_aux[:, b, :], ps[:, 4 + b % 2, :], x_aux[:, b, :], ALU.add))
                    for ex in range(E0):
                        i = e.scalar_tensor_tensor(out=x_aux[:, b, :], in0=mask[:, b % 2, ex, :],
                                                   scalar=v("f_b2", ex), in1=x_aux[:, b, :], op0=ALU.mult, op1=ALU.add)
                        if ex < E0 - 1:
                            link(e, i)
                    i.then_inc(sem("b3_sum"), 1)
                masks(0)
                for b in range(B):
                    if b + 1 < B:
                        masks(b + 1)
                    total(b)

            def moe_sp(e):
                e.wait_ge(sem("b2_out"), B)
                e.dma_start(reg1[:, 0:width["wD"]], groups["wD"]).then_inc(sem("load_wD"), 16)
                e.wait_ge(sem("b4_o"), 1) if stages >= 4 else e.wait_ge(sem("moe_down"), B * NI)
                e.dma_start(reg2[:, 0:width["wM1"]], groups["wM1"]).then_inc(sem("load_wM1"), 16)
            pe_steps.append(moe_pe)
            act_steps.append(moe_act)
            pool_steps.append(moe_pool)
            dve_steps.append(moe_dve)
            sp_steps.append(moe_sp)
            n = make_norm(batches(x_aux, x_aux), counted("b3_sum"), gain="f_ln2_g", bias="f_ln2_b")
            add_norm(n)
            dve_steps.append(residual("b3_both", 0, n))
            n = make_norm(batches(x_aux, x_cur), counted("b3_both"))
            add_norm(n)
            final = n

        def gated(tag, per, rows, src, src_done, w_gate, w_up, w_down, act_r, weight=None, load=None, weight_ready=None,
                  extra=None):
            s_up, s_silu, s_prod, s_down = (sem(f"{tag}_{x}") for x in ("up", "silu", "prod", "down"))
            s_in = sem(tag + "_gated") if weight else s_prod
            extra = extra or {}
            R = rows

            def pe(e):
                if load:
                    e.wait_ge(sem("load_" + load), 16)
                e.wait_ge(*src_done[B - 1])
                for step in extra.get("pe_first", ()):
                    step(e)
                for b in range(B):
                    for i in range(per + 2):
                        n = b * per + i
                        if i < per:
                            if n >= 2:
                                e.wait_ge(s_silu, n - 1)
                                e.wait_ge(s_prod, n - 1)
                            e.matmul(ps[0:R, n % 2, :], w_gate(i), src[:, b, :], start=True, stop=True)
                            e.matmul(ps[0:R, 2 + n % 2, :], w_up(i), src[:, b, :], start=True,
                                     stop=True).then_inc(s_up, 1)
                        if i >= 2:
                            m = n - 2
                            e.wait_ge(s_in, m + 1)
                            if i == 2 and b >= 2:
                                e.wait_ge(sem(tag + "_sum"), b - 1)
                            e.matmul(ps[:, 4 + b % 2, :], w_down(i - 2), act_r[0:R, m % 4, :], start=(i == 2),
                                     stop=(i == per + 1)).then_inc(s_down, 1)
                        if "pe" in extra:
                            extra["pe"](e, b, i)

            def act(e):
                for step in extra.get("act_first", ()):
                    step(e)
                for n in range(B * per):
                    e.wait_ge(s_up, n + 1)
                    if n >= 4:
                        e.wait_ge(s_down, n - 3)
                    e.activation(act_r[0:R, n % 4, :], ps[0:R, n % 2, :], ACT.Silu).then_inc(s_silu, 1)
                    if "act" in extra:
                        extra["act"](e, n // per, n % per)

            def dve(e):
                for step in extra.get("dve_first", ()):
                    step(e)
                for b in range(B):
                    for i in range(per):
                        n = b * per + i
                        e.wait_ge(s_silu, n + 1)
                        e.tensor_tensor(act_r[0:R, n % 4, :], act_r[0:R, n % 4, :], ps[0:R, 2 + n % 2, :],
                                        ALU.mult).then_inc(s_prod, 1)
                        if "dve" in extra:
                            extra["dve"](e, b, i)
                    e.wait_ge(s_down, (b + 1) * per)
                    extra["total"](e, b).then_inc(sem(tag + "_sum"), 1)

            def pool(e):
                for b in range(B):
                    for i in range(per):
                        n = b * per + i
                        if i == 0:
                            e.wait_ge(*weight_ready(b))
                        e.wait_ge(s_prod, n + 1)
                        e.tensor_tensor(act_r[:, n % 4, :], act_r[:, n % 4, :], weight(b, i),
                                        ALU.mult).then_inc(s_in, 1)
            pe_steps.append(pe)
            act_steps.append(act)
            dve_steps.append(dve)
            if weight:
                pool_steps.append(pool)

        if stages >= 4:
            c = Carve()
            blocks = lambda x: x.rearrange("p (n i d) -> p n i d", i=BL, d=HD)
            q_raw = c(T * HD).rearrange("p (t d) -> p t d", d=HD)
            k_hat = c(T * HD).rearrange("p (t d) -> p t d", d=HD)
            y_flat = c(T * 12)
            y = y_flat.rearrange("p (t w) -> p t w", w=12)
            hist_flat = c((NB + 1) * 32)
            hist = hist_flat.rearrange("p (n j d) -> p n j d", j=4, d=HD)
            terms_flat = c(2 * CB * 144)
            terms = terms_flat.rearrange("p (c n i j d) -> p (c n) i j d", c=2, n=CB, i=BL, j=4)
            alpha, beta, gamma, to_end, t_one, t_two = (c(T) for _ in range(6))
            rank1 = c(2 * 32 * (BL + 1)).rearrange("p (a j d l) -> p a j d l", a=2, j=4, l=BL + 1)
            k_sq = terms_flat[:, 0:T * HD].rearrange("p (t d) -> p t d", d=HD)
            prod_k = terms_flat
            q_sq = hist_flat[:, 0:T * HD].rearrange("p (t d) -> p t d", d=HD)
            kk_dot = hist_flat[:, 0:3 * T].rearrange("p (s n i) -> p s n i", s=3, i=BL)
            xp = y_flat[:, 0:B * (T + CTAPS - 1)].rearrange("p (b t) -> p b t", b=B)
            qk_dot = x_aux.rearrange("p s (n i) -> p s n i", i=BL)
            prod_q = (reg2[:, 0:T * HD], reg2[:, T * HD:T * HD + T * HD // 2])
            prod_o = reg2[:, 0:2 * CB * BL * 32].rearrange("p (c n i j d) -> p c n i j d", c=2, n=CB, i=BL, j=4)
            o_tmp = terms_flat[:, 0:4 * T].rearrange("p (n i j) -> p n i j", i=BL, j=4)
            r_k, r_q, coef = dev[:, 0, :], dev[:, 1, :], dev[:, 2, :]
            neg_delta = reg2[:, T * HD:T * (HD + 4)].rearrange("p (n i j) -> p n i j", i=BL, j=4)
            o_tok = cent.rearrange("p b t -> p (b t)").rearrange("p (t j) -> p t j", j=4)
            PADW = CTAPS - 1
            n = make_norm([(x_cur[:, b, :], xp[:, b, PADW:], T, b) for b in range(B)],
                          [final.done(b) for b in range(B)], gain="norm1_w", eps="eps6", mean=False)
            add_norm(n)
            n4 = n
            cols = [("a_s", 0), ("b_s", 0)] + [("k_s", d) for d in range(8)] + [("q_s", d) for d in range(8)] \
                + [("v_s", j) for j in range(4)]

            def b4_pe(e):
                e.wait_ge(sem("load_wD"), 16)
                e.wait_ge(sem("b4_xc"), 1)
                for g, (w, d) in enumerate(cols):
                    if 8 <= g < 10:
                        e.wait_ge(sem("b4_act_read"), g - 7)
                    elif g >= 10:
                        e.wait_ge(sem("b4_dve_read"), g - 9)
                    for b in range(B):
                        i = e.matmul(ps[32 * b:32 * b + 32, g % 8, :], wt[w][:, d * 32:d * 32 + 32], x_aux[:, b, :],
                                     start=True, stop=True)
                    i.then_inc(sem("b4_proj"), 1)

            def b4_act(e):
                e.wait_ge(sem("b4_conv"), CTAPS)
                e.activation(x_aux[:, :, :], x_aux[:, :, :], ACT.Silu, bias=v("conv_b")).then_inc(sem("b4_xc"), 1)
                e.wait_ge(sem("b4_proj"), 1)
                e.activation(alpha, ps[:, 0, :], ACT.Sigmoid, bias=v("four")).then_inc(sem("b4_act_read"), 1)
                e.wait_ge(sem("b4_proj"), 2)
                e.activation(beta, ps[:, 1, :], ACT.Sigmoid).then_inc(sem("b4_act_read"), 1)
                e.preload_act_table_set("natural_log_exp_and_others")
                e.wait_ge(sem("b4_dve_read"), 8)
                e.activation(k_sq, k_hat, ACT.Square).then_inc(sem("b4_square"), 1)
                e.wait_ge(sem("b4_dve_read"), 16)
                e.activation(q_sq, q_raw, ACT.Square).then_inc(sem("b4_square"), 1)
                for n_, r in enumerate((r_k, r_q)):
                    e.wait_ge(sem("b4_len"), n_ + 1)
                    e.activation(r, r, ACT.Ln, bias=v("eps6")).then_inc(sem("b4_ln"), 1)
                    e.wait_ge(sem("b4_ln"), n_ + 1)
                    e.activation(r, r, ACT.Exp, scale=-0.5).then_inc(sem("b4_rlen"), 1)
                e.wait_ge(sem("b4_solved"), 1)
                for n_ in range(NB):
                    if n_:
                        e.wait_ge(sem("b4_state"), n_)
                    e.activation(rank1[:, n_ % 2, :, :, BL], hist[:, n_, :, :], ACT.Copy,
                                 scale=gamma[:, BL * n_ + BL - 1:BL * n_ + BL]).then_inc(sem("b4_carry"), 1)

            def per_d(x, n_=HD):
                return x.unsqueeze(2).to_broadcast([128, T, n_])

            def b4_dve(e):
                link(e, e.memset(xp[:, :, 0:PADW], 0.0))
                for b in range(B):
                    e.wait_ge(*n4.done(b))
                for k in range(CTAPS):
                    if k == 0:
                        i = e.tensor_scalar(x_aux[:, :, :], xp[:, :, 0:T], v("conv_w"), None, ALU.mult)
                    else:
                        e.wait_ge(sem("b4_conv"), k)
                        i = e.scalar_tensor_tensor(out=x_aux[:, :, :], in0=xp[:, :, k:k + T], scalar=v("conv_w", k),
                                                   in1=x_aux[:, :, :], op0=ALU.mult, op1=ALU.add)
                    i.then_inc(sem("b4_conv"), 1)
                for g in range(2, 22):
                    e.wait_ge(sem("b4_proj"), g + 1)
                    if g < 10:
                        i = e.tensor_copy(k_hat[:, :, g - 2], ps[:, g % 8, :])
                    elif g < 18:
                        i = e.tensor_copy(q_raw[:, :, g - 10], ps[:, g % 8, :])
                    else:
                        e.wait_ge(sem("b4_act_read"), 2)
                        i = e.scalar_tensor_tensor(out=y[:, :, g - 10], in0=ps[:, g % 8, :], scalar=-1.0,
                                                   in1=beta, op0=ALU.mult, op1=ALU.mult)
                    i.then_inc(sem("b4_dve_read"), 1)
                e.wait_ge(sem("b4_square"), 1)
                e.tensor_reduce(r_k, k_sq, AX.X, ALU.add).then_inc(sem("b4_len"), 1)
                e.wait_ge(sem("b4_square"), 2)
                e.tensor_reduce(r_q, q_sq, AX.X, ALU.add).then_inc(sem("b4_len"), 1)
                blk = lambda x: x.rearrange("p (n i) -> p n i", i=BL)
                a_, g_, e_, t1, t2, cf = (blk(x) for x in (alpha, gamma, to_end, t_one, t_two, coef))
                link(e, e.tensor_copy(gamma, alpha))
                for i in range(1, BL):
                    link(e, e.tensor_tensor(g_[:, :, i], g_[:, :, i - 1], a_[:, :, i], ALU.mult))
                e.tensor_tensor(t1[:, :, 1:], a_[:, :, 1:], a_[:, :, :BL - 1], ALU.mult).then_inc(sem("b4_decay"), 1)
                e.wait_ge(sem("b4_decay"), 1)
                link(e, e.tensor_tensor(t2[:, :, 2:], t1[:, :, 2:], a_[:, :, :BL - 2], ALU.mult))
                e.memset(e_[:, :, 3], -1.0)
                e.tensor_scalar(e_[:, :, 2], a_[:, :, 3], -1.0, None, ALU.mult)
                e.tensor_scalar(e_[:, :, 1], t1[:, :, 3], -1.0, None, ALU.mult)
                link(e, e.tensor_scalar(e_[:, :, 0], t2[:, :, 3], -1.0, None, ALU.mult))
                e.wait_ge(sem("b4_rlen"), 1)
                e.tensor_tensor(k_hat, k_hat, per_d(r_k), ALU.mult).then_inc(sem("b4_khat"), 1)
                e.wait_ge(sem("b4_khat"), 1)
                k4, q4, y4 = (x.rearrange("p (n i) d -> p n i d", i=BL) for x in (k_hat, q_raw, y))
                span = (None, a_, t1, t2)

                def dots(red, out_, s_):
                    view = red[:, 0:NB * (BL - s_) * HD].rearrange("p (n i d) -> p n i d", n=NB, d=HD)
                    return e.tensor_reduce(out_[:, :, s_:], view, AX.X, ALU.add)

                def spread(x, i0, i1, w):
                    return x[:, :, i0:i1].unsqueeze(3).to_broadcast([128, NB, i1 - i0, w])
                for s_ in range(1, BL):
                    view = prod_k[:, 0:NB * (BL - s_) * HD].rearrange("p (n i d) -> p n i d", n=NB, d=HD)
                    link(e, e.tensor_tensor(view, k4[:, :, s_:, :], k4[:, :, :BL - s_, :], ALU.mult))
                    link(e, dots(prod_k, kk_dot[:, s_ - 1], s_))
                    link(e, e.tensor_tensor(kk_dot[:, s_ - 1, :, s_:], kk_dot[:, s_ - 1, :, s_:], span[s_][:, :, s_:],
                                            ALU.mult))
                    link(e, e.tensor_tensor(kk_dot[:, s_ - 1, :, s_:], kk_dot[:, s_ - 1, :, s_:],
                                            blk(beta)[:, :, s_:], ALU.mult))
                link(e, e.tensor_tensor(coef, gamma, beta, ALU.mult))
                link(e, e.tensor_tensor(y[:, :, 0:HD], k_hat, per_d(coef), ALU.mult))
                tmp12 = prod_k[:, 0:NB * 12].rearrange("p (n w) -> p n w", w=12)
                for i in range(1, BL):
                    for s_ in range(1, i + 1):
                        c_ = kk_dot[:, s_ - 1, :, i].unsqueeze(2).to_broadcast([128, NB, 12])
                        link(e, e.tensor_tensor(tmp12, y4[:, :, i - s_, :], c_, ALU.mult))
                        link(e, e.tensor_tensor(y4[:, :, i, :], y4[:, :, i, :], tmp12, ALU.subtract))
                e.memset(hist[:, 0, :, :], 0.0).then_inc(sem("b4_solved"), 1)
                for n_, s_ in enumerate((0, 2, 1, 3)):
                    e.wait_ge(sem("b4_qk"), n_ + 1)
                    i = dots(prod_q[n_ % 2], qk_dot[:, s_], s_)
                    i.then_inc(sem("b4_qkred"), 1)
                e.wait_ge(sem("b4_qkred"), 4)
                for s_ in range(1, BL):
                    link(e, e.tensor_tensor(qk_dot[:, s_, :, s_:], qk_dot[:, s_, :, s_:], span[s_][:, :, s_:], ALU.mult))
                link(e, e.tensor_tensor(k_hat, k_hat, per_d(to_end), ALU.mult))
                e.wait_ge(sem("b4_solved"), 1)

                def outputs(ch):
                    e.wait_ge(sem("b4_qprod"), ch + 1)
                    o_ = o_tok[:, ch * CB * BL:(ch + 1) * CB * BL, :]
                    return e.tensor_reduce(o_, prod_o[:, ch % 2].rearrange("p n i j d -> p (n i) j d"), AX.X, ALU.add)
                for n_ in range(NB):
                    ch = n_ // CB
                    if n_ % CB == 0:
                        e.wait_ge(sem("b4_vset"), ch + 1)
                        if ch >= 2:
                            outputs(ch - 2)
                    if n_:
                        e.wait_ge(sem("b4_state"), n_)
                    slot = n_ % (2 * CB)
                    e.tensor_tensor(terms[:, slot, :, :, 0:HD],
                                    y4[:, n_, :, 0:HD].unsqueeze(2).to_broadcast([128, BL, 4, HD]),
                                    hist[:, n_, :, :].unsqueeze(1).to_broadcast([128, BL, 4, HD]),
                                    ALU.mult).then_inc(sem("b4_scan"), 1)
                    e.wait_ge(sem("b4_scan"), 3 * n_ + 1)
                    e.tensor_reduce(neg_delta[:, n_, :, :], terms[:, slot, :, :, :], AX.X,
                                    ALU.add).then_inc(sem("b4_scan"), 1)
                    e.wait_ge(sem("b4_scan"), 3 * n_ + 2)
                    e.tensor_tensor(rank1[:, n_ % 2, :, :, 0:BL],
                                    neg_delta[:, n_, :, :].rearrange("p l j -> p j l").unsqueeze(2).to_broadcast(
                                        [128, 4, HD, BL]),
                                    k4[:, n_, :, :].rearrange("p l d -> p d l").unsqueeze(1).to_broadcast(
                                        [128, 4, HD, BL]), ALU.mult).then_inc(sem("b4_scan"), 1)
                    e.wait_ge(sem("b4_scan"), 3 * n_ + 3)
                    e.wait_ge(sem("b4_carry"), n_ + 1)
                    e.tensor_reduce(hist[:, n_ + 1, :, :], rank1[:, n_ % 2, :, :, :], AX.X,
                                    ALU.add).then_inc(sem("b4_state"), 1)
                outputs(NCB - 2)
                link(e, outputs(NCB - 1))
                o4 = o_tok.rearrange("p (n i) j -> p n i j", i=BL)
                for s_ in range(BL):
                    link(e, e.tensor_tensor(o_tmp[:, :, s_:, :], neg_delta[:, :, :BL - s_, :],
                                            spread(qk_dot[:, s_], s_, BL, 4), ALU.mult))
                    link(e, e.tensor_tensor(o4[:, :, s_:, :], o4[:, :, s_:, :], o_tmp[:, :, s_:, :], ALU.subtract))
                e.tensor_tensor(o_tok, o_tok, per_d(r_q, 4), ALU.mult).then_inc(sem("b4_o"), 1)
                for b in range(B):
                    e.wait_ge(sem("b4_mix"), b + 1)
                    e.tensor_tensor(x_aux[:, b, :], ps[:, b, :], x_cur[:, b, :], ALU.add).then_inc(sem("b4_h"), 1)

            def b4_pool(e):
                k4, q4 = (x.rearrange("p (n i) d -> p n i d", i=BL) for x in (k_hat, q_raw))
                e.wait_ge(sem("b4_khat"), 1)
                for n_, s_ in enumerate((0, 2, 1, 3)):
                    if n_ >= 2:
                        e.wait_ge(sem("b4_qkred"), n_ - 1)
                    view = prod_q[n_ % 2][:, 0:NB * (BL - s_) * HD].rearrange("p (n i d) -> p n i d", n=NB, d=HD)
                    e.tensor_tensor(view, q4[:, :, s_:, :], k4[:, :, :BL - s_, :], ALU.mult).then_inc(sem("b4_qk"), 1)
                e.wait_ge(sem("b4_qk"), 4)
                e.tensor_tensor(q_raw, q_raw, per_d(gamma), ALU.mult).then_inc(sem("b4_qdecay"), 1)
                e.wait_ge(sem("b4_qdecay"), 1)

                def vset(ch):
                    if ch >= 2:
                        e.wait_ge(sem("b4_scan"), 3 * CB * (ch - 1))
                    for i in range(BL):
                        o = e.tensor_copy(terms[:, ch % 2 * CB:(ch % 2 + 1) * CB, i, :, HD],
                                          y[:, ch * CB * BL + i:(ch + 1) * CB * BL:BL, HD:12])
                    o.then_inc(sem("b4_vset"), 1)
                e.wait_ge(sem("b4_solved"), 1)
                vset(0)
                vset(1)
                for ch in range(NCB):
                    e.wait_ge(sem("b4_scan"), 3 * CB * ch + 3 * CB)
                    for i in range(BL):
                        o = e.tensor_tensor(prod_o[:, ch % 2, :, i, :, :],
                                            q4[:, ch * CB:(ch + 1) * CB, i, :].unsqueeze(2).to_broadcast([128, CB, 4, HD]),
                                            hist[:, ch * CB:(ch + 1) * CB, :, :], ALU.mult)
                    o.then_inc(sem("b4_qprod"), 1)
                    if ch + 2 < NCB:
                        vset(ch + 2)

            def b4_pe2(e):
                e.wait_ge(sem("b4_o"), 1)
                for b in range(B):
                    for j in range(4):
                        i = e.matmul(ps[:, b, :], wt["o_s"][:, (b * 4 + j) * 128:(b * 4 + j + 1) * 128],
                                     o_tok[:, :, j], start=(j == 0), stop=(j == 3))
                    i.then_inc(sem("b4_mix"), 1)
            pe_steps += [b4_pe, b4_pe2]
            act_steps.append(b4_act)
            dve_steps.append(b4_dve)
            pool_steps.append(b4_pool)

            c = Carve()
            hn = c(B * T).rearrange("p (b t) -> p b t", b=B)
            act4 = c(4 * T).rearrange("p (s t) -> p s t", s=4)
            n = make_norm([(x_aux[:, b, :], hn[:, b, :], T, b) for b in range(B)], counted("b4_h"), gain="norm2_w",
                          eps="eps6", mean=False)
            add_norm(n)

            def b4_total(e, b):
                link(e, e.tensor_tensor(x_aux[:, b, :], ps[:, 4 + b % 2, :], x_aux[:, b, :], ALU.add))
                return e.tensor_tensor(x_aux[:, b, :], x_aux[:, b, :], x_cur[:, b, :], ALU.add)
            gated("b4f", FC, FW, hn, [n.done(b) for b in range(B)],
                  lambda i: wt["wg"][:, i * FW:(i + 1) * FW], lambda i: wt["wu"][:, i * FW:(i + 1) * FW],
                  lambda i: wt["wd"][0:FW, i * 128:(i + 1) * 128], act4, extra={"total": b4_total})
            n = make_norm(batches(x_aux, x_cur), counted("b4f_sum"), other_table=True)
            add_norm(n)
            final = n

        if stages >= 5:
            c = Carve()
            qc = c(B * T).rearrange("p (b t) -> p b t", b=B)
            kc = c(B * S).rearrange("p (b s) -> p b s", b=B)
            kblk = c(B * H * S).rearrange("p (b h s) -> p b h s", b=B, h=H)
            vblk = c(B * 4 * 128).rearrange("p (b c n) -> p b c n", b=B, c=4)
            pc = c(4 * T).rearrange("p (a h s) -> p a h s", a=4, h=H)
            ptc = c(2 * 4 * T).rearrange("p (a c q) -> p a c q", a=2, c=4)
            oc = c(2 * T).rearrange("p (a t) -> p a t", a=2)
            st5 = c(3 * 4 * H).rearrange("p (k a h) -> p k a h", k=3, a=4)
            fin5 = final
            N5 = B * QB

            def b5_pe(e):
                e.wait_ge(sem("load_wE"), 16)
                e.wait_ge(*fin5.done(B - 1))
                for b in range(B):
                    e.matmul(ps[:, b, :], wt["c_Wq"], x_cur[:, b, :], start=True, stop=True).then_inc(sem("b5_proj"), 1)
                e.wait_ge(sem("load_ctx"), 16)
                e.matmul(ps[:, 4, 0:B * S], wt["c_Wk"], ctx_in[:, :], start=True, stop=True).then_inc(sem("b5_proj"), 1)
                for b in range(B):
                    for r in range(4):
                        i = e.matmul(ps[32 * r:32 * r + 32, 5, b * 128:b * 128 + 128], ctx_in[:, b * S:b * S + S],
                                     wt["c_Wv"], start=True, stop=True)
                i.then_inc(sem("b5_proj"), 1)
                e.wait_ge(sem("b5_blocks"), 1)

                def pv(b):
                    e.wait_ge(sem("b5_evac"), QB * (b + 1))
                    if b >= 2:
                        e.wait_ge(sem("b5_heads"), b - 1)
                    for k in range(4):
                        i = e.matmul(ps[:, 4 + b % 2, :], vblk[:, b, k, :], ptc[:, b % 2, k, :], start=(k == 0),
                                     stop=(k == 3))
                    i.then_inc(sem("b5_pv"), 1)

                def outp(b):
                    e.wait_ge(sem("b5_heads"), b + 1)
                    if b >= 2:
                        e.wait_ge(sem("b5_sum"), b - 1)
                    e.matmul(ps[:, 6 + b % 2, :], wt["c_Wo"], oc[:, b % 2, :], start=True,
                             stop=True).then_inc(sem("b5_out"), 1)
                for n_ in range(N5 + 6):
                    b, q = n_ // QB, n_ % QB
                    if n_ < N5:
                        if n_ >= 2:
                            e.wait_ge(sem("b5_shift"), n_ - 1)
                        e.matmul(ps[:, n_ % 2, :], qc[:, b, q * 128:q * 128 + 128], kblk[:, b, :, :], start=True,
                                 stop=True).then_inc(sem("b5_score"), 1)
                    if 2 <= n_ < N5 + 2:
                        m = n_ - 2
                        e.wait_ge(sem("b5_prob"), m + 1)
                        if m >= 2:
                            e.wait_ge(sem("b5_evac"), m - 1)
                        for k in range(4):
                            i = e.transpose(ps[:, 2 + m % 2, k * 128:k * 128 + 128], pc[:, m % 4, 4 * k:4 * k + 4, :],
                                            ident)
                        i.then_inc(sem("b5_turn"), 1)
                    if n_ >= 7 and (n_ - 7) % 4 == 0:
                        pv((n_ - 7) // 4)
                    if n_ >= 9 and (n_ - 9) % 4 == 0:
                        outp((n_ - 9) // 4)

            def b5_act(e):
                for n_ in range(N5 + 2):
                    if n_ < N5:
                        e.wait_ge(sem("b5_shift"), n_ + 1)
                        e.activation(pc[:, n_ % 4, :, :], pc[:, n_ % 4, :, :], ACT.Exp).then_inc(sem("b5_exp"), 1)
                    if n_ >= 2:
                        m = n_ - 2
                        b, q = m // QB, m % QB
                        e.wait_ge(sem("b5_turn"), m + 1)
                        if b >= 2 and q == 0:
                            e.wait_ge(sem("b5_pv"), b - 1)
                        e.copy(ptc[:, b % 2, :, q * 128:q * 128 + 128],
                               ps[:, 2 + m % 2, :].rearrange("p (k q) -> p k q", k=4)).then_inc(sem("b5_evac"), 1)

            def b5_dve(e):
                for b in range(B):
                    e.wait_ge(sem("b5_proj"), b + 1)
                    e.tensor_scalar(qc[:, b, :], ps[:, b, :], v("c_bq"), HD ** -0.5, ALU.add, ALU.mult)
                e.wait_ge(sem("b5_proj"), 5)
                link(e, e.tensor_scalar(kc, ps[:, 4, 0:B * S].rearrange("p (b s) -> p b s", b=B), v("c_bk"), None,
                                        ALU.add))
                e.wait_ge(sem("b5_proj"), 6)
                for b in range(B):
                    e.tensor_tensor(kblk[:, b, :, :], kc[:, b, :].unsqueeze(1).to_broadcast([128, H, S]),
                                    v("head_mask", 0, H).unsqueeze(2).to_broadcast([128, H, S]), ALU.mult)
                    i = e.tensor_tensor(vblk[:, b, :, :],
                                        ps[:, 5, b * 128:b * 128 + 128].unsqueeze(1).to_broadcast([128, 4, 128]),
                                        wt["v_mask"].rearrange("p (c n) -> p c n", c=4), ALU.mult)
                i.then_inc(sem("b5_blocks"), 1)

                def heads(b):
                    e.wait_ge(sem("b5_pv"), b + 1)
                    if b >= 2:
                        e.wait_ge(sem("b5_out"), b - 1)
                    e.tensor_scalar(oc[:, b % 2, :], ps[:, 4 + b % 2, :], v("c_bv"), None,
                                    ALU.add).then_inc(sem("b5_heads"), 1)

                def total(b):
                    e.wait_ge(sem("b5_out"), b + 1)
                    e.scalar_tensor_tensor(out=x_aux[:, b, :], in0=ps[:, 6 + b % 2, :], scalar=v("c_bo"),
                                           in1=x_cur[:, b, :], op0=ALU.add, op1=ALU.add).then_inc(sem("b5_sum"), 1)
                hs = lambda x: x.unsqueeze(2).to_broadcast([128, H, S])
                for n_ in range(N5 + 7):
                    if n_ < N5:
                        a = n_ % 4
                        score = ps[:, n_ % 2, :].rearrange("p (h s) -> p h s", h=H)
                        e.wait_ge(sem("b5_score"), n_ + 1)
                        link(e, e.tensor_reduce(st5[:, 0, a, :], score, AX.X, ALU.max))
                        if n_ >= 4:
                            e.wait_ge(sem("b5_turn"), n_ - 3)
                        e.tensor_tensor(pc[:, a, :, :], score, hs(st5[:, 0, a, :]),
                                        ALU.subtract).then_inc(sem("b5_shift"), 1)
                    if 1 <= n_ <= N5:
                        m, a = n_ - 1, (n_ - 1) % 4
                        e.wait_ge(sem("b5_exp"), m + 1)
                        link(e, e.tensor_reduce(st5[:, 1, a, :], pc[:, a, :, :], AX.X, ALU.add))
                        link(e, e.reciprocal(st5[:, 2, a, :], st5[:, 1, a, :]))
                        e.tensor_tensor(pc[:, a, :, :], pc[:, a, :, :], hs(st5[:, 2, a, :]),
                                        ALU.mult).then_inc(sem("b5_prob"), 1)
                    if n_ >= 8 and (n_ - 8) % 4 == 0:
                        heads((n_ - 8) // 4)
                    if n_ >= 10 and (n_ - 10) % 4 == 0:
                        total((n_ - 10) // 4)
            pe_steps.append(b5_pe)
            act_steps.append(b5_act)
            dve_steps.append(b5_dve)
            n = make_norm(batches(x_aux, x_cur), counted("b5_sum"))
            add_norm(n)
            final = n

        if stages >= 6:
            n6 = make_norm(batches(x_cur, x_aux), [final.done(b) for b in range(B)], gain="m_ln1_w", mean=False)
            add_norm(n6)
            b6_res = narrow(x_aux, [n6.done(b) for b in range(B)], x_aux, "b6", "wF", "m_q", "m_k", "m_v", "m_wo",
                            rope=("m_qr", "m_kr"))
            c = Carve()
            hn6 = c(B * T).rearrange("p (b t) -> p b t", b=B)
            n7 = make_norm(batches(x_aux, hn6), b6_res, gain="m_ln2_w", mean=False)
            add_norm(n7)
            wide_w = c(2 * E1 * T).rearrange("p (a e t) -> p a e t", a=2, e=E1)
            act6 = c(4 * T).rearrange("p (s t) -> p s t", s=4)
            w_pad = c(QB * 128).rearrange("p (q n) -> p q n", q=QB)
            w_T = c(T)
            r8 = [c(QB * E1).rearrange("p (q e) -> p q e", q=QB) for _ in range(6)]
            r1 = [c(QB) for _ in range(8)]
            sel = wt["sel"].rearrange("p (e n) -> p e n", e=E1)
            rank = v("tie_rank", 0, QB * E1).rearrange("p (q e) -> p q e", q=QB)

            def r_logit(e, b):
                if b:
                    e.wait_ge(sem("r_wide"), 8 * b)
                for q in range(QB):
                    i = e.matmul(ps[:, 6, q * E1:q * E1 + E1], hn6[:, b, q * 128:q * 128 + 128], wt["m_gate"],
                                 start=True, stop=True)
                i.then_inc(sem("r_logit"), 1)

            def r_turn(e, b):
                e.wait_ge(sem("r_weights"), b + 1)
                for q in range(QB):
                    i = e.transpose(ps[:, 7, q * 128:q * 128 + 128], w_pad[:, q, :], ident)
                i.then_inc(sem("r_turn"), 1)

            def r_spread(e, b, ex):
                n_ = b * E1 + ex
                e.wait_ge(sem("r_turned"), b + 1)
                if ex >= 2:
                    e.wait_ge(sem("r_wide"), n_ - 1)
                e.matmul(ps[:, 6 + ex % 2, :], sel[:, ex, :], w_T, start=True, stop=True).then_inc(sem("r_spread"), 1)

            def r_exp(e, b):
                e.wait_ge(sem("r_shift"), b + 1)
                e.activation(r8[0], r8[0], ACT.Exp).then_inc(sem("r_exp"), 1)

            def r_wide(e, b, ex):
                n_ = b * E1 + ex
                e.wait_ge(sem("r_spread"), n_ + 1)
                if b >= 2 and ex == 0:
                    e.wait_ge(sem("b6f_gated"), (b - 1) * E1 * C1)
                e.copy(wide_w[:, b % 2, ex, :], ps[:, 6 + ex % 2, :]).then_inc(sem("r_wide"), 1)

            def top2_a(e, b):
                pr = r8[0]
                lg = ps[:, 6, 0:QB * E1].rearrange("p (q e) -> p q e", q=QB)
                bc = lambda x: x.unsqueeze(2).to_broadcast([128, QB, E1])
                e.wait_ge(sem("r_logit"), b + 1)
                link(e, e.tensor_reduce(r1[0], lg, AX.X, ALU.max))
                e.tensor_tensor(pr, lg, bc(r1[0]), ALU.subtract).then_inc(sem("r_shift"), 1)

            def top2_b(e, b):
                pr, eq, sel1, p2, sel2, both = r8
                bc = lambda x: x.unsqueeze(2).to_broadcast([128, QB, E1])
                e.wait_ge(sem("r_exp"), b + 1)
                link(e, e.tensor_reduce(r1[1], pr, AX.X, ALU.add))
                link(e, e.reciprocal(r1[2], r1[1]))
                link(e, e.tensor_tensor(pr, pr, bc(r1[2]), ALU.mult))
                link(e, e.tensor_reduce(r1[3], pr, AX.X, ALU.max))
                link(e, e.tensor_tensor(eq, pr, bc(r1[3]), ALU.is_equal))
                link(e, e.tensor_tensor(eq, eq, rank, ALU.mult))
                link(e, e.tensor_reduce(r1[4], eq, AX.X, ALU.max))
                link(e, e.tensor_tensor(sel1, eq, bc(r1[4]), ALU.is_equal))
                link(e, e.scalar_tensor_tensor(out=p2, in0=sel1, scalar=-2.0, in1=pr, op0=ALU.mult, op1=ALU.add))
                link(e, e.tensor_reduce(r1[5], p2, AX.X, ALU.max))
                link(e, e.tensor_tensor(eq, p2, bc(r1[5]), ALU.is_equal))
                link(e, e.tensor_tensor(eq, eq, rank, ALU.mult))
                link(e, e.tensor_reduce(r1[6], eq, AX.X, ALU.max))
                link(e, e.tensor_tensor(sel2, eq, bc(r1[6]), ALU.is_equal))
                link(e, e.tensor_tensor(r1[7], r1[3], r1[5], ALU.add))
                link(e, e.reciprocal(r1[7], r1[7]))
                link(e, e.tensor_tensor(both, sel1, sel2, ALU.add))
                link(e, e.tensor_tensor(both, both, pr, ALU.mult))
                if b:
                    e.wait_ge(sem("r_turn"), b)
                e.tensor_tensor(w_pad[:, :, 0:E1], both, bc(r1[7]), ALU.mult).then_inc(sem("r_weights"), 1)

            def r_turned(e, b):
                e.wait_ge(sem("r_turn"), b + 1)
                if b:
                    e.wait_ge(sem("r_spread"), E1 * b)
                e.tensor_copy(w_T, ps[:, 7, :]).then_inc(sem("r_turned"), 1)

            def pe_extra(e, b, i):
                if b + 1 < B:
                    if i == 1:
                        r_logit(e, b + 1)
                    if i == 5:
                        r_turn(e, b + 1)
                    if 8 <= i < 16:
                        r_spread(e, b + 1, i - 8)

            def act_extra(e, b, i):
                if b + 1 < B:
                    if i == 1:
                        r_exp(e, b + 1)
                    if 8 <= i < 16:
                        r_wide(e, b + 1, i - 8)

            def dve_extra(e, b, i):
                if b + 1 < B:
                    if i == 1:
                        top2_a(e, b + 1)
                    if i == 2:
                        top2_b(e, b + 1)
                    if i == 6:
                        r_turned(e, b + 1)

            def b6_total(e, b):
                link(e, e.tensor_tensor(x_aux[:, b, :], ps[:, 4 + b % 2, :], x_aux[:, b, :], ALU.add))
                return e.tensor_tensor(x_aux[:, b, :], x_aux[:, b, :], x_cur[:, b, :], ALU.add)

            def first_pe(e):
                r_logit(e, 0)
                r_turn(e, 0)
                for ex in range(E1):
                    r_spread(e, 0, ex)

            def first_act(e):
                r_exp(e, 0)
                for ex in range(E1):
                    r_wide(e, 0, ex)

            def first_dve(e):
                e.memset(w_pad, 0.0)
                top2_a(e, 0)
                top2_b(e, 0)
                r_turned(e, 0)
            w13, w2 = wt["w13"], wt["w2"]

            def w13_of(i, half):
                ex, k = i // C1, i % C1
                at_ = ex * 512 + half * 256 + k * 128
                return w13[:, at_:at_ + 128]
            gated("b6f", E1 * C1, 128, hn6, [n7.done(b) for b in range(B)], lambda i: w13_of(i, 0),
                  lambda i: w13_of(i, 1), lambda i: w2[:, i * 128:(i + 1) * 128], act6, load="wM1",
                  weight=lambda b, i: wide_w[:, b % 2, i // C1, :], weight_ready=lambda b: (sem("r_wide"), E1 * (b + 1)),
                  extra={"pe": pe_extra, "act": act_extra, "dve": dve_extra, "total": b6_total,
                         "pe_first": [first_pe], "act_first": [first_act], "dve_first": [first_dve]})
            n = make_norm(batches(x_aux, x_cur), counted("b6f_sum"), other_table=True)
            add_norm(n)
            final = n

        def store(e):
            for b in range(B):
                e.wait_ge(*final.done(b))
                e.dma_start(out[:, b, :], x_cur[:, b, :]).then_inc(sem("stored"), 16)
            e.wait_ge(sem("stored"), 16 * B)
        sp_steps.append(store)

        block = ctx.enter_context(nc.Block())

        @block.sync
        def _(eng):
            for step in sp_steps:
                step(eng)

        @block.tensor
        def _(eng):
            for step in pe_steps:
                step(eng)

        @block.scalar
        def _(eng):
            for step in act_steps:
                step(eng)

        @block.vector
        def _(eng):
            for step in dve_steps:
                step(eng)

        @block.gpsimd
        def _(eng):
            for step in pool_steps:
                step(eng)


def feature_major(a):
    return np.ascontiguousarray(np.transpose(a, (2, 0, 1)))


def spread_rows(w):
    n = w.shape[1]
    out = np.zeros((4, 32, 4, n), w.dtype)
    out[:, :8] = np.transpose(w.reshape(4, 4, 8, n), (1, 2, 0, 3))
    return out.reshape(128, 4 * n)


def by_dim(w, axis):
    parts = w.shape[:axis] + (H, HD) + w.shape[axis + 1:]
    return np.ascontiguousarray(np.swapaxes(w.reshape(parts), axis, axis + 1)).reshape(w.shape)


def layouts(i):
    f = np.float32
    one = lambda a: np.asarray(a).reshape(-1, 1)
    vec = {
        "gate_w": i["L0_attn_gate_w"].reshape(D, 7), "cand_w": i["L0_attn_cand_w"].reshape(D, 7),
        "gate_b": one(i["L0_attn_gate_b"]), "cand_b": one(i["L0_attn_cand_b"]),
        "log_decay": one(i["L0_attn_log_decay"]), "out_b": one(i["L0_attn_out_b"]),
        "norm_w": one(i["L0_attn_norm_w"]),
        "x_ln1_g": one(i["L0_xattn_ln1_g"]), "x_ln1_b": one(i["L0_xattn_ln1_b"]),
        "x_ln2_g": one(i["L0_xattn_ln2_g"]), "x_ln2_b": one(i["L0_xattn_ln2_b"]),
        "f_bq": by_dim(one(i["L0_ffn_bq"]), 0), "f_bk": by_dim(one(i["L0_ffn_bk"]), 0),
        "f_bo": one(i["L0_ffn_bo"]), "router_b": np.repeat(one(i["L0_ffn_router_b"]), 128, 0),
        "f_b1": np.transpose(i["L0_ffn_b1"].reshape(16, 128)), "f_b2": np.transpose(i["L0_ffn_b2"]),
        "f_ln1_g": one(i["L0_ffn_ln1_g"]), "f_ln1_b": one(i["L0_ffn_ln1_b"]),
        "f_ln2_g": one(i["L0_ffn_ln2_g"]), "f_ln2_b": one(i["L0_ffn_ln2_b"]),
        "norm1_w": one(i["L1_attn_norm1_w"]), "norm2_w": one(i["L1_attn_norm2_w"]),
        "conv_w": i["L1_attn_conv_w"], "conv_b": one(i["L1_attn_conv_b"]),
        "c_bq": one(i["L1_xattn_bq"]), "c_bk": one(i["L1_xattn_bk"]), "c_bv": one(i["L1_xattn_bv"]),
        "c_bo": one(i["L1_xattn_bo"]), "m_ln1_w": one(i["L1_ffn_ln1_w"]), "m_ln2_w": one(i["L1_ffn_ln2_w"]),
        "eps_attn": np.full((128, 1), 1.1920929e-07, f), "eps5": np.full((128, 1), 1e-5, f),
        "eps6": np.full((128, 1), 1e-6, f), "four": np.full((128, 1), 4.0, f),
        "head_mask": np.repeat(np.eye(H, dtype=f), HD, 0),
        "sum_pick": (np.arange(128)[:, None] == 32 * np.arange(4)[None, :] + HD).astype(f),
        "tie_rank": np.tile(np.arange(E1, 0, -1).astype(f), (128, 4)),
    }
    for n, (_, w) in VEC.items():
        assert vec[n].shape == (128, w), (n, vec[n].shape)
    tr = np.transpose
    qkv = i["L1_ffn_wqkv"]
    group = np.repeat(np.arange(4), 4)
    mk = qkv[128:160].reshape(4, 8, 128)[group].reshape(128, 128)
    mv = qkv[160:192].reshape(4, 8, 128)[group].reshape(128, 128)
    swap = lambda w: w.reshape(16, 2, 4, 128)[:, ::-1].reshape(128, 128)
    inv = (1.0 / f(10000.0) ** (np.arange(0, HD, 2, dtype=f) / f(HD))).astype(f)
    ang = np.arange(T, dtype=f)[:, None] * inv[None, :]
    cos, sin = np.cos(ang).astype(f), np.sin(ang).astype(f)
    cosT = np.tile(np.concatenate([cos, cos], 1).T, (16, 1))
    sinT = np.tile(np.concatenate([-sin, sin], 1).T, (16, 1))
    ws = i["L1_attn_wq"], i["L1_attn_wk"]
    dhv = lambda w: np.repeat(tr(w.reshape(128, 16, 8), (0, 2, 1)), 2, 2).reshape(128, 256)
    o_s = np.zeros((4, 16, 2, 4, 4, 128), f)
    for b in range(4):
        o_s[b, :, :, b] = i["L1_attn_wo"].reshape(16, 2, 4, 128)
    wd = np.zeros((128, 3, 128), f)
    wd[:FW] = tr(i["L1_attn_wd"].reshape(3, FW, 128), (1, 0, 2))
    vm = (np.arange(128)[:, None, None] // 32 + 4 * np.arange(4)[None, :, None]
          == np.arange(128)[None, None, :] // 8).astype(f).reshape(128, 512)
    causal = np.where(np.arange(128)[None, :] > np.arange(128)[:, None], f(NEG), f(0))
    sel = np.zeros((128, 8, 128), f)
    for ex in range(8):
        sel[ex, ex] = 1.0
    mats = {
        "out_w": tr(i["L0_attn_out_w"]), "ident": np.eye(128, dtype=f), "ones": np.full((128, 128), 1.0 / D, f),
        "Wq": i["L0_xattn_Wq"], "Wkv": i["L0_xattn_Wkv"],
        "Wo": tr(i["L0_xattn_Wo"].reshape(8, 128, 128), (1, 0, 2)).reshape(128, 1024),
        "f_Wq": by_dim(i["L0_ffn_Wq"], 1), "f_Wk": by_dim(i["L0_ffn_Wk"], 1), "f_Wv": i["L0_ffn_Wv"],
        "f_bv": np.repeat(i["L0_ffn_bv"].reshape(1, 128), 128, 0),
        "f_Wo": spread_rows(i["L0_ffn_Wo"]), "router": np.repeat(i["L0_ffn_router_w"], 128, 1),
        "W1": tr(i["L0_ffn_W1"], (1, 0, 2)).reshape(128, 2048),
        "W2": tr(i["L0_ffn_W2"].reshape(16, 128, 128), (1, 0, 2)).reshape(128, 2048),
        "q_s": dhv(ws[0]), "k_s": dhv(ws[1]),
        "v_s": tr(i["L1_attn_wv"].reshape(128, 32, 4), (0, 2, 1)).reshape(128, 128),
        "b_s": np.repeat(i["L1_attn_wb"], 2, 1), "a_s": np.repeat(i["L1_attn_wa"], 2, 1),
        "o_s": o_s.reshape(128, 2048), "wg": i["L1_attn_wg"], "wu": i["L1_attn_wu"], "wd": wd.reshape(128, 384),
        "c_Wq": tr(i["L1_xattn_Wq"]), "c_Wk": tr(i["L1_xattn_Wk"]), "c_Wv": tr(i["L1_xattn_Wv"]),
        "c_Wo": tr(i["L1_xattn_Wo"]), "v_mask": vm,
        "m_q": by_dim(tr(qkv[:128]), 1), "m_qr": by_dim(tr(swap(qkv[:128])), 1), "m_k": by_dim(tr(mk), 1),
        "m_kr": by_dim(tr(swap(mk)), 1), "m_v": tr(mv), "m_wo": spread_rows(tr(i["L1_ffn_wo"])), "m_gate": tr(i["L1_ffn_gate_w"]),
        "cos": by_dim(cosT, 0), "sin": by_dim(sinT, 0), "causal": causal, "sel": sel.reshape(128, 1024),
        "w13": tr(i["L1_ffn_w13"], (2, 0, 1)).reshape(128, 4096),
        "w2": tr(i["L1_ffn_w2"].reshape(8, 128, 2, 128), (3, 0, 2, 1)).reshape(128, 2048),
    }
    arrays = {"xT": feature_major(i["x"]), "ctxT": feature_major(i["ctx_1024"]).reshape(128, B * S),
              "vecs": np.concatenate([vec[n] for n in VEC], 1)}
    for g, cols in GROUPS.items():
        for n, w in cols:
            assert mats[n].shape == (128, w), (n, mats[n].shape)
        arrays[g] = np.concatenate([mats[n] for n, _ in cols], 1)
    return {k: np.ascontiguousarray(a) for k, a in arrays.items()}


def kernel(**inputs):
    import concourse.bacc as _bacc
    from concourse.bass_utils import run_bass_kernel_spmd as _run

    arrays = layouts(inputs)
    nc = _bacc.Bacc("TRN2", target_bir_lowering=False, num_devices=1)
    aps = {k: nc.dram_tensor(k + "_dram", a.shape, F32, kind="ExternalInput").ap() for k, a in arrays.items()}
    out = nc.dram_tensor("out_dram", (128, B, T), F32, kind="ExternalOutput").ap()
    program(nc, aps["xT"], aps["ctxT"], aps["vecs"], {g: aps[g] for g in GROUPS}, out)
    r = _run(nc, [{k + "_dram": a for k, a in arrays.items()}], core_ids=[0])
    return np.ascontiguousarray(np.transpose(r.results[0]["out_dram"], (1, 2, 0)))
```

```python
from contextlib import ExitStack

import numpy as np
import concourse.bass as bass
from concourse import mybir

ALU = mybir.AluOpType
ACT = mybir.ActivationFunctionType
AX = mybir.AxisListType
F32 = mybir.dt.float32
I32 = mybir.dt.int32
BF16 = mybir.dt.bfloat16

B, T, D = 4, 512, 128
H, HD = 16, 8
XH, XD = 16, 64
S = 32
KEYS = T + S
QB = T // 128
UNITS = H * QB
E0, C0 = 4, 4
E1, C1 = 8, 2
FI, FC = 345, 3
FW = FI // FC
TAPS, CTAPS = 7, 4
PV_AT = 7
BL = 4
NB = T // BL
CB = 16
NCB = NB // CB
QK_OPS = 19
OUT_OPS = 5 + 2 * BL
NEG = -1.0e30
TURN_AT = 3
PV_PARTS = ((), (), (), (), (), (0,), (1, 2), (3, 4))
QK_AT = (1, 3)

VEC = {}
for _n, _w in (("gate_w", 7), ("cand_w", 7), ("gate_b", 1), ("cand_b", 1), ("log_decay", 1), ("out_b", 1),
               ("norm_w", 1), ("x_ln1_g", 1), ("x_ln1_b", 1), ("x_ln2_g", 1), ("x_ln2_b", 1), ("f_bq", 1),
               ("f_bk", 1), ("f_bo", 1), ("router_b", 1), ("f_b1", 16), ("f_b2", 4), ("f_ln1_g", 1),
               ("f_ln1_b", 1), ("f_ln2_g", 1), ("f_ln2_b", 1), ("norm1_w", 1), ("norm2_w", 1), ("conv_w", 4),
               ("conv_b", 1), ("c_bq", 1), ("c_bk", 1), ("c_bv", 1), ("c_bo", 1), ("m_ln1_w", 1), ("m_ln2_w", 1),
               ("eps_attn", 1), ("eps5", 1), ("eps6", 1), ("four", 1), ("head_mask", 16), ("sum_pick", 4), ("tie_rank", 32)):
    VEC[_n] = (sum(w for _, w in VEC.values()), _w)
NVEC = sum(w for _, w in VEC.values())

GROUPS = {
    "wA": (("out_w", 128), ("ident", 128), ("ones", 128)),
    "wB": (("Wq", 1024), ("Wkv", 2048), ("Wo", 1024)),
    "wC": (("f_Wq", 128), ("f_Wk", 128), ("f_Wv", 128), ("f_bv", 128), ("f_Wo", 512), ("router", 128)),
    "wM0": (("W1", 2048), ("W2", 2048)),
    "wD": (("q_s", 256), ("k_s", 256), ("v_s", 128), ("b_s", 32), ("a_s", 32), ("o_s", 2048), ("wg", FI),
           ("wu", FI), ("wd", 384)),
    "wE": (("c_Wq", 128), ("c_Wk", 128), ("c_Wv", 128), ("c_Wo", 128), ("v_mask", 512)),
    "wF": (("m_q", 128), ("m_qr", 128), ("m_k", 128), ("m_kr", 128), ("m_v", 128), ("m_wo", 512), ("m_gate", 8),
           ("cos", 512), ("sin", 512), ("causal", 128), ("sel", 1024)),
    "wM1": (("w13", 4096), ("w2", 2048)),
}


def program(nc, xT, ctxT, vecs, groups, out, stages=6):
    ctx = ExitStack()
    with ctx:
        def sb(name, cols, dt=F32):
            return ctx.enter_context(nc.sbuf_tensor(name, [128, cols], dt))

        sem_of = {}

        def sem(name):
            if name not in sem_of:
                sem_of[name] = ctx.enter_context(nc.semaphore(name))
            return sem_of[name]

        vec = sb("vec", NVEC)
        x_cur = sb("x_cur", B * T).rearrange("p (b t) -> p b t", b=B)
        x_aux = sb("x_aux", B * T).rearrange("p (b t) -> p b t", b=B)
        cent = sb("cent", B * T).rearrange("p (b t) -> p b t", b=B)
        dev = sb("dev", B * T).rearrange("p (b t) -> p b t", b=B)
        ctx_in = sb("ctx_in", B * S)
        ctx_ln = sb("ctx_ln", B * S)
        stat = sb("stat", 64)
        width = {g: sum(w for _, w in cols) for g, cols in GROUPS.items()}
        reg1 = sb("reg1", max(width["wB"], width["wD"]))
        reg2 = sb("reg2", max(width["wM0"], width["wM1"]))
        place = {"wB": reg1, "wD": reg1, "wM0": reg2, "wM1": reg2}
        for g in ("wA", "wC", "wE", "wF"):
            place[g] = sb(g + "_sb", width[g])
        wt = {}
        for g, cols in GROUPS.items():
            at = 0
            for n, w in cols:
                wt[n] = place[g][:, at:at + w]
                at += w
        wt_bf = sb("wt_bf", 256, BF16)
        arena_cols = 28160
        arena = sb("arena", arena_cols)
        ps = ctx.enter_context(nc.psum_tensor("ps", [128, 8, 512], F32))

        def v(name, i=0, n=1):
            c = VEC[name][0] + i
            return vec[:, c:c + n]

        class Carve:
            def __init__(self):
                self.at = 0

            def __call__(self, cols):
                a = arena[:, self.at:self.at + cols]
                self.at += cols
                assert self.at <= arena_cols, self.at
                return a

        ident, ones = wt["ident"], wt["ones"]

        class Norm:
            count = 0

            def __init__(self, chunks, ready, gain=None, bias=None, eps="eps5", mean=True,
                         other_table=False):
                self.other_table = other_table
                self.chunks, self.ready, self.gain, self.bias, self.eps, self.mean = chunks, ready, gain, bias, eps, mean
                self.first = Norm.count
                Norm.count += len(chunks)

            def tmp(self, buf, n):
                _, _, w, slot = self.chunks[n]
                return buf[:, slot, 0:w]

            def pe(self, e):
                def mean(n):
                    src, _, w, slot = self.chunks[n]
                    e.wait_ge(*self.ready[n])
                    if self.first >= 1:
                        e.wait_ge(sem("norm_done"), self.first)
                    e.matmul(ps[:, slot, 0:w], ones, src, start=True, stop=True).then_inc(sem("norm_mean"), 1)

                def var(n):
                    src, _, w, slot = self.chunks[n]
                    if not self.mean and self.first >= 1:
                        e.wait_ge(sem("norm_done"), self.first)
                    e.wait_ge(sem("norm_sq"), self.first + n + 1)
                    e.matmul(ps[:, 4 + slot, 0:w], ones, self.tmp(dev, n), start=True,
                             stop=True).then_inc(sem("norm_var"), 1)
                N = len(self.chunks)
                for n in range(N + 2):
                    if self.mean and n < N:
                        mean(n)
                    if n >= 2:
                        var(n - 2)

            def act(self, e):
                if self.other_table:
                    e.preload_act_table_set("natural_log_exp_and_others")
                for n, (src, _, w, slot) in enumerate(self.chunks):
                    e.wait_ge(sem("norm_var"), self.first + n + 1)
                    e.activation(self.tmp(dev, n), ps[:, 4 + slot, 0:w], ACT.Ln,
                                 bias=v(self.eps)).then_inc(sem("norm_ln"), 1)
                    e.wait_ge(sem("norm_ln"), self.first + n + 1)
                    e.activation(self.tmp(dev, n), self.tmp(dev, n), ACT.Exp, scale=-0.5).then_inc(sem("norm_dev"), 1)

            def dve(self, e):
                self.dve_squares(e)
                self.dve_scale(e)

            def dve_squares(self, e):
                for n, (src, dst, w, slot) in enumerate(self.chunks):
                    c = src
                    if self.mean:
                        c = self.tmp(cent, n)
                        e.wait_ge(sem("norm_mean"), self.first_mean + n + 1)
                        e.tensor_tensor(c, src, ps[:, slot, 0:w], ALU.subtract).then_inc(sem("norm_cent"), 1)
                        e.wait_ge(sem("norm_cent"), self.first_mean + n + 1)
                    else:
                        e.wait_ge(*self.ready[n])
                    if self.first:
                        e.wait_ge(sem("norm_done"), self.first)
                    e.tensor_tensor(self.tmp(dev, n), c, c, ALU.mult).then_inc(sem("norm_sq"), 1)

            def dve_scale(self, e):
                for n, (src, dst, w, slot) in enumerate(self.chunks):
                    c = self.tmp(cent, n) if self.mean else src
                    e.wait_ge(sem("norm_dev"), self.first + n + 1)
                    if self.gain is None:
                        e.tensor_tensor(dst, c, self.tmp(dev, n), ALU.mult).then_inc(sem("norm_done"), 1)
                    elif self.bias is None:
                        e.scalar_tensor_tensor(out=dst, in0=c, scalar=v(self.gain), in1=self.tmp(dev, n),
                                               op0=ALU.mult, op1=ALU.mult).then_inc(sem("norm_done"), 1)
                    else:
                        e.scalar_tensor_tensor(out=self.tmp(cent, n), in0=c, scalar=v(self.gain),
                                               in1=self.tmp(dev, n), op0=ALU.mult,
                                               op1=ALU.mult).then_inc(sem("norm_scaled"), 1)
                        e.wait_ge(sem("norm_scaled"), self.scaled + n + 1)
                        e.tensor_scalar(dst, self.tmp(cent, n), v(self.bias), None,
                                        ALU.add).then_inc(sem("norm_done"), 1)

            def done(self, n):
                return sem("norm_done"), self.first + n + 1

        mean_count, scaled_count = [0], [0]

        def make_norm(*a, **k):
            n = Norm(*a, **k)
            n.first_mean, n.scaled = mean_count[0], scaled_count[0]
            if n.mean:
                mean_count[0] += len(n.chunks)
            if n.bias is not None:
                scaled_count[0] += len(n.chunks)
            return n

        def batches(src, dst):
            return [(src[:, b, :], dst[:, b, :], T, b) for b in range(B)]

        def counted(name, base=0, step=1):
            return [(sem(name), base + step * (b + 1)) for b in range(B)]

        pe_steps, act_steps, dve_steps, pool_steps, sp_steps = [], [], [], [], []
        final = None

        def add_norm(n):
            pe_steps.append(n.pe)
            act_steps.append(n.act)
            dve_steps.append(n.dve)

        link_count = [0]

        def link(e, ins):
            link_count[0] += 1
            ins.then_inc(sem("dve_link"), 1)
            e.wait_ge(sem("dve_link"), link_count[0])

        def load_first(e):
            for g in ("wB", "wC", "wM0", "wE", "wF"):
                e.dma_start(place[g][:, 0:width[g]], groups[g]).then_inc(sem("load_" + g), 16)
        P = TAPS // 2
        cv = Carve()
        x_pad = cv(B * (T + 2 * P)).rearrange("p (b t) -> p b t", b=B)
        gate = cv(B * T).rearrange("p (b t) -> p b t", b=B)
        cand = cv(B * T).rearrange("p (b t) -> p b t", b=B)
        hid = cv(B * T).rearrange("p (b t) -> p b t", b=B)
        y1 = cv(B * T).rearrange("p (b t) -> p b t", b=B)
        decay = stat[:, 63:64]
        diag = cv(TAPS * D).rearrange("p (k n) -> p k n", k=TAPS)
        PB = B - 1

        def load_x(e):
            e.dma_start(vec[:, :], vecs).then_inc(sem("load_vec"), 16)
            e.dma_start(place["wA"][:, :], groups["wA"]).then_inc(sem("load_wA"), 16)
            e.dma_start(x_pad[:, :, P:P + T], xT).then_inc(sem("load_xpad"), 16)
            e.dma_start(x_cur[:, :, :], xT).then_inc(sem("load_x"), 16)
            e.dma_start(ctx_in[:, :], ctxT).then_inc(sem("load_ctx"), 16)
        sp_steps += [load_x, load_first]

        n_ctx = make_norm([(ctx_in[:, :], ctx_ln[:, :], B * S, 3)], [(sem("load_ctx"), 16)], gain="x_ln1_g",
                          bias="x_ln1_b", other_table=True)

        def b1_dve(e):
            e.memset(x_pad[:, :, 0:P], 0.0)
            e.memset(x_pad[:, :, P + T:], 0.0).then_inc(sem("b1_pad"), 1)
            e.wait_ge(sem("b1_pad"), 1)
            e.wait_ge(sem("load_vec"), 16)
            e.wait_ge(sem("load_xpad"), 16)
            for n, (acc, w, b0) in enumerate(((cand, "cand_w", 0), (gate, "gate_w", PB))):
                for k in range(TAPS):
                    src = x_pad[:, b0:, k:k + T]
                    if k == 0:
                        e.tensor_scalar(acc[:, b0:, :], src, v(w, k), None, ALU.mult).then_inc(sem(f"tap{n}"), 1)
                    else:
                        e.wait_ge(sem(f"tap{n}"), k)
                        e.scalar_tensor_tensor(out=acc[:, b0:, :], in0=src, scalar=v(w, k), in1=acc[:, b0:, :],
                                               op0=ALU.mult, op1=ALU.add).then_inc(sem(f"tap{n}"), 1)
            n_ctx.dve_squares(e)
            e.wait_ge(sem("load_x"), 16)
            for b in range(B):
                e.wait_ge(sem("b1_cand"), b + 1)
                link(e, e.tensor_tensor(gate[:, b, :], gate[:, b, :], cand[:, b, :], ALU.mult))
                e.wait_ge(sem("b1_decay"), 1)
                e.tensor_tensor_scan(hid[:, b, :], decay.to_broadcast([128, T]), gate[:, b, :], 0.0, ALU.mult,
                                     ALU.add).then_inc(sem("b1_scan"), 1)
            for b in range(B):
                e.wait_ge(sem("b1_proj"), b + 1)
                e.scalar_tensor_tensor(out=y1[:, b, :], in0=ps[:, b, :], scalar=v("out_b"), in1=x_cur[:, b, :],
                                       op0=ALU.add, op1=ALU.add).then_inc(sem("b1_y"), 1)
            n_ctx.dve_scale(e)

        def b1_act(e):
            e.wait_ge(sem("load_vec"), 16)
            e.activation(decay, v("log_decay"), ACT.Exp).then_inc(sem("b1_decay"), 1)
            for b in range(B):
                if b < PB:
                    e.wait_ge(sem("b1_gate"), b + 1)
                    e.activation(gate[:, b, :], ps[:, 4 + b, :], ACT.Sigmoid, bias=v("gate_b"))
                else:
                    e.wait_ge(sem("tap1"), TAPS)
                    e.activation(gate[:, b, :], gate[:, b, :], ACT.Sigmoid, bias=v("gate_b"))
                e.wait_ge(sem("tap0"), TAPS)
                e.activation(cand[:, b, :], cand[:, b, :], ACT.Tanh, bias=v("cand_b")).then_inc(sem("b1_cand"), 1)
            n_ctx.act(e)

        def b1_pool(e):
            e.wait_ge(sem("load_vec"), 16)
            e.wait_ge(sem("load_wA"), 16)
            for k in range(TAPS):
                e.tensor_scalar(diag[:, k, :], ident, v("gate_w", k), 1.0, ALU.mult, ALU.mult).then_inc(sem("b1_diag"), 1)

        def b1_pe(e):
            e.wait_ge(sem("load_wA"), 16)
            e.wait_ge(sem("load_xpad"), 16)
            e.wait_ge(sem("b1_pad"), 1)
            for b in range(PB):
                for k in range(TAPS):
                    if b == 0:
                        e.wait_ge(sem("b1_diag"), k + 1)
                    i = e.matmul(ps[:, 4 + b, :], diag[:, k, :], x_pad[:, b, k:k + T], start=(k == 0),
                                 stop=(k == TAPS - 1))
                i.then_inc(sem("b1_gate"), 1)
            n_ctx.pe(e)
            for b in range(B):
                e.wait_ge(sem("b1_scan"), b + 1)
                if b == B - 1:
                    e.wait_ge(sem("norm_cent"), 1)
                e.matmul(ps[:, b, :], wt["out_w"], hid[:, b, :], start=True, stop=True).then_inc(sem("b1_proj"), 1)
        pool_steps.append(b1_pool)
        pe_steps.append(b1_pe)
        act_steps.append(b1_act)
        dve_steps.append(b1_dve)
        n = make_norm(batches(y1, x_aux), counted("b1_y"), gain="norm_w", eps="eps_attn", mean=False)
        add_norm(n)

        def residual(name, k, prev):
            def f(e):
                for b in range(B):
                    e.wait_ge(*prev.done(b))
                    e.tensor_tensor(x_aux[:, b, :], x_aux[:, b, :], x_cur[:, b, :], ALU.add).then_inc(sem(name), 1)
            return f
        dve_steps.append(residual("b1_sum", 0, n))
        n = make_norm(batches(x_aux, x_cur), counted("b1_sum"))
        add_norm(n)
        final = n

        class Attn:
            def __init__(self, k, wide=False, causal=False):
                self.k, self.wide, self.causal = k, wide, causal
                self.base = k * B * UNITS
                c = Carve()
                if wide:
                    self.slots = 4
                    self.pt = c(4 * 4 * T).rearrange("p (s k q) -> p s k q", s=4, k=4)
                    self.ptc = c(4 * T).rearrange("p (s q) -> p s q", s=4)
                    self.p = c(8 * KEYS).rearrange("p (s k) -> p s k", s=8)
                    self.np = 8
                    self.qz = c(4 * T).rearrange("p (a r t) -> p a r t", a=2, r=2)
                    self.kt = c(2 * KEYS).rearrange("p (a t) -> p a t", a=2)
                    self.vv = c(4 * XH * XD).rearrange("p (k n) -> p k n", k=4)
                    self.vc = c(XH * XD)
                    self.kc = c(8 * B * S).rearrange("p (h n) -> p h n", h=8)
                else:
                    self.slots = 8
                    self.pt = c(8 * 4 * T).rearrange("p (s k q) -> p s k q", s=8, k=4)
                    self.p = c(4 * T).rearrange("p (s k) -> p s k", s=4)
                    self.np = 4
                    self.qt, self.kt = c(T), c(T)
                    self.qm = c(2 * T).rearrange("p (a t) -> p a t", a=2)
                    self.vv = c(4 * T).rearrange("p (k n) -> p k n", k=4)
                    self.x2 = c(T * B).rearrange("p (b t) -> p b t", b=B) if causal else None
                    self.ot = cent
                self.nm = stat[:, 0:4]
                self.sm = stat[:, 4:8]
                self.rs = stat[:, 8:12]

            def keys(self, u):
                return (u % QB + 1) * 128 if self.causal else (KEYS if self.wide else T)

            def s_view(self, u):
                if self.wide:
                    return ps[:, 2 * (u % 2):2 * (u % 2) + 2, 0:KEYS // 2]
                return ps[:, u % 4, 0:self.keys(u)]

            def p_view(self, u):
                if self.wide:
                    return self.p[:, u % self.np, :].rearrange("p (a k) -> p a k", a=2)
                return self.p[:, u % self.np, 0:self.keys(u)]

            def scores(self, e, b, u):
                n = self.base + b * UNITS + u
                h, q = u // QB, u % QB
                deep = 2 if self.wide else 4
                if n - deep >= 0:
                    e.wait_ge(sem("exp_done"), n - deep + 1)
                if self.wide:
                    e.wait_ge(sem("bank7_read"), self.at7["k", b * 8 + h // 2])
                    e.wait_ge(sem("ctx_keys"), b * 8 + h // 2 + 1)
                    for a in range(2):
                        i = e.matmul(ps[:, 2 * (u % 2) + a, 0:KEYS // 2],
                                     self.qz[:, h // 2 % 2, h % 2, q * 128:q * 128 + 128],
                                     self.kt[:, h // 2 % 2, a * KEYS // 2:(a + 1) * KEYS // 2], start=True, stop=True)
                else:
                    e.wait_ge(sem("q_masked"), self.qm0 + b * H + h + 1)
                    i = e.matmul(self.s_view(u), self.qm[:, h % 2, q * 128:q * 128 + 128], self.kt[:, 0:self.keys(u)],
                                 start=True, stop=True)
                i.then_inc(sem("scored"), 1)

            def neg_max(self, e, b, u):
                n = self.base + b * UNITS + u
                e.wait_ge(sem("scored"), n + 1)
                if n >= 4:
                    e.wait_ge(sem("exp_done"), n - 3)
                if self.causal:
                    q = u % QB
                    link(e, e.tensor_tensor(ps[:, u % 4, q * 128:q * 128 + 128], ps[:, u % 4, q * 128:q * 128 + 128],
                                            wt["causal"], ALU.add))
                e.tensor_reduce(self.nm[:, u % 4:u % 4 + 1], self.s_view(u), AX.XY if self.wide else AX.X, ALU.max,
                                negate=True).then_inc(sem("max_done"), 1)

            def exp(self, e, b, u):
                n = self.base + b * UNITS + u
                e.wait_ge(sem("max_done"), n + 1)
                if self.wide:
                    if u % QB == 0 and n // QB >= 2:
                        e.wait_ge(sem("ctx_turned"), n // QB - 1)
                elif n - self.base >= 4:
                    e.wait_ge(sem("transposed"), n - 3)
                e.activation(self.p_view(u), self.s_view(u), ACT.Exp, bias=self.nm[:, u % 4:u % 4 + 1],
                             accum_out=self.sm[:, u % 4:u % 4 + 1]).then_inc(sem("exp_done"), 1)

            def normalise(self, e, b, u):
                n = self.base + b * UNITS + u
                e.wait_ge(sem("exp_done"), n + 1)
                i = e.reciprocal(self.rs[:, u % 4:u % 4 + 1], self.sm[:, u % 4:u % 4 + 1])
                link(e, i)
                w = self.keys(u)
                e.tensor_scalar(self.p[:, u % self.np, 0:w], self.p[:, u % self.np, 0:w], self.rs[:, u % 4:u % 4 + 1], None,
                                ALU.mult).then_inc(sem("prob_done"), 1)

            def transpose(self, e, b, u):
                n = self.base + b * UNITS + u
                e.wait_ge(sem("prob_done"), n + 1)
                if n >= 2:
                    e.wait_ge(sem("evacuated"), n - 1)
                for k in range((u % QB + 1) if self.causal else 4):
                    i = e.transpose(ps[:, 4 + u % 2, k * 128:k * 128 + 128], self.p[:, u % self.np, k * 128:k * 128 + 128],
                                    ident)
                i.then_inc(sem("transposed"), 1)
                if self.wide and u % QB == QB - 1:
                    if b * XH + u // QB >= 1:
                        e.wait_ge(sem("ctx_probs"), b * XH + u // QB)
                    for q in range(QB):
                        i = e.transpose(ps[0:S, 6, q * 128:q * 128 + 128],
                                        self.p[:, (u - QB + 1 + q) % self.np, T:KEYS], ident)
                    i.then_inc(sem("ctx_turned"), 1)

            def evacuate(self, e, b, u):
                n = self.base + b * UNITS + u
                h, q = u // QB, u % QB
                e.wait_ge(sem("transposed"), n + 1)
                if q == 0:
                    g = (b * H + h - self.slots) // self.per
                    if g >= 0:
                        e.wait_ge(sem("pv_done"), self.pv0 + g + 1)
                kk = (q + 1) if self.causal else 4
                e.copy(self.pt[:, h % self.slots, 0:kk, q * 128:q * 128 + 128],
                       ps[:, 4 + u % 2, 0:kk * 128].rearrange("p (k q) -> p k q", k=kk)).then_inc(sem("evacuated"), 1)

            def pv(self, e, b, g, parts=range(4)):
                per, w = self.per, 128 // self.per
                h0 = g * per
                bank = 7 if self.wide else 6
                if parts[0] == 0:
                    e.wait_ge(sem("evacuated"), self.base + b * UNITS + (h0 + per) * QB)
                    if self.wide:
                        e.wait_ge(sem("ctx_probs"), b * XH + h0 + per)
                        self.bank_wait(("pv", b * 8 + g))
                    elif self.pv0 + b * (H // per) + g >= 1:
                        e.wait_ge(sem("pv_read"), self.pr0 + b * (H // per) + g)
                last = 4 if self.wide else 3
                for k in parts:
                    for j in range(per):
                        h = h0 + j
                        q0 = k * 128 if self.causal else 0
                        v_of = self.vv[:, k, :] if k < 4 else self.vc
                        p_of = self.pt[:, h % self.slots, k, q0:T] if k < 4 else self.ptc[:, h % self.slots, :]
                        i = e.matmul(ps[w * j:w * j + w, bank, q0:T], v_of[:, h * w:h * w + w], p_of,
                                     start=(k == 0), stop=(k == last), skip_group_check=True)
                if parts[-1] == last:
                    i.then_inc(sem("pv_done"), 1)

        if stages >= 2:
            b1_done = final.done(B - 1)
            n_lat = make_norm(batches(x_cur, x_aux), [final.done(b) for b in range(B)], gain="x_ln2_g", bias="x_ln2_b")
            add_norm(n_lat)
            ot_lo, ot_hi = cent, dev
            at = Attn(0, wide=True)
            at.per, at.pv0 = 2, 0
            Wq, Wkv, Wo = wt["Wq"], wt["Wkv"], wt["Wo"]

            uses7 = [("q", 0), ("k", 0)]
            for b in range(B):
                for hp in range(9):
                    nxt = b * 8 + hp + 1
                    if hp < 8 and nxt < B * 8:
                        uses7 += [("q", nxt), ("k", nxt)]
                    if hp:
                        uses7.append(("pv", b * 8 + hp - 1))
                    if hp == 0 and b:
                        at_ = len(uses7) - 2
                        uses7.insert(at_, ("out", b - 1))
            uses7.append(("out", B - 1))
            at7 = {u: n_ + 1 for n_, u in enumerate(uses7)}
            at.at7 = at7

            def ot_of(g):
                return (ot_lo if g < 4 else ot_hi)[:, g % 4, :]

            def b2_pe(e):
                def b7(use):
                    if at7[use] > 1:
                        e.wait_ge(sem("bank7_read"), at7[use] - 1)
                at.bank_wait = b7
                e.wait_ge(sem("load_wB"), 16)
                e.wait_ge(*n_ctx.done(0))
                for hp in range(8):
                    if hp == 4:
                        e.wait_ge(sem("ctx_k_read"), 4)
                    i = e.matmul(ps[:, hp % 4, 0:B * S], Wkv[:, hp * 128:hp * 128 + 128], ctx_ln[:, :], start=True,
                                 stop=True)
                    i.then_inc(sem("ctx_k_proj"), 1)

                def proj(what, n_):
                    b, hp = n_ // 8, n_ % 8
                    if hp == 0:
                        e.wait_ge(*n_lat.done(b))
                    b7((what, n_))
                    e.matmul(ps[:, 7, :], (Wq if what == "q" else Wkv)[:, hp * 128:hp * 128 + 128], x_aux[:, b, :],
                             start=True, stop=True).then_inc(sem("bank7_written"), 1)

                def outp(b):
                    b7(("out", b))
                    for hp in range(8):
                        i = e.matmul(ps[:, 7, :], Wo[:, hp * 128:hp * 128 + 128], ot_of(hp), start=(hp == 0),
                                     stop=(hp == 7))
                    i.then_inc(sem("b2_out"), 1)
                for b in range(B):
                    e.wait_ge(*n_lat.done(b))
                    for k in range(5):
                        src = x_aux[:, b, k * 128:k * 128 + 128] if k < 4 else ctx_ln[:, b * S:b * S + S]
                        m = 128 if k < 4 else S
                        for a in range(2):
                            j = b * 10 + 2 * k + a
                            if j >= 2:
                                e.wait_ge(sem("v_read"), j - 1)
                            if b >= 1 and j % 10 < 2:
                                e.wait_ge(sem("evacuated"), at.base + b * UNITS)
                            e.matmul(ps[0:m, 4 + j % 2, :], src, Wkv[:, 1024 + a * 512:1536 + a * 512], start=True,
                                     stop=True).then_inc(sem("v_proj"), 1)
                    if b == 0:
                        proj("q", 0)
                        proj("k", 0)
                    e.wait_ge(sem("v_read"), 10 * b + 10)
                    for i in range(UNITS + 8):
                        if i < UNITS:
                            at.scores(e, b, i)
                        if b and i == 0:
                            outp(b - 1)
                        if TURN_AT <= i < UNITS + TURN_AT:
                            at.transpose(e, b, i - TURN_AT)
                        hp, r = i // 8, i % 8
                        if r in QK_AT and hp < 8 and b * 8 + hp + 1 < 8 * B:
                            proj("qk"[QK_AT.index(r)], b * 8 + hp + 1)
                        if hp >= 1 and PV_PARTS[r]:
                            at.pv(e, b, hp - 1, PV_PARTS[r])
                outp(B - 1)

            def b2_act(e):
                e.wait_ge(sem("b2_zeros"), 1)
                for hp in range(8):
                    e.wait_ge(sem("ctx_k_proj"), hp + 1)
                    e.copy(at.kc[:, hp, :], ps[:, hp % 4, 0:B * S]).then_inc(sem("ctx_k_read"), 1)
                for b in range(B):
                    for k in range(5):
                        m = 128 if k < 4 else S
                        if b >= 1 and k == 0:
                            e.wait_ge(sem("pv_done"), 8 * b)
                        for a in range(2):
                            j = b * 10 + 2 * k + a
                            e.wait_ge(sem("v_proj"), j + 1)
                            dst = at.vv[:, k, a * 512:a * 512 + 512] if k < 4 else at.vc[0:S, a * 512:a * 512 + 512]
                            e.copy(dst, ps[0:m, 4 + j % 2, :]).then_inc(sem("v_read"), 1)
                    for i in range(UNITS + TURN_AT):
                        if i < UNITS:
                            at.exp(e, b, i)
                        if i >= TURN_AT:
                            at.evacuate(e, b, i - TURN_AT)

            def b2_dve(e):
                written, pvs = [0], [0]
                e.wait_ge(sem("b2_zeros"), 1)

                def qread(b, hp):
                    written[0] += 1
                    e.wait_ge(sem("bank7_written"), written[0])
                    if b * 8 + hp >= 2:
                        e.wait_ge(sem("scored"), (b * 8 + hp - 1) * 8)
                    for r in range(2):
                        i = e.tensor_scalar(at.qz[64 * r:64 * r + 64, hp % 2, r, :], ps[64 * r:64 * r + 64, 7, :],
                                            0.125, None, ALU.mult)
                    i.then_inc(sem("bank7_read"), 1)

                def kread(b, hp):
                    written[0] += 1
                    e.wait_ge(sem("bank7_written"), written[0])
                    e.tensor_copy(at.kt[:, hp % 2, 0:T], ps[:, 7, :]).then_inc(sem("bank7_read"), 1)

                def pread(b, g):
                    pvs[0] += 1
                    e.wait_ge(sem("pv_done"), pvs[0])
                    if b >= 1 and g == 0:
                        e.wait_ge(sem("b2_out"), b)
                    e.tensor_copy(ot_of(g), ps[:, 7, :]).then_inc(sem("bank7_read"), 1)

                def cread(b, h):
                    n = b * XH + h
                    e.wait_ge(sem("ctx_turned"), n + 1)
                    if n >= 4:
                        e.wait_ge(sem("pv_done"), (n - 4) // 2 + 1)
                    e.tensor_copy(at.ptc[0:S, h % 4, :], ps[0:S, 6, :]).then_inc(sem("ctx_probs"), 1)

                def total(b):
                    e.wait_ge(sem("b2_out"), b + 1)
                    e.tensor_tensor(x_aux[:, b, :], ps[:, 7, :], x_cur[:, b, :], ALU.add).then_inc(sem("bank7_read"), 1)
                qread(0, 0)
                kread(0, 0)
                for b in range(B):
                    for i in range(UNITS + 9):
                        if i < UNITS:
                            at.neg_max(e, b, i)
                        if 1 <= i <= UNITS:
                            at.normalise(e, b, i - 1)
                        if b and i == 0:
                            total(b - 1)
                        if i >= 4 + TURN_AT and (i - TURN_AT) % 4 == 0 and (i - TURN_AT) // 4 - 1 < XH:
                            cread(b, (i - TURN_AT) // 4 - 1)
                        hp, r = i // 8, i % 8
                        if r == 0 and hp >= 2:
                            pread(b, hp - 2)
                        if r in QK_AT and hp < 8 and b * 8 + hp + 1 < 8 * B:
                            (qread if r == QK_AT[0] else kread)(*divmod(b * 8 + hp + 1, 8))
                total(B - 1)

            def b2_pool(e):
                e.wait_ge(*b1_done)
                e.memset(at.vc, 0.0)
                e.memset(at.qz[:, :, :, :], 0.0)
                e.memset(at.ptc[:, :, :], 0.0).then_inc(sem("b2_zeros"), 1)
                for b in range(B):
                    for hp in range(8):
                        n = b * 8 + hp
                        e.wait_ge(sem("ctx_k_read"), hp + 1)
                        if n >= 2:
                            e.wait_ge(sem("scored"), (n - 1) * 8)
                        e.tensor_copy(at.kt[:, hp % 2, T:KEYS],
                                      at.kc[:, hp, b * S:b * S + S]).then_inc(sem("ctx_keys"), 1)

            pe_steps.append(b2_pe)
            act_steps.append(b2_act)
            dve_steps.append(b2_dve)
            pool_steps.append(b2_pool)
            n = make_norm(batches(x_aux, x_cur), [(sem("bank7_read"), at7["out", b]) for b in range(B)])
            add_norm(n)
            final = n

        def narrow(nth, src, src_ready, dst, tag, load, wq, wk, wv, wo, bias_v=None, rope=None):
            causal = rope is not None
            SC = HD ** -0.5
            NG, LAG, STEPS = B * 4, 2, B * 4 + 3
            S1, S2 = 3, 2
            ROWS = 9 * HD
            NQ = 4 if rope else 2
            c = Carve()
            packs = [[c(H * T // 2).bitcast(BF16).rearrange("p (h t) -> p h t", h=H) for _ in range(2)]
                     for _ in range(2)]
            q_pack, k_pack = packs
            p_t = c(8 * T).rearrange("p (s t) -> p s t", s=8)
            vv = c(2 * 4 * H * 32).rearrange("p (a k h n) -> p a k h n", a=2, k=4, h=H)
            parts = c(2 * 3 * T // 2).bitcast(BF16).rearrange("p (w i t) -> p w i t", w=2, i=3)
            raw = c(2 * T).rearrange("p (a t) -> p a t", a=2)
            m_t, m_rest = c(128)[0:16], c(128)[0:16]
            m_parts = c(192)[0:16].bitcast(BF16).rearrange("p (i t) -> p i t", i=3)
            rs_wide = c(T)
            ones_row = p_t[0:3, 7, 0:T // 2].bitcast(BF16)
            nm = stat[:, 16:48].rearrange("p (a u) -> p a u", a=2)
            rs = stat[:, 48:64]
            ot = cent
            scr = nc.dram_tensor(tag + "_parts", (B, 2, 3 * HD, H * T), BF16, kind="Internal").ap()
            scr_m = nc.dram_tensor(tag + "_maxima", (NG, 3, 16 * 128), BF16, kind="Internal").ap()
            (score, max_done, score2, exp_done, turned, m_split, m_out, m_rows, part_done, raw_done, b6_read, written,
             b7_read, qk_ready, split_q, split_k, parts_out, packed, rs_spread) = (
                sem(f"{tag}_{x}") for x in ("score", "max", "score2", "exp", "turned", "m_split", "m_out", "m_rows",
                                            "part", "raw", "b6_read", "written", "b7_read", "qk_ready", "split_q",
                                            "split_k", "parts_out", "packed", "rs_spread"))
            ones_set, vv_set, ones_rows = (sem(x) for x in ("ones_set", "vv_set", "ones_rows"))
            group_w = lambda G: slice(G % 4 * 4, G % 4 * 4 + 4)

            uses = [("qk", 0, j) for j in range(NQ)]
            for G in range(STEPS):
                if G % 4 == 0 and G // 4 + 1 < B:
                    uses += [("qk", G // 4 + 1, j) for j in range(NQ)]
                if G % 4 == 0 and G // 4 < B:
                    uses.append(("v", G // 4, 0))
                if G % 4 == 2 and G >= 6:
                    uses.append(("out", (G - 6) // 4, 0))
            at7 = {u: n_ + 1 for n_, u in enumerate(uses)}

            def at6(G, i):
                before = min(max(G - 1, 0), NG) + 2 * min(max(G - 3, 0), NG)
                return before + (1 if 1 <= G <= NG and i else 0) + (i if i else 1)

            def keys(u):
                return (u % 4 + 1) * 128 if causal else T

            def pe(e):
                e.wait_ge(sem("load_" + load), 16)
                e.wait_ge(*src_ready[B - 1])
                mats = [wt[w] for w in ([wq, rope[0], wk, rope[1]] if rope else [wq, wk])]

                def qk(b, j):
                    if b:
                        e.wait_ge(b7_read, at7["qk", b, j] - 1)
                    e.matmul(ps[:, 7 if b else 4 + j, :], mats[j], src[:, b, :], start=True,
                             stop=True).then_inc(written, 1)

                def pv(n_):
                    G, p = n_ // 4, n_ % 4
                    b = G // 4
                    e.wait_ge(exp_done, 4 * n_ + 4)
                    if p == 0:
                        e.wait_ge(b7_read, at7["v", b, 0])
                        if G:
                            e.wait_ge(raw_done, G)
                    q0 = p * 128 if causal else 0
                    for j in range(4):
                        i = e.matmul(ps[32 * j:32 * j + 32, 5, q0:T], vv[:, b % 2, p, G % 4 * 4 + j, :],
                                     p_t[:, n_ % 2 * 4 + j, q0:T], start=(p == 0), stop=(p == 3),
                                     skip_group_check=True)
                    i.then_inc(part_done, 1)
                for j in range(NQ):
                    qk(0, j)
                for step in range(STEPS * 16):
                    G, u = step // 16, step % 16
                    if G < NG:
                        h, q = G % 4 * 4 + u // 4, u % 4
                        if u == 0 and G % 4 == 0:
                            e.wait_ge(packed, 16 * 12 * (G // 4 + 1))
                        if step >= S1:
                            e.wait_ge(max_done, step - S1 + 1)
                        pack = (G // 4) % 2
                        i = e.matmul(ps[:, step % S1, 0:keys(u)], q_pack[pack][0:ROWS, h, q * 128:q * 128 + 128],
                                     k_pack[pack][0:ROWS, h, 0:keys(u)], start=True, stop=not causal,
                                     skip_group_check=True)
                        if causal:
                            i = e.matmul(ps[:, step % S1, q * 128:q * 128 + 128], wt_bf[:, 0:128], wt_bf[:, 128:256],
                                         start=False, stop=True, skip_group_check=True)
                        i.then_inc(score, 1)
                    if 2 <= G < NG + 2:
                        G2, m = G - LAG, step - 16 * LAG
                        h, k = G2 % 4 * 4 + u % 4, u // 4
                        if u == 0:
                            e.wait_ge(m_rows, 16 * (G2 + 1))
                            if G2 == 0:
                                e.wait_ge(ones_rows, 32 * (nth + 1))
                        if m >= S2:
                            e.wait_ge(exp_done, m - S2 + 1)
                        pack = (G2 // 4) % 2
                        q0 = k * 128 if causal else 0
                        i = e.matmul(ps[:, S1 + m % S2, q0:T], k_pack[pack][0:ROWS + 3, h, k * 128:k * 128 + 128],
                                     q_pack[pack][0:ROWS + 3, h, q0:T], start=True, stop=not causal,
                                     skip_group_check=True)
                        if causal:
                            i = e.matmul(ps[:, S1 + m % S2, q0:q0 + 128], wt_bf[:, 128:256], wt_bf[:, 0:128],
                                         start=False, stop=True, skip_group_check=True)
                        i.then_inc(score2, 1)
                    n_ = (step - 16 * LAG - PV_AT) // 4
                    if (step - PV_AT) % 4 == 0 and 0 <= n_ < 4 * NG:
                        pv(n_)
                    if u == 1 and 1 <= G <= NG:
                        e.wait_ge(max_done, 16 * G)
                        if at6(G, 0) > 1:
                            e.wait_ge(b6_read, at6(G, 0) - 1)
                        e.transpose(ps[0:16, 6, 0:128], nm[:, (G - 1) % 2, :], ident).then_inc(turned, 1)
                    if u == 5 and G >= 3:
                        e.wait_ge(raw_done, G - 2)
                        e.wait_ge(b6_read, at6(G, 1) - 1)
                        for q in range(4):
                            i = e.matmul(ps[:, 6, 4 * q:4 * q + 4], raw[:, (G - 3) % 2, q * 128:q * 128 + 128],
                                         v("sum_pick", 0, 4), start=True, stop=True)
                        i.then_inc(turned, 1)
                    if u == 8 and G >= 3:
                        e.wait_ge(rs_spread, G - 2)
                        for q in range(4):
                            i = e.matmul(ps[:, 6, q * 128:q * 128 + 128], rs_wide[:, q * 128:q * 128 + 128], ident,
                                         start=True, stop=True)
                        i.then_inc(turned, 1)
                    if G % 4 == 0 and G // 4 + 1 < B and u % 3 == 0 and 3 <= u < 3 + 3 * NQ:
                        qk(G // 4 + 1, u // 3 - 1)
                    if G % 4 == 0 and G // 4 < B and u == 15:
                        b = G // 4
                        e.wait_ge(b7_read, at7["v", b, 0] - 1)
                        for k in range(4):
                            i = e.matmul(ps[:, 7, k * 128:k * 128 + 128], src[:, b, k * 128:k * 128 + 128], wt[wv],
                                         start=True, stop=True)
                        i.then_inc(written, 1)
                    if G % 4 == 2 and G >= 6 and 11 <= u < 15:
                        b, g = (G - 6) // 4, u - 11
                        if g == 0:
                            e.wait_ge(b6_read, at6(G, 2))
                            e.wait_ge(b7_read, at7["out", b, 0] - 1)
                        i = e.matmul(ps[:, 7, :], wt[wo][:, g * 128:g * 128 + 128], ot[:, g, :], start=(g == 0),
                                     stop=(g == 3), skip_group_check=True)
                        if g == 3:
                            i.then_inc(written, 1)

            def act(e):
                e.wait_ge(parts_out, 32)
                for i in (1, 2):
                    pack_k(e, 0, i)
                for m in range(16 * (NG + 1)):
                    G, u = m // 16 + LAG, m % 16
                    if m < 16 * NG:
                        e.wait_ge(score2, m + 1)
                        if m >= 8:
                            e.wait_ge(part_done, (m - 8) // 4 + 1)
                        q0 = u // 4 * 128 if causal else 0
                        e.activation(p_t[:, m % 8, q0:T], ps[:, S1 + m % S2, q0:T], ACT.Exp).then_inc(exp_done, 1)
                    if u == 3 and G >= 3:
                        e.wait_ge(part_done, 4 * (G - 2))
                        if G >= 5:
                            e.wait_ge(b6_read, at6(G - 2, 2))
                        e.copy(raw[:, (G - 3) % 2, :], ps[:, 5, :]).then_inc(raw_done, 1)
                    if u == 6 and G >= 3:
                        e.wait_ge(b6_read, at6(G, 1))
                        if G >= 4:
                            e.wait_ge(turned, at6(G - 1, 2))
                        e.copy(rs_wide.rearrange("p (n r) -> p n r", r=32),
                               rs.unsqueeze(2).to_broadcast([128, 16, 32])).then_inc(rs_spread, 1)

            def split(e, b, which):
                for step in range(4):
                    for w in which:
                        s_, base = (split_q, split_k)[w], 4 * b
                        x, rest, part = dev[:, 2 * w, :], dev[:, 2 * w + 1, :], parts[:, w, :, :]
                        if step == 0:
                            e.wait_ge(qk_ready, 2 * b + w + 1)
                            if b:
                                e.wait_ge(parts_out, 16 * 2 * b)
                            i = e.tensor_copy(part[:, 0, :], x)
                        else:
                            e.wait_ge(s_, base + step)
                            if step == 1:
                                i = e.tensor_tensor(rest, x, part[:, 0, :], ALU.subtract)
                            elif step == 2:
                                i = e.tensor_copy(part[:, 1, :], rest)
                            else:
                                i = e.tensor_tensor(part[:, 2, :], rest, part[:, 1, :], ALU.subtract)
                        i.then_inc(s_, 1)

            def dve(e):
                e.memset(ones_row, 1.0).then_inc(ones_set, 1)
                if causal:
                    e.wait_ge(sem("load_" + load), 16)
                    e.tensor_copy(wt_bf[:, 0:128], ident)
                    link(e, e.tensor_copy(wt_bf[:, 128:256], wt["causal"]))

                def qk(b, j):
                    e.wait_ge(written, at7["qk", b, j])
                    if b and j == 0:
                        e.wait_ge(split_q, 4 * b)
                        e.wait_ge(split_k, 4 * b)
                    bank = ps[:, 7 if b else 4 + j, :]
                    if rope:
                        e.scalar_tensor_tensor(out=dev[:, j, :], in0=bank, scalar=SC if j < 2 else 1.0,
                                               in1=wt["sin" if j % 2 else "cos"], op0=ALU.mult,
                                               op1=ALU.mult).then_inc(b7_read, 1)
                        if j % 2:
                            e.wait_ge(b7_read, at7["qk", b, j])
                            e.tensor_tensor(dev[:, j - 1, :], dev[:, j - 1, :], dev[:, j, :],
                                            ALU.add).then_inc(qk_ready, 1)
                    else:
                        if j == 0:
                            i = e.tensor_scalar(dev[:, 0, :], bank, v("f_bq"), SC, ALU.add, ALU.mult)
                        else:
                            i = e.tensor_scalar(dev[:, 2, :], bank, v("f_bk"), None, ALU.add)
                        i.then_inc(b7_read, 1)
                        e.wait_ge(b7_read, at7["qk", b, j])
                        e.nop().then_inc(qk_ready, 1)
                for j in range(NQ):
                    qk(0, j)
                split(e, 0, (0, 1))
                for step in range(STEPS * 16):
                    G, u = step // 16, step % 16
                    if G < NG:
                        e.wait_ge(score, step + 1)
                        if u == 0 and G >= 2:
                            e.wait_ge(turned, at6(G - 1, 0))
                        e.tensor_reduce(nm[:, G % 2, u:u + 1], ps[:, step % S1, 0:keys(u)], AX.X, ALU.max,
                                        negate=True).then_inc(max_done, 1)
                    if u == 2 and 1 <= G <= NG:
                        e.wait_ge(turned, at6(G, 0))
                        if G >= 2:
                            e.wait_ge(m_split, 4 * (G - 1))
                        e.tensor_copy(m_t, ps[0:16, 6, 0:128]).then_inc(b6_read, 1)
                    if u == 6 and G >= 3:
                        e.wait_ge(turned, at6(G, 1))
                        e.reciprocal(rs, ps[:, 6, 0:16]).then_inc(b6_read, 1)
                    if u == 9 and G >= 3:
                        G3 = G - 3
                        e.wait_ge(turned, at6(G, 2))
                        if G3 % 4 == 0 and G3:
                            e.wait_ge(written, at7["out", G3 // 4 - 1, 0])
                        e.tensor_tensor(ot[:, G3 % 4, :], raw[:, G3 % 2, :], ps[:, 6, :],
                                        ALU.mult).then_inc(b6_read, 1)
                    if G % 4 == 0 and G // 4 + 1 < B and u % 3 == 1 and 3 <= u < 3 + 3 * NQ:
                        qk(G // 4 + 1, u // 3 - 1)
                    if G % 4 == 1 and G // 4 < B and u == 0:
                        b = G // 4
                        e.wait_ge(written, at7["v", b, 0])
                        e.wait_ge(vv_set, 3 * (nth + 1))
                        if b >= 2:
                            e.wait_ge(part_done, 16 * (b - 1))
                        out_v = vv[:, b % 2, :, :, 0:HD]
                        in_v = ps[:, 7, :].rearrange("p (k h d) -> p k h d", k=4, h=H)
                        if bias_v:
                            bias = wt[bias_v].rearrange("p (h d) -> p h d", h=H).unsqueeze(1).to_broadcast(
                                [128, 4, H, HD])
                            e.tensor_tensor(out_v, in_v, bias, ALU.add).then_inc(b7_read, 1)
                        else:
                            e.tensor_copy(out_v, in_v).then_inc(b7_read, 1)
                    if G % 4 == 2 and G >= 6 and u == 15:
                        b = (G - 6) // 4
                        e.wait_ge(written, at7["out", b, 0])
                        if bias_v:
                            o = e.scalar_tensor_tensor(out=dst[:, b, :], in0=ps[:, 7, :], scalar=v("f_bo"),
                                                       in1=x_cur[:, b, :], op0=ALU.add, op1=ALU.add)
                        else:
                            o = e.tensor_tensor(dst[:, b, :], ps[:, 7, :], x_cur[:, b, :], ALU.add)
                        o.then_inc(b7_read, 1)

            def pool(e):
                e.wait_ge(*src_ready[B - 1])
                e.memset(vv[:, 0, :, :, :], 0.0).then_inc(vv_set, 1)
                e.memset(vv[:, 1, :, :, :], 0.0).then_inc(vv_set, 1)
                e.wait_ge(vv_set, 3 * nth + 2)
                e.memset(vv[:, :, :, :, HD:HD + 1].rearrange("p a k h n -> p (a k h) n"), 1.0).then_inc(vv_set, 1)
                for G in range(NG + 1):
                    if G:
                        s_, base = m_split, 4 * (G - 1)
                        e.wait_ge(b6_read, at6(G, 0))
                        if G >= 2:
                            e.wait_ge(m_out, 16 * (G - 1))
                        e.tensor_copy(m_parts[:, 0, :], m_t).then_inc(s_, 1)
                        e.wait_ge(s_, base + 1)
                        e.tensor_tensor(m_rest, m_t, m_parts[:, 0, :], ALU.subtract).then_inc(s_, 1)
                        e.wait_ge(s_, base + 2)
                        e.tensor_copy(m_parts[:, 1, :], m_rest).then_inc(s_, 1)
                        e.wait_ge(s_, base + 3)
                        e.tensor_tensor(m_parts[:, 2, :], m_rest, m_parts[:, 1, :], ALU.subtract).then_inc(s_, 1)
                        e.wait_ge(s_, base + 4)
                        e.dma_start(scr_m[G - 1].rearrange("i (u t) -> u i t", u=16), m_parts).then_inc(m_out, 16)
                        e.wait_ge(m_out, 16 * G)
                        e.dma_start(q_pack[(G - 1) // 4 % 2][ROWS:ROWS + 3, group_w(G - 1), :],
                                    scr_m[G - 1].rearrange("i (h t) -> i h t", h=4)).then_inc(m_rows, 16)
                    if G % 4 < 2 and G // 4 + 1 < B:
                        split(e, G // 4 + 1, (G % 4,))

            def pack_k(e, b, i):
                for j in range(3):
                    r = 24 * i + 8 * j
                    e.dma_start(k_pack[b % 2][r:r + 8, :, :], scr[b, 1, 8 * i:8 * i + 8].rearrange(
                        "r (h t) -> r h t", h=H)).then_inc(packed, 16)

            def sp(e):
                e.wait_ge(ones_set, nth + 1)
                for a in range(2):
                    e.dma_start(k_pack[a][ROWS:ROWS + 3, :, :],
                                ones_row.unsqueeze(1).to_broadcast([3, H, T])).then_inc(ones_rows, 16)
                for b in range(B):
                    for w in range(2):
                        e.wait_ge((split_q, split_k)[w], 4 * b + 4)
                        e.dma_start(scr[b, w].rearrange("(i d) (h t) -> (d h) i t", i=3, h=H),
                                    parts[:, w, :, :]).then_inc(parts_out, 16)
                    e.wait_ge(parts_out, 16 * 2 * (b + 1))
                    if b >= 2:
                        e.wait_ge(score2, 64 * (b - 1))
                    for i in range(3):
                        e.dma_start(q_pack[b % 2][24 * i:24 * i + 24, :, :],
                                    scr[b, 0].rearrange("r (h t) -> r h t", h=H)).then_inc(packed, 16)
                    for i in (range(3) if b else (0,)):
                        pack_k(e, b, i)
            pe_steps.append(pe)
            act_steps.append(act)
            dve_steps.append(dve)
            pool_steps.append(pool)
            sp_steps.append(sp)
            return [(b7_read, at7["out", b, 0]) for b in range(B)]

        if stages >= 3:
            b3_res = narrow(0, x_cur, [final.done(b) for b in range(B)], x_aux, "b3", "wC", "f_Wq", "f_Wk", "f_Wv", "f_Wo",
                            bias_v="f_bv")
            n3 = make_norm(batches(x_aux, x_aux), b3_res, gain="f_ln1_g", bias="f_ln1_b")
            add_norm(n3)

            c = Carve()
            mask = c(2 * 4 * T).rearrange("p (a e t) -> p a e t", a=2, e=4)
            act_r = c(4 * T).rearrange("p (s t) -> p s t", s=4)
            key, key_f, key_c = c(T), c(T), c(T)
            key_i = c(T).bitcast(I32)
            W1, W2 = wt["W1"], wt["W2"]
            NI = E0 * C0

            def moe_pe(e):
                e.wait_ge(sem("load_wM0"), 16)

                def route(b):
                    e.wait_ge(*n3.done(b))
                    if b == 0:
                        e.wait_ge(*n3.done(3))
                    if b >= 2:
                        e.wait_ge(sem("key_read"), b - 1)
                    e.matmul(ps[:, 6 + b % 2, :], wt["router"], x_aux[:, b, :], start=True,
                             stop=True).then_inc(sem("routed"), 1)

                def down(b, i):
                    e.wait_ge(sem("relu_gated"), b * NI + i + 1)
                    if i == 0 and b >= 2:
                        e.wait_ge(sem("b3_sum"), b - 1)
                    e.matmul(ps[:, 4 + b % 2, :], W2[:, i * 128:i * 128 + 128], act_r[:, i % 4, :], start=(i == 0),
                             stop=(i == NI - 1)).then_inc(sem("moe_down"), 1)
                route(0)
                for b in range(B):
                    if b + 1 < B:
                        route(b + 1)
                    for i in range(NI + 3):
                        if i < NI:
                            n = b * NI + i
                            if n >= 4:
                                e.wait_ge(sem("relu_done"), n - 3)
                            e.matmul(ps[:, i % 4, :], W1[:, i * 128:i * 128 + 128], x_aux[:, b, :], start=True,
                                     stop=True).then_inc(sem("moe_up"), 1)
                        if i >= 3:
                            down(b, i - 3)

            def moe_act(e):
                for n in range(B * NI):
                    e.wait_ge(sem("moe_up"), n + 1)
                    if n >= 4:
                        e.wait_ge(sem("moe_down"), n - 3)
                    e.activation(act_r[:, n % 4, :], ps[:, n % 4, :], ACT.Relu,
                                 bias=v("f_b1", n % NI)).then_inc(sem("relu_done"), 1)

            def moe_pool(e):
                for n in range(B * NI):
                    b, ex = n // NI, n % NI // C0
                    e.wait_ge(sem("masks"), b + 1)
                    e.wait_ge(sem("relu_done"), n + 1)
                    e.tensor_tensor(act_r[:, n % 4, :], act_r[:, n % 4, :], mask[:, b % 2, ex, :],
                                    ALU.mult).then_inc(sem("relu_gated"), 1)

            def moe_dve(e):
                def masks(b):
                    e.wait_ge(sem("routed"), b + 1)
                    if b >= 2:
                        e.wait_ge(sem("relu_gated"), (b - 1) * NI)
                    i = e.tensor_scalar(key, ps[:, 6 + b % 2, :], v("router_b"), None, ALU.add)
                    i.then_inc(sem("key_read"), 1)
                    e.wait_ge(sem("key_read"), b + 1)
                    link(e, e.tensor_copy(key_i, key))
                    link(e, e.tensor_copy(key_f, key_i))
                    link(e, e.tensor_tensor(key_c, key_f, key, ALU.is_gt))
                    link(e, e.tensor_tensor(key_f, key_f, key_c, ALU.subtract))
                    link(e, e.tensor_copy(key_i, key_f))
                    link(e, e.tensor_scalar(key_i, key_i, E0 - 1, None, ALU.bitwise_and))
                    link(e, e.tensor_copy(key_f, key_i))
                    for ex in range(E0):
                        i = e.tensor_scalar(mask[:, b % 2, ex, :], key_f, float(ex), None, ALU.is_equal)
                    i.then_inc(sem("masks"), 1)

                def total(b):
                    e.wait_ge(sem("moe_down"), (b + 1) * NI)
                    e.wait_ge(sem("masks"), b + 1)
                    link(e, e.tensor_tensor(x_aux[:, b, :], ps[:, 4 + b % 2, :], x_aux[:, b, :], ALU.add))
                    for ex in range(E0):
                        i = e.scalar_tensor_tensor(out=x_aux[:, b, :], in0=mask[:, b % 2, ex, :],
                                                   scalar=v("f_b2", ex), in1=x_aux[:, b, :], op0=ALU.mult, op1=ALU.add)
                        if ex < E0 - 1:
                            link(e, i)
                    i.then_inc(sem("b3_sum"), 1)
                masks(0)
                for b in range(B):
                    if b + 1 < B:
                        masks(b + 1)
                    total(b)

            def moe_sp(e):
                e.wait_ge(sem("b2_out"), B)
                e.dma_start(reg1[:, 0:width["wD"]], groups["wD"]).then_inc(sem("load_wD"), 16)
                if stages >= 4:
                    e.wait_ge(sem("b4_out"), OUT_OPS * (NCB - 1))
                    e.wait_ge(sem("b4_last_out"), OUT_OPS)
                else:
                    e.wait_ge(sem("moe_down"), B * NI)
                e.dma_start(reg2[:, 0:width["wM1"]], groups["wM1"]).then_inc(sem("load_wM1"), 16)
            pe_steps.append(moe_pe)
            act_steps.append(moe_act)
            pool_steps.append(moe_pool)
            dve_steps.append(moe_dve)
            sp_steps.append(moe_sp)
            n = make_norm(batches(x_aux, x_aux), counted("b3_sum"), gain="f_ln2_g", bias="f_ln2_b")
            add_norm(n)
            dve_steps.append(residual("b3_both", 0, n))
            n = make_norm(batches(x_aux, x_cur), counted("b3_both"))
            add_norm(n)
            final = n

        def gated(tag, per, rows, src, src_done, w_gate, w_up, w_down, act_r, weight=None, load=None, weight_ready=None,
                  extra=None):
            s_up, s_silu, s_prod, s_down = (sem(f"{tag}_{x}") for x in ("up", "silu", "prod", "down"))
            s_in = sem(tag + "_gated") if weight else s_prod
            extra = extra or {}
            R = rows

            def pe(e):
                if load:
                    e.wait_ge(sem("load_" + load), 16)
                e.wait_ge(*src_done[B - 1])
                for step in extra.get("pe_first", ()):
                    step(e)
                for b in range(B):
                    for i in range(per + 2):
                        n = b * per + i
                        if i < per:
                            if n >= 2:
                                e.wait_ge(s_silu, n - 1)
                                e.wait_ge(s_prod, n - 1)
                            e.matmul(ps[0:R, n % 2, :], w_gate(i), src[:, b, :], start=True, stop=True)
                            e.matmul(ps[0:R, 2 + n % 2, :], w_up(i), src[:, b, :], start=True,
                                     stop=True).then_inc(s_up, 1)
                        if i >= 2:
                            m = n - 2
                            e.wait_ge(s_in, m + 1)
                            if i == 2 and b >= 2:
                                e.wait_ge(sem(tag + "_sum"), b - 1)
                            e.matmul(ps[:, 4 + b % 2, :], w_down(i - 2), act_r[0:R, m % 4, :], start=(i == 2),
                                     stop=(i == per + 1)).then_inc(s_down, 1)
                        if "pe" in extra:
                            extra["pe"](e, b, i)

            def act(e):
                for step in extra.get("act_first", ()):
                    step(e)
                for n in range(B * per):
                    e.wait_ge(s_up, n + 1)
                    if n >= 4:
                        e.wait_ge(s_down, n - 3)
                    e.activation(act_r[0:R, n % 4, :], ps[0:R, n % 2, :], ACT.Silu).then_inc(s_silu, 1)
                    if "act" in extra:
                        extra["act"](e, n // per, n % per)

            def dve(e):
                for step in extra.get("dve_first", ()):
                    step(e)
                for b in range(B):
                    for i in range(per):
                        n = b * per + i
                        e.wait_ge(s_silu, n + 1)
                        e.tensor_tensor(act_r[0:R, n % 4, :], act_r[0:R, n % 4, :], ps[0:R, 2 + n % 2, :],
                                        ALU.mult).then_inc(s_prod, 1)
                        if "dve" in extra:
                            extra["dve"](e, b, i)
                    e.wait_ge(s_down, (b + 1) * per)
                    extra["total"](e, b).then_inc(sem(tag + "_sum"), 1)

            def pool(e):
                for b in range(B):
                    for i in range(per):
                        n = b * per + i
                        if i == 0:
                            e.wait_ge(*weight_ready(b))
                        e.wait_ge(s_prod, n + 1)
                        e.tensor_tensor(act_r[:, n % 4, :], act_r[:, n % 4, :], weight(b, i),
                                        ALU.mult).then_inc(s_in, 1)
            pe_steps.append(pe)
            act_steps.append(act)
            dve_steps.append(dve)
            if weight:
                pool_steps.append(pool)

        if stages >= 4:
            c = Carve()
            o_all = cent.rearrange("p b t -> p (b t)")
            q_raw = c(T * HD).rearrange("p (t d) -> p t d", d=HD)
            k_hat = c(T * HD).rearrange("p (t d) -> p t d", d=HD)
            y_flat = c(T * 12)
            y = y_flat.rearrange("p (t w) -> p t w", w=12)
            hist_flat = c((NB + 1) * 32)
            hist = hist_flat.rearrange("p (n j d) -> p n j d", j=4, d=HD)
            terms_flat = c(2 * CB * 144)
            terms = terms_flat.rearrange("p (c n i j d) -> p (c n) i j d", c=2, n=CB, i=BL, j=4)
            alpha, beta, gamma, to_end, t_one, t_two = (c(T) for _ in range(6))
            rank1 = c(2 * 32 * (BL + 1)).rearrange("p (a j d l) -> p a j d l", a=2, j=4, l=BL + 1)
            k_sq = terms_flat[:, 0:T * HD].rearrange("p (t d) -> p t d", d=HD)
            prod_k = terms_flat
            q_sq = hist_flat[:, 0:T * HD].rearrange("p (t d) -> p t d", d=HD)
            kk_dot = hist_flat[:, 0:3 * T].rearrange("p (s n i) -> p s n i", s=3, i=BL)
            xp = y_flat[:, 0:B * (T + CTAPS - 1)].rearrange("p (b t) -> p b t", b=B)
            qk_dot = x_aux.rearrange("p s (n i) -> p s n i", i=BL)
            prod_q = {1: reg2[:, 0:3072], 0: reg2[:, 0:4096], 2: reg2[:, 4096:6144], 3: o_all[:, 0:1024]}
            OC = CB * BL * 32
            prod_o = [reg2[:, a * OC:(a + 1) * OC] for a in range(2)]
            r_k, r_q, coef = dev[:, 0, :], dev[:, 1, :], dev[:, 2, :]
            neg_delta = reg2[:, T * HD:T * (HD + 4)].rearrange("p (n i j) -> p n i j", i=BL, j=4)
            o_tok = o_all.rearrange("p (t j) -> p t j", j=4)
            PADW = CTAPS - 1
            n = make_norm([(x_cur[:, b, :], xp[:, b, PADW:], T, b) for b in range(B)],
                          [final.done(b) for b in range(B)], gain="norm1_w", eps="eps6", mean=False)
            add_norm(n)
            n4 = n
            cols = [("a_s", 0), ("b_s", 0)] + [("k_s", d) for d in range(8)] + [("q_s", d) for d in range(8)] \
                + [("v_s", j) for j in range(4)]

            def b4_pe(e):
                e.wait_ge(sem("load_wD"), 16)
                e.wait_ge(sem("b4_xc"), 1)
                for g, (w, d) in enumerate(cols):
                    if 8 <= g < 10:
                        e.wait_ge(sem("b4_act_read"), g - 7)
                    elif 10 <= g < 18:
                        e.wait_ge(sem("b4_dve_read"), g - 9)
                    elif g >= 18:
                        e.wait_ge(sem("b4_act_read"), g - 15)
                    for b in range(B):
                        i = e.matmul(ps[32 * b:32 * b + 32, g % 8, :], wt[w][:, d * 32:d * 32 + 32], x_aux[:, b, :],
                                     start=True, stop=True)
                    i.then_inc(sem("b4_proj"), 1)

            def b4_act(e):
                e.wait_ge(sem("b4_conv"), CTAPS)
                e.activation(x_aux[:, :, :], x_aux[:, :, :], ACT.Silu, bias=v("conv_b")).then_inc(sem("b4_xc"), 1)
                e.wait_ge(sem("b4_proj"), 1)
                e.activation(alpha, ps[:, 0, :], ACT.Sigmoid, bias=v("four")).then_inc(sem("b4_act_read"), 1)
                e.wait_ge(sem("b4_proj"), 2)
                e.activation(beta, ps[:, 1, :], ACT.Sigmoid).then_inc(sem("b4_act_read"), 1)
                e.preload_act_table_set("natural_log_exp_and_others")
                e.wait_ge(sem("b4_dve_read"), 8)
                e.activation(k_sq, k_hat, ACT.Square).then_inc(sem("b4_square"), 1)
                for g in range(10, 18):
                    e.wait_ge(sem("b4_proj"), g + 1)
                    e.copy(q_raw[:, :, g - 10], ps[:, g % 8, :]).then_inc(sem("b4_act_read"), 1)
                for n_, r in enumerate((r_k, r_q)):
                    if n_:
                        e.wait_ge(sem("b4_act_read"), 10)
                        e.activation(q_sq, q_raw, ACT.Square).then_inc(sem("b4_square"), 1)
                    e.wait_ge(sem("b4_len"), n_ + 1)
                    e.activation(r, r, ACT.Ln, bias=v("eps6")).then_inc(sem("b4_ln"), 1)
                    e.wait_ge(sem("b4_ln"), n_ + 1)
                    e.activation(r, r, ACT.Exp, scale=-0.5).then_inc(sem("b4_rlen"), 1)
                e.wait_ge(sem("b4_solved"), 1)
                for n_ in range(NB):
                    if n_:
                        e.wait_ge(sem("b4_state"), n_)
                    e.activation(rank1[:, n_ % 2, :, :, BL], hist[:, n_, :, :], ACT.Copy,
                                 scale=gamma[:, BL * n_ + BL - 1:BL * n_ + BL]).then_inc(sem("b4_carry"), 1)

            def per_d(x, n_=HD):
                return x.unsqueeze(2).to_broadcast([128, T, n_])

            def b4_dve(e):
                link(e, e.memset(xp[:, :, 0:PADW], 0.0))
                for b in range(B):
                    e.wait_ge(*n4.done(b))
                for k in range(CTAPS):
                    if k == 0:
                        i = e.tensor_scalar(x_aux[:, :, :], xp[:, :, 0:T], v("conv_w"), None, ALU.mult)
                    else:
                        e.wait_ge(sem("b4_conv"), k)
                        i = e.scalar_tensor_tensor(out=x_aux[:, :, :], in0=xp[:, :, k:k + T], scalar=v("conv_w", k),
                                                   in1=x_aux[:, :, :], op0=ALU.mult, op1=ALU.add)
                    i.then_inc(sem("b4_conv"), 1)
                for g in range(2, 10):
                    e.wait_ge(sem("b4_proj"), g + 1)
                    e.tensor_copy(k_hat[:, :, g - 2], ps[:, g % 8, :]).then_inc(sem("b4_dve_read"), 1)
                e.wait_ge(sem("b4_square"), 1)
                e.tensor_reduce(r_k, k_sq, AX.X, ALU.add).then_inc(sem("b4_len"), 1)
                e.wait_ge(sem("b4_act_read"), 2)
                blk = lambda x: x.rearrange("p (n i) -> p n i", i=BL)
                a_, g_, e_, t1, t2, cf = (blk(x) for x in (alpha, gamma, to_end, t_one, t_two, coef))
                link(e, e.tensor_copy(gamma, alpha))
                for i in range(1, BL):
                    link(e, e.tensor_tensor(g_[:, :, i], g_[:, :, i - 1], a_[:, :, i], ALU.mult))
                e.tensor_tensor(t1[:, :, 1:], a_[:, :, 1:], a_[:, :, :BL - 1], ALU.mult).then_inc(sem("b4_decay"), 1)
                e.wait_ge(sem("b4_decay"), 1)
                link(e, e.tensor_tensor(t2[:, :, 2:], t1[:, :, 2:], a_[:, :, :BL - 2], ALU.mult))
                e.memset(e_[:, :, 3], -1.0)
                e.tensor_scalar(e_[:, :, 2], a_[:, :, 3], -1.0, None, ALU.mult)
                e.tensor_scalar(e_[:, :, 1], t1[:, :, 3], -1.0, None, ALU.mult)
                link(e, e.tensor_scalar(e_[:, :, 0], t2[:, :, 3], -1.0, None, ALU.mult))
                for g in range(18, 22):
                    e.wait_ge(sem("b4_proj"), g + 1)
                    e.scalar_tensor_tensor(out=y[:, :, g - 10], in0=ps[:, g % 8, :], scalar=-1.0, in1=beta,
                                           op0=ALU.mult, op1=ALU.mult).then_inc(sem("b4_dve_read"), 1)
                e.wait_ge(sem("b4_rlen"), 1)
                e.tensor_tensor(k_hat, k_hat, per_d(r_k), ALU.mult).then_inc(sem("b4_khat"), 1)
                e.wait_ge(sem("b4_square"), 2)
                link(e, e.tensor_reduce(r_q, q_sq, AX.X, ALU.add))
                e.nop().then_inc(sem("b4_len"), 1)
                e.wait_ge(sem("b4_dve_read"), 12)
                e.wait_ge(sem("b4_khat"), 1)
                k4, q4, y4 = (x.rearrange("p (n i) d -> p n i d", i=BL) for x in (k_hat, q_raw, y))
                span = (None, a_, t1, t2)

                def dots(red, out_, s_):
                    view = red[:, 0:NB * (BL - s_) * HD].rearrange("p (n i d) -> p n i d", n=NB, d=HD)
                    return e.tensor_reduce(out_[:, :, s_:], view, AX.X, ALU.add)

                def spread(x, i0, i1, w):
                    return x[:, :, i0:i1].unsqueeze(3).to_broadcast([128, NB, i1 - i0, w])
                for s_ in range(1, BL):
                    view = prod_k[:, 0:NB * (BL - s_) * HD].rearrange("p (n i d) -> p n i d", n=NB, d=HD)
                    link(e, e.tensor_tensor(view, k4[:, :, s_:, :], k4[:, :, :BL - s_, :], ALU.mult))
                    link(e, dots(prod_k, kk_dot[:, s_ - 1], s_))
                    link(e, e.tensor_tensor(kk_dot[:, s_ - 1, :, s_:], kk_dot[:, s_ - 1, :, s_:], span[s_][:, :, s_:],
                                            ALU.mult))
                    link(e, e.tensor_tensor(kk_dot[:, s_ - 1, :, s_:], kk_dot[:, s_ - 1, :, s_:],
                                            blk(beta)[:, :, s_:], ALU.mult))
                link(e, e.tensor_tensor(coef, gamma, beta, ALU.mult))
                link(e, e.tensor_tensor(y[:, :, 0:HD], k_hat, per_d(coef), ALU.mult))
                tmp12 = prod_k[:, 0:NB * 12].rearrange("p (n w) -> p n w", w=12)
                for i in range(1, BL):
                    for s_ in range(1, i + 1):
                        c_ = kk_dot[:, s_ - 1, :, i].unsqueeze(2).to_broadcast([128, NB, 12])
                        link(e, e.tensor_tensor(tmp12, y4[:, :, i - s_, :], c_, ALU.mult))
                        link(e, e.tensor_tensor(y4[:, :, i, :], y4[:, :, i, :], tmp12, ALU.subtract))
                e.memset(hist[:, 0, :, :], 0.0).then_inc(sem("b4_solved"), 1)
                e.wait_ge(sem("b4_qk"), 7)
                link(e, e.tensor_tensor(k_hat, k_hat, per_d(to_end), ALU.mult))
                e.wait_ge(sem("b4_solved"), 1)
                e.wait_ge(sem("b4_qk"), QK_OPS)

                for n_ in range(NB):
                    ch = n_ // CB
                    if n_ % CB == 0:
                        e.wait_ge(sem("b4_vset"), ch + 1)
                    if n_:
                        e.wait_ge(sem("b4_state"), n_)
                    slot = n_ % (2 * CB)
                    e.tensor_tensor(terms[:, slot, :, :, 0:HD],
                                    y4[:, n_, :, 0:HD].unsqueeze(2).to_broadcast([128, BL, 4, HD]),
                                    hist[:, n_, :, :].unsqueeze(1).to_broadcast([128, BL, 4, HD]),
                                    ALU.mult).then_inc(sem("b4_scan"), 1)
                    e.wait_ge(sem("b4_scan"), 3 * n_ + 1)
                    e.tensor_reduce(neg_delta[:, n_, :, :], terms[:, slot, :, :, :], AX.X,
                                    ALU.add).then_inc(sem("b4_scan"), 1)
                    e.wait_ge(sem("b4_scan"), 3 * n_ + 2)
                    e.tensor_tensor(rank1[:, n_ % 2, :, :, 0:BL],
                                    neg_delta[:, n_, :, :].rearrange("p l j -> p j l").unsqueeze(2).to_broadcast(
                                        [128, 4, HD, BL]),
                                    k4[:, n_, :, :].rearrange("p l d -> p d l").unsqueeze(1).to_broadcast(
                                        [128, 4, HD, BL]), ALU.mult).then_inc(sem("b4_scan"), 1)
                    e.wait_ge(sem("b4_scan"), 3 * n_ + 3)
                    e.wait_ge(sem("b4_carry"), n_ + 1)
                    e.tensor_reduce(hist[:, n_ + 1, :, :], rank1[:, n_ % 2, :, :, :], AX.X,
                                    ALU.add).then_inc(sem("b4_state"), 1)
                e.wait_ge(sem("b4_out"), OUT_OPS * (NCB - 2))
                outputs(e, NCB - 1, sem("b4_last_out"), 0)
                for b in range(B):
                    e.wait_ge(sem("b4_mix"), b + 1)
                    e.tensor_tensor(x_aux[:, b, :], ps[:, b, :], x_cur[:, b, :], ALU.add).then_inc(sem("b4_h"), 1)

            def outputs(e, ch, s_, base):
                count = [base]

                def then(i):
                    count[0] += 1
                    i.then_inc(s_, 1)
                    e.wait_ge(s_, count[0])
                q4 = q_raw.rearrange("p (n i) d -> p n i d", i=BL)
                blks = slice(ch * CB, (ch + 1) * CB)
                prod = prod_o[ch % 2].rearrange("p (n i j d) -> p n i j d", n=CB, i=BL, j=4)
                for i in range(BL):
                    o = e.tensor_tensor(prod[:, :, i, :, :],
                                        q4[:, blks, i, :].unsqueeze(2).to_broadcast([128, CB, 4, HD]),
                                        hist[:, blks, :, :], ALU.mult)
                then(o)
                flat = prod_o[ch % 2].rearrange("p (x d) -> p x d", d=HD)
                then(e.tensor_tensor(flat[:, :, 0:4], flat[:, :, 0:4], flat[:, :, 4:8], ALU.add))
                then(e.tensor_tensor(flat[:, :, 0:2], flat[:, :, 0:2], flat[:, :, 2:4], ALU.add))
                out_ = o_all[:, ch * CB * BL * 4:(ch + 1) * CB * BL * 4]
                then(e.tensor_tensor(out_, flat[:, :, 0], flat[:, :, 1], ALU.add))
                o4 = out_.rearrange("p (n i j) -> p n i j", i=BL, j=4)
                own = prod_o[ch % 2][:, 0:CB * BL * 4].rearrange("p (n i j) -> p n i j", i=BL, j=4)
                for s2 in range(BL):
                    then(e.tensor_tensor(own[:, :, s2:, :], neg_delta[:, blks, :BL - s2, :],
                                         qk_dot[:, s2, blks, s2:].unsqueeze(3).to_broadcast([128, CB, BL - s2, 4]),
                                         ALU.mult))
                    then(e.tensor_tensor(o4[:, :, s2:, :], o4[:, :, s2:, :], own[:, :, s2:, :], ALU.subtract))
                then(e.tensor_tensor(out_.rearrange("p (t j) -> p t j", j=4), out_.rearrange("p (t j) -> p t j", j=4),
                                     r_q[:, ch * CB * BL:(ch + 1) * CB * BL].unsqueeze(2).to_broadcast(
                                         [128, CB * BL, 4]), ALU.mult))

            def b4_pool(e):
                k4, q4 = (x.rearrange("p (n i) d -> p n i d", i=BL) for x in (k_hat, q_raw))
                spans = [x.rearrange("p (n i) -> p n i", i=BL) for x in (alpha, alpha, t_one, t_two)]
                count = [0]

                def then(i, wait=True):
                    count[0] += 1
                    i.then_inc(sem("b4_qk"), 1)
                    if wait:
                        e.wait_ge(sem("b4_qk"), count[0])

                def view(s_):
                    return prod_q[s_][:, 0:NB * (BL - s_) * HD].rearrange("p (n i d) -> p n i d", n=NB, d=HD)

                def product(s_):
                    then(e.tensor_tensor(view(s_), q4[:, :, s_:, :], k4[:, :, :BL - s_, :], ALU.mult))

                def dots(s_):
                    x = view(s_)
                    then(e.tensor_tensor(x[:, :, :, 0:4], x[:, :, :, 0:4], x[:, :, :, 4:8], ALU.add))
                    then(e.tensor_tensor(x[:, :, :, 0:2], x[:, :, :, 0:2], x[:, :, :, 2:4], ALU.add))
                    then(e.tensor_tensor(qk_dot[:, s_, :, s_:], x[:, :, :, 0], x[:, :, :, 1], ALU.add))
                e.wait_ge(sem("b4_khat"), 1)
                e.wait_ge(sem("b4_act_read"), 10)
                product(1)
                dots(1)
                for s_ in (0, 2, 3):
                    product(s_)
                for s_ in (2, 3, 0):
                    dots(s_)
                for s_ in (1, 2, 3):
                    then(e.tensor_tensor(qk_dot[:, s_, :, s_:], qk_dot[:, s_, :, s_:], spans[s_][:, :, s_:], ALU.mult))
                assert count[0] == QK_OPS

                def vset(ch):
                    if ch >= 2:
                        e.wait_ge(sem("b4_scan"), 3 * CB * (ch - 1))
                    for i in range(BL):
                        o = e.tensor_copy(terms[:, ch % 2 * CB:(ch % 2 + 1) * CB, i, :, HD],
                                          y[:, ch * CB * BL + i:(ch + 1) * CB * BL:BL, HD:12])
                    o.then_inc(sem("b4_vset"), 1)
                e.wait_ge(sem("b4_solved"), 1)
                vset(0)
                vset(1)
                e.wait_ge(sem("b4_square"), 2)
                e.tensor_tensor(q_raw, q_raw, gamma.unsqueeze(2).to_broadcast([128, T, HD]),
                                ALU.mult).then_inc(sem("b4_qdecay"), 1)
                e.wait_ge(sem("b4_qdecay"), 1)
                e.wait_ge(sem("b4_rlen"), 2)
                for ch in range(NCB - 1):
                    e.wait_ge(sem("b4_scan"), 3 * CB * ch + 3 * CB)
                    if ch + 2 < NCB:
                        vset(ch + 2)
                    outputs(e, ch, sem("b4_out"), OUT_OPS * ch)

            def b4_pe2(e):
                e.wait_ge(sem("b4_dve_read"), 12)
                for ch in range(NCB):
                    if ch < NCB - 1:
                        e.wait_ge(sem("b4_out"), OUT_OPS * (ch + 1))
                    else:
                        e.wait_ge(sem("b4_last_out"), OUT_OPS)
                    cols_ = slice(ch * CB * BL, (ch + 1) * CB * BL)
                    for b in range(B):
                        for j in range(4):
                            i = e.matmul(ps[:, b, cols_], wt["o_s"][:, (b * 4 + j) * 128:(b * 4 + j + 1) * 128],
                                         o_tok[:, cols_, j], start=(j == 0), stop=(j == 3))
                        if ch == NCB - 1:
                            i.then_inc(sem("b4_mix"), 1)
            pe_steps += [b4_pe, b4_pe2]
            act_steps.append(b4_act)
            dve_steps.append(b4_dve)
            pool_steps.append(b4_pool)

            c = Carve()
            hn = c(B * T).rearrange("p (b t) -> p b t", b=B)
            act4 = c(4 * T).rearrange("p (s t) -> p s t", s=4)
            n = make_norm([(x_aux[:, b, :], hn[:, b, :], T, b) for b in range(B)], counted("b4_h"), gain="norm2_w",
                          eps="eps6", mean=False)
            add_norm(n)

            def b4_total(e, b):
                link(e, e.tensor_tensor(x_aux[:, b, :], ps[:, 4 + b % 2, :], x_aux[:, b, :], ALU.add))
                return e.tensor_tensor(x_aux[:, b, :], x_aux[:, b, :], x_cur[:, b, :], ALU.add)
            gated("b4f", FC, FW, hn, [n.done(b) for b in range(B)],
                  lambda i: wt["wg"][:, i * FW:(i + 1) * FW], lambda i: wt["wu"][:, i * FW:(i + 1) * FW],
                  lambda i: wt["wd"][0:FW, i * 128:(i + 1) * 128], act4, extra={"total": b4_total})
            n = make_norm(batches(x_aux, x_cur), counted("b4f_sum"), other_table=True)
            add_norm(n)
            final = n

        if stages >= 5:
            c = Carve()
            qc = c(B * T).rearrange("p (b t) -> p b t", b=B)
            kc = c(B * S).rearrange("p (b s) -> p b s", b=B)
            kblk = c(B * H * S).rearrange("p (b h s) -> p b h s", b=B, h=H)
            vblk = c(B * 4 * 128).rearrange("p (b c n) -> p b c n", b=B, c=4)
            pc = c(4 * T).rearrange("p (a h s) -> p a h s", a=4, h=H)
            ptc = c(2 * 4 * T).rearrange("p (a c q) -> p a c q", a=2, c=4)
            oc = c(2 * T).rearrange("p (a t) -> p a t", a=2)
            st5 = c(3 * 4 * H).rearrange("p (k a h) -> p k a h", k=3, a=4)
            fin5 = final
            N5 = B * QB

            def b5_pe(e):
                e.wait_ge(sem("load_wE"), 16)
                e.wait_ge(*fin5.done(B - 1))
                e.wait_ge(sem("load_ctx"), 16)
                e.matmul(ps[:, 4, 0:B * S], wt["c_Wk"], ctx_in[:, :], start=True, stop=True).then_inc(sem("b5_proj"), 1)
                for b in range(B):
                    for r in range(4):
                        i = e.matmul(ps[32 * r:32 * r + 32, 5, b * 128:b * 128 + 128], ctx_in[:, b * S:b * S + S],
                                     wt["c_Wv"], start=True, stop=True)
                i.then_inc(sem("b5_proj"), 1)
                for b in range(B):
                    e.matmul(ps[:, b, :], wt["c_Wq"], x_cur[:, b, :], start=True, stop=True).then_inc(sem("b5_proj"), 1)
                e.wait_ge(sem("b5_exp"), B)
                e.wait_ge(sem("b5_blocks"), 1)

                def pv(b):
                    e.wait_ge(sem("b5_evac"), QB * (b + 1))
                    if b >= 2:
                        e.wait_ge(sem("b5_heads"), b - 1)
                    for k in range(4):
                        i = e.matmul(ps[:, 4 + b % 2, :], vblk[:, b, k, :], ptc[:, b % 2, k, :], start=(k == 0),
                                     stop=(k == 3))
                    i.then_inc(sem("b5_pv"), 1)

                def outp(b):
                    e.wait_ge(sem("b5_heads"), b + 1)
                    if b >= 2:
                        e.wait_ge(sem("b5_sum"), b - 1)
                    e.matmul(ps[:, 6 + b % 2, :], wt["c_Wo"], oc[:, b % 2, :], start=True,
                             stop=True).then_inc(sem("b5_out"), 1)
                for n_ in range(N5 + 7):
                    b, q = n_ // QB, n_ % QB
                    if n_ < N5:
                        if n_ >= 2:
                            e.wait_ge(sem("b5_shift"), n_ - 1)
                        e.matmul(ps[:, n_ % 2, :], qc[:, b, q * 128:q * 128 + 128], kblk[:, b, :, :], start=True,
                                 stop=True).then_inc(sem("b5_score"), 1)
                    if 3 <= n_ < N5 + 3:
                        m = n_ - 3
                        e.wait_ge(sem("b5_prob"), m + 1)
                        if m >= 2:
                            e.wait_ge(sem("b5_evac"), m - 1)
                        for k in range(4):
                            i = e.transpose(ps[:, 2 + m % 2, k * 128:k * 128 + 128], pc[:, m % 4, 4 * k:4 * k + 4, :],
                                            ident)
                        i.then_inc(sem("b5_turn"), 1)
                    if n_ >= 8 and (n_ - 8) % 4 == 0:
                        pv((n_ - 8) // 4)
                    if n_ >= 10 and (n_ - 10) % 4 == 0:
                        outp((n_ - 10) // 4)

            def b5_act(e):
                for b in range(B):
                    e.wait_ge(sem("b5_proj"), 3 + b)
                    e.activation(qc[:, b, :], ps[:, b, :], ACT.Identity, bias=v("c_bq")).then_inc(sem("b5_exp"), 1)
                for n_ in range(N5 + 3):
                    if n_ < N5:
                        e.wait_ge(sem("b5_shift"), n_ + 1)
                        e.activation(pc[:, n_ % 4, :, :], pc[:, n_ % 4, :, :], ACT.Exp).then_inc(sem("b5_exp"), 1)
                    if n_ >= 3:
                        m = n_ - 3
                        b, q = m // QB, m % QB
                        e.wait_ge(sem("b5_turn"), m + 1)
                        if b >= 2 and q == 0:
                            e.wait_ge(sem("b5_pv"), b - 1)
                        e.copy(ptc[:, b % 2, :, q * 128:q * 128 + 128],
                               ps[:, 2 + m % 2, :].rearrange("p (k q) -> p k q", k=4)).then_inc(sem("b5_evac"), 1)

            def b5_dve(e):
                e.wait_ge(sem("b5_proj"), 1)
                link(e, e.tensor_scalar(kc, ps[:, 4, 0:B * S].rearrange("p (b s) -> p b s", b=B), v("c_bk"),
                                        HD ** -0.5, ALU.add, ALU.mult))
                e.wait_ge(sem("b5_proj"), 2)
                for b in range(B):
                    e.tensor_tensor(kblk[:, b, :, :], kc[:, b, :].unsqueeze(1).to_broadcast([128, H, S]),
                                    v("head_mask", 0, H).unsqueeze(2).to_broadcast([128, H, S]), ALU.mult)
                    i = e.tensor_tensor(vblk[:, b, :, :],
                                        ps[:, 5, b * 128:b * 128 + 128].unsqueeze(1).to_broadcast([128, 4, 128]),
                                        wt["v_mask"].rearrange("p (c n) -> p c n", c=4), ALU.mult)
                i.then_inc(sem("b5_blocks"), 1)

                def heads(b):
                    e.wait_ge(sem("b5_pv"), b + 1)
                    if b >= 2:
                        e.wait_ge(sem("b5_out"), b - 1)
                    e.tensor_scalar(oc[:, b % 2, :], ps[:, 4 + b % 2, :], v("c_bv"), None,
                                    ALU.add).then_inc(sem("b5_heads"), 1)

                def total(b):
                    e.wait_ge(sem("b5_out"), b + 1)
                    e.scalar_tensor_tensor(out=x_aux[:, b, :], in0=ps[:, 6 + b % 2, :], scalar=v("c_bo"),
                                           in1=x_cur[:, b, :], op0=ALU.add, op1=ALU.add).then_inc(sem("b5_sum"), 1)
                hs = lambda x: x.unsqueeze(2).to_broadcast([128, H, S])
                for n_ in range(N5 + 8):
                    if n_ < N5:
                        a = n_ % 4
                        score = ps[:, n_ % 2, :].rearrange("p (h s) -> p h s", h=H)
                        e.wait_ge(sem("b5_score"), n_ + 1)
                        link(e, e.tensor_reduce(st5[:, 0, a, :], score, AX.X, ALU.max))
                        if n_ >= 4:
                            e.wait_ge(sem("b5_turn"), n_ - 3)
                        e.tensor_tensor(pc[:, a, :, :], score, hs(st5[:, 0, a, :]),
                                        ALU.subtract).then_inc(sem("b5_shift"), 1)
                    if 1 <= n_ <= N5:
                        m, a = n_ - 1, (n_ - 1) % 4
                        e.wait_ge(sem("b5_exp"), B + m + 1)
                        link(e, e.tensor_reduce(st5[:, 1, a, :], pc[:, a, :, :], AX.X, ALU.add))
                        e.reciprocal(st5[:, 2, a, :], st5[:, 1, a, :]).then_inc(sem("b5_recip"), 1)
                    if n_ >= 9 and (n_ - 9) % 4 == 0:
                        heads((n_ - 9) // 4)
                    if n_ >= 11 and (n_ - 11) % 4 == 0:
                        total((n_ - 11) // 4)

            def b5_pool(e):
                for n_ in range(N5):
                    a = n_ % 4
                    e.wait_ge(sem("b5_recip"), n_ + 1)
                    e.tensor_tensor(pc[:, a, :, :], pc[:, a, :, :],
                                    st5[:, 2, a, :].unsqueeze(2).to_broadcast([128, H, S]),
                                    ALU.mult).then_inc(sem("b5_prob"), 1)
            pool_steps.append(b5_pool)
            pe_steps.append(b5_pe)
            act_steps.append(b5_act)
            dve_steps.append(b5_dve)
            n = make_norm(batches(x_aux, x_cur), counted("b5_sum"))
            add_norm(n)
            final = n

        if stages >= 6:
            n6 = make_norm(batches(x_cur, x_aux), [final.done(b) for b in range(B)], gain="m_ln1_w", mean=False)
            add_norm(n6)
            b6_res = narrow(1, x_aux, [n6.done(b) for b in range(B)], x_aux, "b6", "wF", "m_q", "m_k", "m_v", "m_wo",
                            rope=("m_qr", "m_kr"))
            c = Carve()
            hn6 = c(B * T).rearrange("p (b t) -> p b t", b=B)
            n7 = make_norm(batches(x_aux, hn6), b6_res, gain="m_ln2_w", mean=False)
            add_norm(n7)
            wide_w = c(2 * E1 * T).rearrange("p (a e t) -> p a e t", a=2, e=E1)
            act6 = c(4 * T).rearrange("p (s t) -> p s t", s=4)
            w_pad = c(QB * 128).rearrange("p (q n) -> p q n", q=QB)
            w_T = c(T // 2).bitcast(BF16)
            sel_bf = c(E1 * 64).bitcast(BF16)
            w_mid, w_rest = (c(QB * E1).rearrange("p (q e) -> p q e", q=QB) for _ in range(2))
            w_part = c(3 * QB * E1 // 2).bitcast(BF16).rearrange("p (i q e) -> p i q e", i=3, q=QB)
            r8 = [c(QB * E1).rearrange("p (q e) -> p q e", q=QB) for _ in range(6)]
            r1 = [c(QB) for _ in range(8)]
            sel = sel_bf.rearrange("p (e n) -> p e n", e=E1)
            rank = v("tie_rank", 0, QB * E1).rearrange("p (q e) -> p q e", q=QB)

            def r_logit(e, b):
                if b:
                    e.wait_ge(sem("r_wide"), 8 * b)
                for q in range(QB):
                    i = e.matmul(ps[:, 6, q * E1:q * E1 + E1], hn6[:, b, q * 128:q * 128 + 128], wt["m_gate"],
                                 start=True, stop=True)
                i.then_inc(sem("r_logit"), 1)

            def r_turn(e, b):
                e.wait_ge(sem("r_weights"), b + 1)
                for q in range(QB):
                    i = e.transpose(ps[:, 7, q * 128:q * 128 + 128], w_pad[:, q, :], ident)
                i.then_inc(sem("r_turn"), 1)

            def r_spread(e, b, ex):
                n_ = b * E1 + ex
                e.wait_ge(sem("r_turned"), b + 1)
                if ex >= 2:
                    e.wait_ge(sem("r_wide"), n_ - 1)
                e.matmul(ps[:, 6 + ex % 2, :], sel[:, ex, :], w_T, start=True, stop=True).then_inc(sem("r_spread"), 1)

            def r_exp(e, b):
                e.wait_ge(sem("r_shift"), b + 1)
                e.activation(r8[0], r8[0], ACT.Exp).then_inc(sem("r_exp"), 1)

            def r_wide(e, b, ex):
                n_ = b * E1 + ex
                e.wait_ge(sem("r_spread"), n_ + 1)
                if b >= 2 and ex == 0:
                    e.wait_ge(sem("b6f_gated"), (b - 1) * E1 * C1)
                e.copy(wide_w[:, b % 2, ex, :], ps[:, 6 + ex % 2, :]).then_inc(sem("r_wide"), 1)

            def top2_a(e, b):
                pr = r8[0]
                lg = ps[:, 6, 0:QB * E1].rearrange("p (q e) -> p q e", q=QB)
                bc = lambda x: x.unsqueeze(2).to_broadcast([128, QB, E1])
                e.wait_ge(sem("r_logit"), b + 1)
                link(e, e.tensor_reduce(r1[0], lg, AX.X, ALU.max))
                e.tensor_tensor(pr, lg, bc(r1[0]), ALU.subtract).then_inc(sem("r_shift"), 1)

            def top2_b(e, b):
                pr, eq, sel1, p2, sel2, both = r8
                bc = lambda x: x.unsqueeze(2).to_broadcast([128, QB, E1])
                e.wait_ge(sem("r_exp"), b + 1)
                link(e, e.tensor_reduce(r1[1], pr, AX.X, ALU.add))
                link(e, e.reciprocal(r1[2], r1[1]))
                link(e, e.tensor_tensor(pr, pr, bc(r1[2]), ALU.mult))
                link(e, e.tensor_reduce(r1[3], pr, AX.X, ALU.max))
                link(e, e.tensor_tensor(eq, pr, bc(r1[3]), ALU.is_equal))
                link(e, e.tensor_tensor(eq, eq, rank, ALU.mult))
                link(e, e.tensor_reduce(r1[4], eq, AX.X, ALU.max))
                link(e, e.tensor_tensor(sel1, eq, bc(r1[4]), ALU.is_equal))
                link(e, e.scalar_tensor_tensor(out=p2, in0=sel1, scalar=-2.0, in1=pr, op0=ALU.mult, op1=ALU.add))
                link(e, e.tensor_reduce(r1[5], p2, AX.X, ALU.max))
                link(e, e.tensor_tensor(eq, p2, bc(r1[5]), ALU.is_equal))
                link(e, e.tensor_tensor(eq, eq, rank, ALU.mult))
                link(e, e.tensor_reduce(r1[6], eq, AX.X, ALU.max))
                link(e, e.tensor_tensor(sel2, eq, bc(r1[6]), ALU.is_equal))
                link(e, e.tensor_tensor(r1[7], r1[3], r1[5], ALU.add))
                link(e, e.reciprocal(r1[7], r1[7]))
                link(e, e.tensor_tensor(both, sel1, sel2, ALU.add))
                link(e, e.tensor_tensor(both, both, pr, ALU.mult))
                if b:
                    e.wait_ge(sem("r_turn"), b)
                link(e, e.tensor_tensor(w_mid, both, bc(r1[7]), ALU.mult))
                link(e, e.tensor_copy(w_part[:, 0], w_mid))
                link(e, e.tensor_tensor(w_rest, w_mid, w_part[:, 0], ALU.subtract))
                link(e, e.tensor_copy(w_part[:, 1], w_rest))
                link(e, e.tensor_tensor(w_part[:, 2], w_rest, w_part[:, 1], ALU.subtract))
                e.tensor_copy(w_pad[:, :, 0:3 * E1].rearrange("p q (i e) -> p i q e", i=3),
                              w_part).then_inc(sem("r_weights"), 1)

            def r_turned(e, b):
                e.wait_ge(sem("r_turn"), b + 1)
                if b:
                    e.wait_ge(sem("r_spread"), E1 * b)
                e.tensor_copy(w_T, ps[:, 7, :]).then_inc(sem("r_turned"), 1)

            def pe_extra(e, b, i):
                if b == 0 and i == 1:
                    r_turn(e, 0)
                    for ex in range(E1):
                        r_spread(e, 0, ex)
                if b + 1 < B:
                    if i == 2:
                        r_logit(e, b + 1)
                    if i == 5:
                        r_turn(e, b + 1)
                    if 8 <= i < 16:
                        r_spread(e, b + 1, i - 8)

            def act_extra(e, b, i):
                if b == 0 and i == 1:
                    for ex in range(E1):
                        r_wide(e, 0, ex)
                if b + 1 < B:
                    if i == 2:
                        r_exp(e, b + 1)
                    if 8 <= i < 16:
                        r_wide(e, b + 1, i - 8)

            def dve_extra(e, b, i):
                if b + 1 < B:
                    if i == 2:
                        top2_a(e, b + 1)
                    if i == 3:
                        top2_b(e, b + 1)
                    if i == 6:
                        r_turned(e, b + 1)

            def b6_total(e, b):
                link(e, e.tensor_tensor(x_aux[:, b, :], ps[:, 4 + b % 2, :], x_aux[:, b, :], ALU.add))
                return e.tensor_tensor(x_aux[:, b, :], x_aux[:, b, :], x_cur[:, b, :], ALU.add)

            def first_pe(e):
                r_logit(e, 0)

            def first_act(e):
                r_exp(e, 0)

            def first_dve(e):
                e.memset(w_pad, 0.0)
                e.tensor_copy(sel_bf, wt["sel"])
                top2_a(e, 0)
                top2_b(e, 0)
                r_turned(e, 0)
            w13, w2 = wt["w13"], wt["w2"]

            def w13_of(i, half):
                ex, k = i // C1, i % C1
                at_ = ex * 512 + half * 256 + k * 128
                return w13[:, at_:at_ + 128]
            gated("b6f", E1 * C1, 128, hn6, [n7.done(b) for b in range(B)], lambda i: w13_of(i, 0),
                  lambda i: w13_of(i, 1), lambda i: w2[:, i * 128:(i + 1) * 128], act6, load="wM1",
                  weight=lambda b, i: wide_w[:, b % 2, i // C1, :], weight_ready=lambda b: (sem("r_wide"), E1 * (b + 1)),
                  extra={"pe": pe_extra, "act": act_extra, "dve": dve_extra, "total": b6_total,
                         "pe_first": [first_pe], "act_first": [first_act], "dve_first": [first_dve]})
            n = make_norm(batches(x_aux, x_cur), counted("b6f_sum"), other_table=True)
            add_norm(n)
            final = n

        def store(e):
            for b in range(B):
                e.wait_ge(*final.done(b))
                e.dma_start(out[:, b, :], x_cur[:, b, :]).then_inc(sem("stored"), 16)
            e.wait_ge(sem("stored"), 16 * B)
        sp_steps.append(store)

        block = ctx.enter_context(nc.Block())

        @block.sync
        def _(eng):
            for step in sp_steps:
                step(eng)

        @block.tensor
        def _(eng):
            for step in pe_steps:
                step(eng)

        @block.scalar
        def _(eng):
            for step in act_steps:
                step(eng)

        @block.vector
        def _(eng):
            for step in dve_steps:
                step(eng)

        @block.gpsimd
        def _(eng):
            for step in pool_steps:
                step(eng)


def feature_major(a):
    return np.ascontiguousarray(np.transpose(a, (2, 0, 1)))


def spread_rows(w):
    n = w.shape[1]
    out = np.zeros((4, 32, 4, n), w.dtype)
    out[:, :8] = np.transpose(w.reshape(4, 4, 8, n), (1, 2, 0, 3))
    return out.reshape(128, 4 * n)


def by_dim(w, axis):
    parts = w.shape[:axis] + (H, HD) + w.shape[axis + 1:]
    return np.ascontiguousarray(np.swapaxes(w.reshape(parts), axis, axis + 1)).reshape(w.shape)


def layouts(i):
    f = np.float32
    one = lambda a: np.asarray(a).reshape(-1, 1)
    vec = {
        "gate_w": i["L0_attn_gate_w"].reshape(D, 7), "cand_w": i["L0_attn_cand_w"].reshape(D, 7),
        "gate_b": one(i["L0_attn_gate_b"]), "cand_b": one(i["L0_attn_cand_b"]),
        "log_decay": one(i["L0_attn_log_decay"]), "out_b": one(i["L0_attn_out_b"]),
        "norm_w": one(i["L0_attn_norm_w"]),
        "x_ln1_g": one(i["L0_xattn_ln1_g"]), "x_ln1_b": one(i["L0_xattn_ln1_b"]),
        "x_ln2_g": one(i["L0_xattn_ln2_g"]), "x_ln2_b": one(i["L0_xattn_ln2_b"]),
        "f_bq": by_dim(one(i["L0_ffn_bq"]), 0), "f_bk": by_dim(one(i["L0_ffn_bk"]), 0),
        "f_bo": one(i["L0_ffn_bo"]), "router_b": np.repeat(one(i["L0_ffn_router_b"]), 128, 0),
        "f_b1": np.transpose(i["L0_ffn_b1"].reshape(16, 128)), "f_b2": np.transpose(i["L0_ffn_b2"]),
        "f_ln1_g": one(i["L0_ffn_ln1_g"]), "f_ln1_b": one(i["L0_ffn_ln1_b"]),
        "f_ln2_g": one(i["L0_ffn_ln2_g"]), "f_ln2_b": one(i["L0_ffn_ln2_b"]),
        "norm1_w": one(i["L1_attn_norm1_w"]), "norm2_w": one(i["L1_attn_norm2_w"]),
        "conv_w": i["L1_attn_conv_w"], "conv_b": one(i["L1_attn_conv_b"]),
        "c_bq": one(i["L1_xattn_bq"]), "c_bk": one(i["L1_xattn_bk"]), "c_bv": one(i["L1_xattn_bv"]),
        "c_bo": one(i["L1_xattn_bo"]), "m_ln1_w": one(i["L1_ffn_ln1_w"]), "m_ln2_w": one(i["L1_ffn_ln2_w"]),
        "eps_attn": np.full((128, 1), 1.1920929e-07, f), "eps5": np.full((128, 1), 1e-5, f),
        "eps6": np.full((128, 1), 1e-6, f), "four": np.full((128, 1), 4.0, f),
        "head_mask": np.repeat(np.eye(H, dtype=f), HD, 0),
        "sum_pick": (np.arange(128)[:, None] == 32 * np.arange(4)[None, :] + HD).astype(f),
        "tie_rank": np.tile(np.arange(E1, 0, -1).astype(f), (128, 4)),
    }
    for n, (_, w) in VEC.items():
        assert vec[n].shape == (128, w), (n, vec[n].shape)
    tr = np.transpose
    qkv = i["L1_ffn_wqkv"]
    group = np.repeat(np.arange(4), 4)
    mk = qkv[128:160].reshape(4, 8, 128)[group].reshape(128, 128)
    mv = qkv[160:192].reshape(4, 8, 128)[group].reshape(128, 128)
    swap = lambda w: w.reshape(16, 2, 4, 128)[:, ::-1].reshape(128, 128)
    inv = (1.0 / f(10000.0) ** (np.arange(0, HD, 2, dtype=f) / f(HD))).astype(f)
    ang = np.arange(T, dtype=f)[:, None] * inv[None, :]
    cos, sin = np.cos(ang).astype(f), np.sin(ang).astype(f)
    cosT = np.tile(np.concatenate([cos, cos], 1).T, (16, 1))
    sinT = np.tile(np.concatenate([-sin, sin], 1).T, (16, 1))
    ws = i["L1_attn_wq"], i["L1_attn_wk"]
    dhv = lambda w: np.repeat(tr(w.reshape(128, 16, 8), (0, 2, 1)), 2, 2).reshape(128, 256)
    o_s = np.zeros((4, 16, 2, 4, 4, 128), f)
    for b in range(4):
        o_s[b, :, :, b] = i["L1_attn_wo"].reshape(16, 2, 4, 128)
    wd = np.zeros((128, 3, 128), f)
    wd[:FW] = tr(i["L1_attn_wd"].reshape(3, FW, 128), (1, 0, 2))
    vm = (np.arange(128)[:, None, None] // 32 + 4 * np.arange(4)[None, :, None]
          == np.arange(128)[None, None, :] // 8).astype(f).reshape(128, 512)
    causal = np.where(np.arange(128)[None, :] > np.arange(128)[:, None], f(NEG), f(0))
    sel = np.zeros((128, 8, 128), f)
    for ex in range(8):
        sel[ex:24:8, ex] = 1.0
    mats = {
        "out_w": tr(i["L0_attn_out_w"]), "ident": np.eye(128, dtype=f), "ones": np.full((128, 128), 1.0 / D, f),
        "Wq": i["L0_xattn_Wq"], "Wkv": i["L0_xattn_Wkv"],
        "Wo": tr(i["L0_xattn_Wo"].reshape(8, 128, 128), (1, 0, 2)).reshape(128, 1024),
        "f_Wq": by_dim(i["L0_ffn_Wq"], 1), "f_Wk": by_dim(i["L0_ffn_Wk"], 1), "f_Wv": i["L0_ffn_Wv"],
        "f_bv": np.repeat(i["L0_ffn_bv"].reshape(1, 128), 128, 0),
        "f_Wo": spread_rows(i["L0_ffn_Wo"]), "router": np.repeat(i["L0_ffn_router_w"], 128, 1),
        "W1": tr(i["L0_ffn_W1"], (1, 0, 2)).reshape(128, 2048),
        "W2": tr(i["L0_ffn_W2"].reshape(16, 128, 128), (1, 0, 2)).reshape(128, 2048),
        "q_s": dhv(ws[0]), "k_s": dhv(ws[1]),
        "v_s": tr(i["L1_attn_wv"].reshape(128, 32, 4), (0, 2, 1)).reshape(128, 128),
        "b_s": np.repeat(i["L1_attn_wb"], 2, 1), "a_s": np.repeat(i["L1_attn_wa"], 2, 1),
        "o_s": o_s.reshape(128, 2048), "wg": i["L1_attn_wg"], "wu": i["L1_attn_wu"], "wd": wd.reshape(128, 384),
        "c_Wq": tr(i["L1_xattn_Wq"]), "c_Wk": tr(i["L1_xattn_Wk"]), "c_Wv": tr(i["L1_xattn_Wv"]),
        "c_Wo": tr(i["L1_xattn_Wo"]), "v_mask": vm,
        "m_q": by_dim(tr(qkv[:128]), 1), "m_qr": by_dim(tr(swap(qkv[:128])), 1), "m_k": by_dim(tr(mk), 1),
        "m_kr": by_dim(tr(swap(mk)), 1), "m_v": tr(mv), "m_wo": spread_rows(tr(i["L1_ffn_wo"])), "m_gate": tr(i["L1_ffn_gate_w"]),
        "cos": by_dim(cosT, 0), "sin": by_dim(sinT, 0), "causal": causal, "sel": sel.reshape(128, 1024),
        "w13": tr(i["L1_ffn_w13"], (2, 0, 1)).reshape(128, 4096),
        "w2": tr(i["L1_ffn_w2"].reshape(8, 128, 2, 128), (3, 0, 2, 1)).reshape(128, 2048),
    }
    arrays = {"xT": feature_major(i["x"]), "ctxT": feature_major(i["ctx_1024"]).reshape(128, B * S),
              "vecs": np.concatenate([vec[n] for n in VEC], 1)}
    for g, cols in GROUPS.items():
        for n, w in cols:
            assert mats[n].shape == (128, w), (n, mats[n].shape)
        arrays[g] = np.concatenate([mats[n] for n, _ in cols], 1)
    return {k: np.ascontiguousarray(a) for k, a in arrays.items()}


def kernel(**inputs):
    import concourse.bacc as _bacc
    from concourse.bass_utils import run_bass_kernel_spmd as _run

    arrays = layouts(inputs)
    nc = _bacc.Bacc("TRN2", target_bir_lowering=False, num_devices=1)
    aps = {k: nc.dram_tensor(k + "_dram", a.shape, F32, kind="ExternalInput").ap() for k, a in arrays.items()}
    out = nc.dram_tensor("out_dram", (128, B, T), F32, kind="ExternalOutput").ap()
    program(nc, aps["xT"], aps["ctxT"], aps["vecs"], {g: aps[g] for g in GROUPS}, out)
    r = _run(nc, [{k + "_dram": a for k, a in arrays.items()}], core_ids=[0])
    return np.ascontiguousarray(np.transpose(r.results[0]["out_dram"], (1, 2, 0)))
```
